# Optimizing a Trainium2 kernel written in Bass

```python
import numpy as np
import jax
import jax.numpy as jnp

def _softmax(x, axis=-1):
    return jax.nn.softmax(x, axis=axis)

def _gelu(x):
    return jax.nn.gelu(x, approximate=True)

def _silu(x):
    return jax.nn.silu(x)

def _sigmoid(x):
    return jax.nn.sigmoid(x)

def _layernorm(x, axis=-1, eps=1e-05):
    m = jnp.mean(x, axis=axis, keepdims=True)
    v = jnp.var(x, axis=axis, keepdims=True)
    return (x - m) / jnp.sqrt(v + eps)

def _scatter_add(tgt, idx, src, axis=0):
    return tgt.at[idx].add(src)

def _segment_sum(src, seg, n):
    return jax.ops.segment_sum(src, seg, n)
kernel_name = 'mk_flamingo_gated_d2_seqx_r8_148d83'

def setup_inputs(seed: int=0):
    np.random.seed(seed)
    _w = jnp.asarray

    def _rec_inputs():
        import jax
        import jax.numpy as jnp
        _rk = jax.random.key(seed)
        x = -0.0003929 + 0.9999 * jax.random.normal(jax.random.fold_in(_rk, 1), (8, 128, 512), jnp.float32)
        _lenS = 128 - jax.random.randint(jax.random.fold_in(_rk, 7), (8,), 0, max(1, 128 // 4) + 1, jnp.int32)
        _lenS2 = 128 - jax.random.randint(jax.random.fold_in(_rk, 8), (8,), 0, max(1, 128 // 4) + 1, jnp.int32)
        _ctx_4096P = jax.random.normal(jax.random.fold_in(_rk, 11), (8, 16, 512), jnp.float32)
        _ctx_4096c = jax.random.dirichlet(jax.random.fold_in(_rk, 511), 0.3 * jnp.ones((16,), jnp.float32), (8, 128))
        _ctx_4096t = jnp.einsum('bsk,bkd->bsd', _ctx_4096c, _ctx_4096P)
        _ctx_4096t = _ctx_4096t * jax.lax.rsqrt(jnp.mean(jnp.square(_ctx_4096t)) + 1e-12) * 0.953939
        ctx_4096 = 2.81802e-05 + 1.00001 * (_ctx_4096t + 0.3 * jax.random.normal(jax.random.fold_in(_rk, 611), (8, 128, 512), jnp.float32))
        pos_BxS2 = jnp.broadcast_to(jnp.arange(128, dtype=jnp.int32), (8, 128))
        _validS = jnp.arange(128)[None, :] < _lenS[:, None]
        _validS2 = jnp.arange(128)[None, :] < _lenS2[:, None]
        _causal = jnp.tril(jnp.ones((128, 128), dtype=bool))
        mask_BxSxS2_ik0 = jnp.where(jnp.broadcast_to(_validS2[:, None, :], (8, 128, 128)), 0, 1).astype(jnp.int32)
        _g = jax.random.normal(jax.random.fold_in(_rk, 9001), (2, 2), jnp.float32)
        _g = jnp.sign(_g) * jnp.maximum(jnp.abs(_g), 1.0) + (_g == 0) * 1.0
        g_xattn = _g[0]
        g_ffn = _g[1]
        return (x, ctx_4096, pos_BxS2, mask_BxSxS2_ik0, g_xattn, g_ffn)
    x, ctx_4096, pos_BxS2, mask_BxSxS2_ik0, g_xattn, g_ffn = _rec_inputs()

    def _L0_xattn_setup():
        import jax, jax.numpy as jnp
        import numpy as np
        B, S, E = (2, 256, 512)
        H, KVH, D = (32, 8, 128)
        GROUPS = H // KVH
        MAX_POS = 512
        ROPE_THETA = 10000.0

        def _rope_tables(max_pos, dim, theta):
            inv_freq = 1.0 / theta ** (jnp.arange(0, dim, 2, dtype=jnp.float32) / dim)
            t = jnp.arange(max_pos, dtype=jnp.float32)
            freqs = jnp.einsum('i,j->ij', t, inv_freq)
            emb = jnp.concatenate([freqs, freqs], axis=-1)
            return (jnp.cos(emb), jnp.sin(emb))

        def _rotate_half(x):
            x1, x2 = (x[..., :x.shape[-1] // 2], x[..., x.shape[-1] // 2:])
            return jnp.concatenate([-x2, x1], axis=-1)
        key = jax.random.key(seed)
        ks = jax.random.split(key, 8)
        scale_w = 1.0 / np.sqrt(E)
        query = jax.random.normal(ks[0], (B, S, E), dtype=jnp.float32)
        k_in = jax.random.normal(ks[1], (B, S, E), dtype=jnp.float32)
        v_in = jax.random.normal(ks[2], (B, S, E), dtype=jnp.float32)
        position_ids = jnp.broadcast_to(jnp.arange(S, dtype=jnp.int64), (B, S))
        src_mask = jnp.tril(jnp.ones((S, S), dtype=jnp.int32))
        src_mask = jnp.broadcast_to(src_mask, (B, S, S))
        Wq = jax.random.normal(ks[3], (E, H * D), dtype=jnp.float32) * scale_w
        Wk = jax.random.normal(ks[4], (E, KVH * D), dtype=jnp.float32) * scale_w
        Wv = jax.random.normal(ks[5], (E, KVH * D), dtype=jnp.float32) * scale_w
        Wo = jax.random.normal(ks[6], (H * D, E), dtype=jnp.float32) * scale_w
        return {'query': query, 'key': k_in, 'value': v_in, 'position_ids': position_ids, 'src_mask': src_mask, 'Wq': Wq, 'Wk': Wk, 'Wv': Wv, 'Wo': Wo}
    _L0_xattn_all = _L0_xattn_setup()
    _L0_xattn_in = {k: v for k, v in _L0_xattn_all.items() if k in ('Wq', 'Wk', 'Wv', 'Wo')}
    del _L0_xattn_all

    def _L0_ffn_setup():
        import jax, jax.numpy as jnp
        import numpy as np
        GROUP = 64

        def _dequantize_sparse_sinq(W_q, scales, zeros, mask, scale2, dtype):
            K, N = W_q.shape
            G = N // GROUP
            Wg = W_q.astype(dtype).reshape(K, G, GROUP)
            W = (Wg - zeros[:, :, None]) * scales[:, :, None]
            W = W.reshape(K, N) * scale2
            W = W * mask.astype(dtype)
            return W
        key = jax.random.key(seed)
        ks = jax.random.split(key, 7)
        B, S, N, K = (4, 256, 512, 512)
        G = N // GROUP
        x = jax.random.normal(ks[0], (B, S, N), dtype=jnp.float32)
        W_q = jax.random.randint(ks[1], (K, N), 0, 16, dtype=jnp.int32)
        scales = jax.random.uniform(ks[2], (K, G), dtype=jnp.float32, minval=0.01, maxval=1.0)
        zeros = jax.random.uniform(ks[3], (K, G), dtype=jnp.float32, minval=0.0, maxval=15.0)
        mask = jax.random.randint(ks[4], (K, N), 0, 2, dtype=jnp.int32)
        scale2 = jax.random.uniform(ks[5], (K, 1), dtype=jnp.float32, minval=0.5, maxval=1.5)
        bias = jax.random.normal(ks[6], (K,), dtype=jnp.float32)
        return {'x': x, 'W_q': W_q, 'scales': scales, 'zeros': zeros, 'mask': mask, 'scale2': scale2, 'bias': bias}
    _L0_ffn_all = _L0_ffn_setup()
    _L0_ffn_in = {k: v for k, v in _L0_ffn_all.items() if k in ('W_q', 'scales', 'zeros', 'mask', 'scale2', 'bias')}
    del _L0_ffn_all

    def _L1_xattn_setup():
        import jax, jax.numpy as jnp
        import numpy as np
        TEXT_DIM = 512
        FEATURE_DIM = 512

        def _xavier_uniform(key, shape):
            fan_in, fan_out = (shape[1], shape[0])
            limit = float(np.sqrt(6.0 / (fan_in + fan_out)))
            return jax.random.uniform(key, shape, jnp.float32, -limit, limit)
        key = jax.random.key(seed)
        k1, k2, k3, k4 = jax.random.split(key, 4)
        text = jax.random.normal(k1, (8, 256, TEXT_DIM), jnp.float32)
        features = jax.random.normal(k2, (8, 72, FEATURE_DIM), jnp.float32)
        Wq = _xavier_uniform(k3, (FEATURE_DIM, TEXT_DIM))
        bq = jnp.zeros((FEATURE_DIM,), jnp.float32)
        Wk = _xavier_uniform(k4, (FEATURE_DIM, FEATURE_DIM))
        bk = jnp.zeros((FEATURE_DIM,), jnp.float32)
        return {'text': text, 'features': features, 'Wq': Wq, 'bq': bq, 'Wk': Wk, 'bk': bk}
    _L1_xattn_all = _L1_xattn_setup()
    _L1_xattn_in = {k: v for k, v in _L1_xattn_all.items() if k in ('Wq', 'bq', 'Wk', 'bk')}
    del _L1_xattn_all

    def _L1_ffn_setup():
        import jax, jax.numpy as jnp
        import numpy as np
        NUM_EXPERTS = 32
        D_MODEL = 512
        TOP_K = 2
        key = jax.random.key(seed)
        k1, k2, k3, k4 = jax.random.split(key, 4)
        x = jax.random.normal(k1, (2, 256, D_MODEL), dtype=jnp.float32)
        gate_w = jax.random.normal(k2, (NUM_EXPERTS, D_MODEL), dtype=jnp.float32) * 0.02
        expert_w = jax.random.normal(k3, (NUM_EXPERTS, D_MODEL, D_MODEL), dtype=jnp.float32) * 0.02
        expert_b = jax.random.normal(k4, (NUM_EXPERTS, D_MODEL), dtype=jnp.float32) * 0.02
        return {'x': x, 'gate_w': gate_w, 'expert_w': expert_w, 'expert_b': expert_b}
    _L1_ffn_all = _L1_ffn_setup()
    _L1_ffn_in = {k: v for k, v in _L1_ffn_all.items() if k in ('gate_w', 'expert_w', 'expert_b')}
    del _L1_ffn_all
    return {'x': x, 'ctx_4096': ctx_4096, 'pos_BxS2': pos_BxS2, 'mask_BxSxS2_ik0': mask_BxSxS2_ik0, 'g_xattn': g_xattn, 'g_ffn': g_ffn, 'L0_xattn_Wq': _L0_xattn_in['Wq'], 'L0_xattn_Wk': _L0_xattn_in['Wk'], 'L0_xattn_Wv': _L0_xattn_in['Wv'], 'L0_xattn_Wo': _L0_xattn_in['Wo'], 'L0_ffn_W_q': _L0_ffn_in['W_q'], 'L0_ffn_scales': _L0_ffn_in['scales'], 'L0_ffn_zeros': _L0_ffn_in['zeros'], 'L0_ffn_mask': _L0_ffn_in['mask'], 'L0_ffn_scale2': _L0_ffn_in['scale2'], 'L0_ffn_bias': _L0_ffn_in['bias'], 'L1_xattn_Wq': _L1_xattn_in['Wq'], 'L1_xattn_bq': _L1_xattn_in['bq'], 'L1_xattn_Wk': _L1_xattn_in['Wk'], 'L1_xattn_bk': _L1_xattn_in['bk'], 'L1_ffn_gate_w': _L1_ffn_in['gate_w'], 'L1_ffn_expert_w': _L1_ffn_in['expert_w'], 'L1_ffn_expert_b': _L1_ffn_in['expert_b']}

def reference(x, ctx_4096, pos_BxS2, mask_BxSxS2_ik0, g_xattn, g_ffn, L0_xattn_Wq, L0_xattn_Wk, L0_xattn_Wv, L0_xattn_Wo, L0_ffn_W_q, L0_ffn_scales, L0_ffn_zeros, L0_ffn_mask, L0_ffn_scale2, L0_ffn_bias, L1_xattn_Wq, L1_xattn_bq, L1_xattn_Wk, L1_xattn_bk, L1_ffn_gate_w, L1_ffn_expert_w, L1_ffn_expert_b):
    import jax
    import jax.numpy as jnp

    def _L0_xattn_ref(query, key, value, position_ids, src_mask, Wq, Wk, Wv, Wo):
        import jax, jax.numpy as jnp
        import numpy as np
        B, S, E = (2, 256, 512)
        H, KVH, D = (32, 8, 128)
        GROUPS = H // KVH
        MAX_POS = 512
        ROPE_THETA = 10000.0

        def _rope_tables(max_pos, dim, theta):
            inv_freq = 1.0 / theta ** (jnp.arange(0, dim, 2, dtype=jnp.float32) / dim)
            t = jnp.arange(max_pos, dtype=jnp.float32)
            freqs = jnp.einsum('i,j->ij', t, inv_freq)
            emb = jnp.concatenate([freqs, freqs], axis=-1)
            return (jnp.cos(emb), jnp.sin(emb))

        def _rotate_half(x):
            x1, x2 = (x[..., :x.shape[-1] // 2], x[..., x.shape[-1] // 2:])
            return jnp.concatenate([-x2, x1], axis=-1)
        nb, q_len, _ = query.shape
        q = (query @ Wq).reshape(nb, q_len, H, D).transpose(0, 2, 1, 3)
        k = (key @ Wk).reshape(nb, q_len, KVH, D).transpose(0, 2, 1, 3)
        v = (value @ Wv).reshape(nb, q_len, KVH, D).transpose(0, 2, 1, 3)
        cos_t, sin_t = _rope_tables(MAX_POS, D, ROPE_THETA)
        cos = cos_t[position_ids][:, None]
        sin = sin_t[position_ids][:, None]
        q = q * cos + _rotate_half(q) * sin
        k = k * cos + _rotate_half(k) * sin
        k = jnp.repeat(k, GROUPS, axis=1)
        v = jnp.repeat(v, GROUPS, axis=1)
        scores = jnp.einsum('bhqd,bhkd->bhqk', q, k) / jnp.sqrt(jnp.float32(D))
        mask = src_mask[:, None]
        scores = jnp.where(mask == 0, jnp.float32(-1000000000.0), scores)
        attn = jax.nn.softmax(scores, axis=-1)
        x = jnp.einsum('bhqk,bhkd->bhqd', attn, v)
        x = x.transpose(0, 2, 1, 3).reshape(nb, q_len, H * D)
        return x @ Wo

    def _L0_ffn_ref(x, W_q, scales, zeros, mask, scale2, bias):
        import jax, jax.numpy as jnp
        import numpy as np
        GROUP = 64

        def _dequantize_sparse_sinq(W_q, scales, zeros, mask, scale2, dtype):
            K, N = W_q.shape
            G = N // GROUP
            Wg = W_q.astype(dtype).reshape(K, G, GROUP)
            W = (Wg - zeros[:, :, None]) * scales[:, :, None]
            W = W.reshape(K, N) * scale2
            W = W * mask.astype(dtype)
            return W
        W = _dequantize_sparse_sinq(W_q, scales, zeros, mask, scale2, x.dtype)
        out = jnp.einsum('bsn,kn->bsk', x, W) + bias
        return out

    def _L1_xattn_ref(text, features, Wq, bq, Wk, bk):
        import jax, jax.numpy as jnp
        import numpy as np
        TEXT_DIM = 512
        FEATURE_DIM = 512

        def _xavier_uniform(key, shape):
            fan_in, fan_out = (shape[1], shape[0])
            limit = float(np.sqrt(6.0 / (fan_in + fan_out)))
            return jax.random.uniform(key, shape, jnp.float32, -limit, limit)
        Q = jnp.einsum('btx,dx->btd', text, Wq) + bq
        K = jnp.einsum('bpx,dx->bpd', features, Wk) + bk
        scale = 1.0 / jnp.sqrt(jnp.asarray(K.shape[-1], K.dtype))
        scores = jnp.einsum('btd,bpd->btp', Q, K) * scale
        attn = jax.nn.softmax(scores, axis=-1)
        attended = jnp.einsum('btp,bpd->btd', attn, features)
        return attended

    def _L1_ffn_ref(x, gate_w, expert_w, expert_b):
        import jax, jax.numpy as jnp
        import numpy as np
        NUM_EXPERTS = 32
        D_MODEL = 512
        TOP_K = 2
        B, S, D = x.shape
        T = B * S
        xf = x.reshape(T, D)
        logits = xf @ gate_w.T
        w, idx = jax.lax.top_k(logits, TOP_K)
        w = jax.nn.softmax(w, axis=-1)
        combine = jnp.zeros((T, NUM_EXPERTS), dtype=x.dtype).at[jnp.arange(T)[:, None], idx].add(w)

        def body(acc, params):
            W, b, c = params
            return (acc + c[:, None] * (xf @ W.T + b), None)
        out, _ = jax.lax.scan(body, jnp.zeros_like(xf), (expert_w, expert_b, combine.T))
        return out.reshape(B, S, D)
    x = x + jnp.tanh(g_xattn[0]) * _L0_xattn_ref(_layernorm(x, axis=-1), ctx_4096, ctx_4096, pos_BxS2, mask_BxSxS2_ik0, L0_xattn_Wq, L0_xattn_Wk, L0_xattn_Wv, L0_xattn_Wo)
    x = x + jnp.tanh(g_ffn[0]) * _L0_ffn_ref(_layernorm(x, axis=-1), L0_ffn_W_q, L0_ffn_scales, L0_ffn_zeros, L0_ffn_mask, L0_ffn_scale2, L0_ffn_bias)
    x = x + jnp.tanh(g_xattn[1]) * _L1_xattn_ref(_layernorm(x, axis=-1), ctx_4096, L1_xattn_Wq, L1_xattn_bq, L1_xattn_Wk, L1_xattn_bk)
    x = x + jnp.tanh(g_ffn[1]) * _L1_ffn_ref(_layernorm(x, axis=-1), L1_ffn_gate_w, L1_ffn_expert_w, L1_ffn_expert_b)
    return x

_drawn_inputs = setup_inputs


def setup_inputs(seed=0):
    import zlib

    import numpy as np

    out = dict(_drawn_inputs(seed))
    spreads = {'g_ffn': (-1.0, 0.6), 'L1_xattn_bq': (0.0, 2.0), 'L1_xattn_bk': (0.0, 2.0)}
    factors = {'L0_ffn_bias': 3.391,
     'L1_xattn_Wq': 8.0,
     'L1_xattn_Wk': 8.0,
     'L1_ffn_gate_w': 8.0,
     'L1_ffn_expert_w': 8.0,
     'L1_ffn_expert_b': 172.267}
    for name, (base, spread) in spreads.items():
        noise = np.random.default_rng([zlib.crc32(name.encode()), seed]).standard_normal(out[name].shape)
        drawn = base * np.exp(spread * noise) if base else spread * noise
        out[name] = jnp.asarray(drawn.astype(out[name].dtype))
    for name, factor in factors.items():
        out[name] = (out[name] * factor).astype(out[name].dtype)
    return out
```

```python
import concourse.bass as bass
from concourse import mybir
from contextlib import ExitStack

F32 = mybir.dt.float32
F32R = mybir.dt.float32r
I32 = mybir.dt.int32
U32 = mybir.dt.uint32
I8 = mybir.dt.int8
ALU = mybir.AluOpType
ACT = mybir.ActivationFunctionType
AX = mybir.AxisListType

P = 128
NB = 8
S = 128
T = NB * S
E = 512
KC = E // P
H, KVH, D = 32, 8, 128
GR = H // KVH
MAX_POS = 512
NX = 32
GROUP = 64
NG = E // GROUP
EPS = 1e-5
MASKED = -1e9


def wait(engine, semaphore, g, per, count):
    assert per + count > 0
    value = g * per + count
    if not (isinstance(g, int) and value <= 0):
        engine.wait_ge(semaphore, value)


def program(nc, a, out):
    root = ExitStack()
    with root:
        def sb(name, shape, dt=F32, ctx=root):
            return ctx.enter_context(nc.sbuf_tensor(name, shape, dt))

        def sem(name):
            return root.enter_context(nc.semaphore(name))

        x = sb("x", [P, NB, E])
        xT_hi = sb("xT_hi", [P, KC, T], F32R)
        xT_lo = sb("xT_lo", [P, KC, T], F32R)
        cT_hi = sb("cT_hi", [P, KC, T], F32R)
        cT_lo = sb("cT_lo", [P, KC, T], F32R)
        ident = sb("ident", [P, P])
        gates = sb("gates", [P, 4])
        stats = sb("stats", [P, NB, 6])
        meanvar = sb("meanvar", [P, NB, 2])
        spread = sb("spread", [P, NB])
        rstd = sb("rstd", [P, NB])
        psum = [root.enter_context(nc.psum_tensor(f"bank{i}", [P, 512], F32)) for i in range(8)]

        ln_stats, ln_aggr, ln_var, ln_std, ln_rstd = (sem(f"ln_{n}") for n in ("stats", "aggr", "var", "std", "rstd"))
        ln_norm, ln_turned, ln_hi, ln_lo = (sem(f"ln_{n}") for n in ("norm", "turned", "hi", "lo"))

        def norm_vector(dve, n, xn):
            for t in range(NB):
                nc.vector.bn_stats(stats[:, t, :], x[:, t, :]).then_inc(ln_stats, 1)
            for t in range(NB):
                dve.wait_ge(ln_stats, n * NB + t + 1)
                nc.vector.bn_aggr(meanvar[:, t, :], stats[:, t, :]).then_inc(ln_aggr, 1)
            dve.wait_ge(ln_aggr, (n + 1) * NB)
            nc.vector.tensor_scalar_add(spread[:, :], meanvar[:, :, 1], EPS).then_inc(ln_var, 1)
            dve.wait_ge(ln_std, n + 1)
            nc.vector.reciprocal(rstd[:, :], spread[:, :]).then_inc(ln_rstd, 1)
            dve.wait_ge(ln_rstd, n + 1)

            def rest(t):
                dve.wait_ge(ln_hi, n * NB + t + 1)
                tok = slice(t * P, (t + 1) * P)
                nc.vector.tensor_tensor(xT_lo[:, :, tok], psum[t % 2][:, :].rearrange("p (c t) -> p c t", c=KC),
                                        xT_hi[:, :, tok].bitcast(F32), ALU.subtract).then_inc(ln_lo, 1)

            for t in range(NB):
                if t >= 2:
                    dve.wait_ge(ln_turned, n * NB + t - 1)
                nc.vector.tensor_scalar(xn[:, t % 2, :], x[:, t, :], meanvar[:, t, 0:1], rstd[:, t:t + 1],
                                        ALU.subtract, ALU.mult).then_inc(ln_norm, 1)
                if t >= 1:
                    rest(t - 1)
            rest(NB - 1)

        def norm_scalar(act, n):
            act.wait_ge(ln_var, n + 1)
            nc.scalar.activation(spread[:, :], spread[:, :], ACT.Sqrt).then_inc(ln_std, 1)
            for t in range(NB):
                act.wait_ge(ln_turned, n * NB + t + 1)
                nc.scalar.activation(xT_hi[:, :, t * P:(t + 1) * P],
                                     psum[t % 2][:, :].rearrange("p (c t) -> p c t", c=KC), ACT.Copy).then_inc(ln_hi, 1)

        def norm_tensor(pe, n, xn):
            for t in range(NB):
                pe.wait_ge(ln_norm, n * NB + t + 1)
                if t >= 2:
                    pe.wait_ge(ln_lo, n * NB + t - 1)
                for c in range(KC):
                    mm = nc.tensor.transpose(psum[t % 2][:, c * P:(c + 1) * P], xn[:, t % 2, c * P:(c + 1) * P], ident[:, :])
                mm.then_inc(ln_turned, 1)

        def product(out_, hi, lo, r_hi, r_lo, start, stop):
            nc.tensor.matmul(out_, hi, r_hi, start=start, stop=False)
            nc.tensor.matmul(out_, hi, r_lo, start=False, stop=False)
            return nc.tensor.matmul(out_, lo, r_hi, start=False, stop=stop)

        phaseA = ExitStack()
        cosT = sb("cosT", [P, T], ctx=phaseA)
        sinT = sb("sinT", [P, T], ctx=phaseA)
        open_key = sb("open_key", [P, NB, S], I8, phaseA)
        key_scale = sb("key_scale", [P, 1], ctx=phaseA)
        filled = sb("filled", [P, NB, GR, S], ctx=phaseA)

        with ExitStack() as ctx:
            xn = sb("xn0", [P, 2, E], ctx=ctx)
            ctx_raw = sb("ctx_raw", [P, KC, T], ctx=ctx)
            mask_raw = sb("mask_raw", [P, NB, S], I32, ctx)
            pos_raw = sb("pos_raw", [P, NB], I32, ctx)
            pos_neg = sb("pos_neg", [P, NB], ctx=ctx)
            pos_wrapped = sb("pos_wrapped", [P, NB], ctx=ctx)
            pos_row = sb("pos_row", [P, NB], U32, ctx)
            rotary = sb("rotary", [P, NB, 2 * D], ctx=ctx)
            gates_raw = sb("gates_raw", [P, 4], ctx=ctx)
            in_x, in_small, in_pos, in_mask, in_ctx = (sem(f"in_{n}") for n in ("x", "small", "pos", "mask", "ctx"))
            in_rot = sem("in_rot")
            pos_step, rot_turned, rot_kept, ctx_hi, mask_done, gate_done, fill_done, ctx_lo = (
                sem(n) for n in ("pos_step", "rot_turned", "rot_kept", "ctx_hi", "mask_done", "gate_done", "fill_done", "ctx_lo"))
            with nc.Block() as block:
                @block.sync
                def _(sp):
                    sp.dma_start(x[:, :, :], a["x"]).then_inc(in_x, 16)
                    sp.dma_start(ident[:, :], a["ident"]).then_inc(in_small, 16)
                    sp.dma_start(gates_raw[:, :], a["gates"].partition_broadcast(P)).then_inc(in_small, 16)
                    sp.dma_start(ctx_raw[:, :, :], a["ctxT"]).then_inc(in_ctx, 16)
                    sp.dma_start(mask_raw[:, :, :], a["mask"]).then_inc(in_mask, 16)

                @block.gpsimd
                def _(pool):
                    pool.dma_start(pos_raw[:, :], a["pos"]).then_inc(in_pos, 16)
                    nc.gpsimd.memset(filled[:, :, :, :], MASKED).then_inc(fill_done, 1)
                    nc.gpsimd.memset(key_scale[:, :], float(D) ** -0.5).then_inc(fill_done, 1)
                    pool.wait_ge(pos_step, 3)
                    for t in range(NB):
                        pool.indirect_dma_start(
                            out=rotary[:, t, :], out_offset=None, in_=a["rotary"],
                            in_offset=bass.IndirectOffsetOnAxis(ap=pos_row[:, t:t + 1], axis=0)).then_inc(in_rot, 16)
                    for c in range(KC):
                        pool.wait_ge(ctx_hi, c + 1)
                        nc.gpsimd.tensor_tensor(cT_lo[:, c, :], ctx_raw[:, c, :], cT_hi[:, c, :].bitcast(F32),
                                                ALU.subtract).then_inc(ctx_lo, 1)

                @block.scalar
                def _(act):
                    act.wait_ge(in_small, 32)
                    nc.scalar.activation(gates[:, :], gates_raw[:, :], ACT.Tanh).then_inc(gate_done, 1)
                    norm_scalar(act, 0)
                    act.wait_ge(in_ctx, 16)
                    for c in range(KC):
                        nc.scalar.activation(cT_hi[:, c, :], ctx_raw[:, c, :], ACT.Copy).then_inc(ctx_hi, 1)

                @block.vector
                def _(dve):
                    dve.wait_ge(in_pos, 16)
                    nc.vector.tensor_scalar(pos_neg[:, :], pos_raw[:, :], 0.0, float(MAX_POS), ALU.is_lt, ALU.mult).then_inc(pos_step, 1)
                    dve.wait_ge(pos_step, 1)
                    nc.vector.tensor_tensor(pos_wrapped[:, :], pos_raw[:, :], pos_neg[:, :], ALU.add).then_inc(pos_step, 1)
                    dve.wait_ge(pos_step, 2)
                    nc.vector.tensor_scalar(pos_row[:, :], pos_wrapped[:, :], 0.0, float(MAX_POS - 1), ALU.max, ALU.min).then_inc(pos_step, 1)
                    dve.wait_ge(in_x, 16)
                    norm_vector(dve, 0, xn)
                    dve.wait_ge(in_mask, 16)
                    nc.vector.tensor_scalar(open_key[:, :, :], mask_raw[:, :, :], 0.0, None, ALU.not_equal).then_inc(mask_done, 1)
                    for t in range(NB):
                        dve.wait_ge(rot_turned, t + 1)
                        tok = slice(t * P, (t + 1) * P)
                        nc.vector.tensor_copy(cosT[:, tok], psum[2 + t % 2][:, 0:P]).then_inc(rot_kept, 1)
                        nc.vector.tensor_copy(sinT[:, tok], psum[2 + t % 2][:, P:2 * P]).then_inc(rot_kept, 1)

                @block.tensor
                def _(pe):
                    pe.wait_ge(in_small, 32)
                    norm_tensor(pe, 0, xn)
                    pe.wait_ge(in_rot, 16 * NB)
                    for t in range(NB):
                        if t >= 2:
                            pe.wait_ge(rot_kept, 2 * (t - 1))
                        nc.tensor.transpose(psum[2 + t % 2][:, 0:P], rotary[:, t, 0:D], ident[:, :])
                        nc.tensor.transpose(psum[2 + t % 2][:, P:2 * P], rotary[:, t, D:2 * D], ident[:, :]).then_inc(rot_turned, 1)

        with phaseA as ctx:
            HALF = T // 2
            PAIR = 2 * S
            raw_big = sb("raw_big", [P, 4 * 512], ctx=ctx)
            raw_k = sb("raw_k", [P, KC, D], ctx=ctx)
            raw_v = sb("raw_v", [P, KC, D], ctx=ctx)
            wq_hi, wq_lo = (sb(f"wq_{n}", [P, KC, GR * D], F32R, ctx) for n in ("hi", "lo"))
            wo_hi, wo_lo = (sb(f"wo_{n}", [P, GR, E], F32R, ctx) for n in ("hi", "lo"))
            wk_hi, wk_lo = (sb(f"wk_{n}", [P, KC, D], F32R, ctx) for n in ("hi", "lo"))
            wv_hi, wv_lo = (sb(f"wv_{n}", [P, KC, D], F32R, ctx) for n in ("hi", "lo"))
            kT = sb("kT", [P, T], ctx=ctx)
            vT = sb("vT", [P, T], ctx=ctx)
            v_hi, v_lo = (sb(f"v_{n}", [P, NB, D], F32R, ctx) for n in ("hi", "lo"))
            qT = sb("qT", [P, 2, GR, PAIR], ctx=ctx)
            straight = sb("straight", [P, 2, 512], ctx=ctx)
            turned = sb("turned", [P, 2, 512], ctx=ctx)
            probs = sb("probs", [P, 2, GR, S], ctx=ctx)
            pT_hi, pT_lo = (sb(f"pT_{n}", [P, 2, GR * S], F32R, ctx) for n in ("hi", "lo"))
            oT_hi, oT_lo = (sb(f"oT_{n}", [P, 2, GR, S], F32R, ctx) for n in ("hi", "lo"))
            negmax = sb("negmax", [P, NB, GR], ctx=ctx)
            gatepost = sb("gatepost", [P, 1], ctx=ctx)
            total = sb("total", [P, NB, GR], ctx=ctx)
            invtotal = sb("invtotal", [P, NB, GR], ctx=ctx)

            bank_rope = psum[0:2]
            bank_scores = psum[2:4]
            bank_pT, bank_o, bank_y, bank_v = psum[4:8]

            big_in, kv_in = sem("big_in"), sem("kv_in")
            wq_hi_s, wq_lo_s, wo_hi_s, wo_lo_s, wkv_hi_s, wkv_lo_s = (
                sem(n) for n in ("wq_hi_done", "wq_lo_done", "wo_hi_done", "wo_lo_done", "wkv_hi_done", "wkv_lo_done"))
            proj_mm, rope_mul, rope_add, rope_sum = (sem(n) for n in ("proj_mm", "rope_mul", "rope_add", "rope_sum"))
            v_mm, v_kept, v_turned, v_hi_s, v_lo_s = (sem(n) for n in ("v_mm", "v_kept", "v_turned", "v_hi_done", "v_lo_done"))
            score_mm, score_kept, score_max, exp_done, inv_done, probs_done = (
                sem(n) for n in ("score_mm", "score_kept", "score_max", "exp_done", "inv_done", "probs_done"))
            pT_mm, pT_hi_s, pT_lo_s = sem("pT_mm"), sem("pT_hi_done"), sem("pT_lo_done")
            o_mm, o_hi_s, o_lo_s = sem("o_mm"), sem("o_hi_done"), sem("o_lo_done")
            y_mm, y_added = sem("y_mm"), sem("y_added")

            ITEMS, UNITS = 10, NB
            ITEMS_OF_STEP = [[5], [6], [7], [8], [9], [10], [11], [12, 13, 14]]
            FIRST_ITEMS = [0, 1, 2, 3, 4]

            def steps(g):
                whole = not isinstance(g, int)
                for step in range(3 if not whole and g == KVH else UNITS):
                    def unit(u):
                        if not whole and (g * UNITS + u < 0 or g * UNITS + u >= KVH * UNITS):
                            return None
                        return u
                    items = [] if not whole and g == KVH else ITEMS_OF_STEP[step]
                    if not whole and g == KVH - 1:
                        items = [i for i in items if i < ITEMS]
                    yield step, unit(step), items, unit(step - 1), unit(step - 2), unit(step - 3)

            def more(g):
                return not isinstance(g, int) or g < KVH - 1

            def place_of(item):
                i = item % ITEMS
                if i in (2, 3):
                    tok = slice((i - 2) * HALF, (i - 1) * HALF)
                    return kT[:, tok], tok, True
                pair, j = (0, i) if i < 2 else ((i - 2) // 2, i % 2)
                return qT[:, pair % 2, 2 * j:2 * j + 2, :], slice(pair * PAIR, (pair + 1) * PAIR), False

            def shaped(ap, key):
                return ap if key else ap.rearrange("p (h t) -> p h t", h=2)

            def spread_over(table, key):
                return table if key else table.unsqueeze(1).broadcast_to([table.shape[0], 2, PAIR])

            with nc.Block() as block:
                @block.sync
                def _(sp):
                    def load(g, first):
                        if not first:
                            sp.wait_ge(wkv_lo_s, 2 * g)
                        sp.dma_start(raw_k[:, :, :], a["wk"][bass.ds(g, 1)].rearrange("o p c n -> p (o c) n")).then_inc(kv_in, 16)
                        sp.dma_start(raw_v[:, :, :], a["wv"][bass.ds(g, 1)].rearrange("o p c n -> p (o c) n")).then_inc(kv_in, 16)
                        if not first:
                            sp.wait_ge(wo_lo_s, GR * g)
                        sp.dma_start(raw_big[:, :], a["wq"][bass.ds(g, 1)].rearrange("o p n -> p (o n)")).then_inc(big_in, 16)
                        sp.wait_ge(wq_lo_s, 2 * g + 2)
                        sp.dma_start(raw_big[:, :], a["wo"][bass.ds(g, 1)].rearrange("o p n -> p (o n)")).then_inc(big_in, 16)

                    load(0, True)
                    with sp.Fori(1, KVH) as g:
                        load(g, False)

                @block.gpsimd
                def _(pool):
                    def queries_weights(g, half):
                        cols = slice(half * 2 * D, (half + 1) * 2 * D)
                        wait(pool, wq_hi_s, g, 2, half + 1)
                        nc.gpsimd.tensor_tensor(wq_lo[:, :, cols], raw_big[:, :].rearrange("p (c n) -> p c n", c=KC)[:, :, cols],
                                                wq_hi[:, :, cols].bitcast(F32), ALU.subtract).then_inc(wq_lo_s, 1)

                    def keys_values_weights(g):
                        wait(pool, wkv_hi_s, g, 2, 2)
                        nc.gpsimd.tensor_tensor(wk_lo[:, :, :], raw_k[:, :, :], wk_hi[:, :, :].bitcast(F32), ALU.subtract).then_inc(wkv_lo_s, 1)
                        nc.gpsimd.tensor_tensor(wv_lo[:, :, :], raw_v[:, :, :], wv_hi[:, :, :].bitcast(F32), ALU.subtract).then_inc(wkv_lo_s, 1)

                    def out_weights(g):
                        for h in range(GR):
                            wait(pool, wo_hi_s, g, GR, h + 1)
                            nc.gpsimd.tensor_tensor(wo_lo[:, h, :], raw_big[:, h * E:(h + 1) * E],
                                                    wo_hi[:, h, :].bitcast(F32), ALU.subtract).then_inc(wo_lo_s, 1)

                    def item_sum(g, item):
                        k = item % 2
                        dst, _, key = place_of(item)
                        wait(pool, rope_mul, g, ITEMS, item + 1)
                        if key:
                            nc.gpsimd.tensor_tensor(straight[:, k, :], straight[:, k, :], turned[:, k, :], ALU.add).then_inc(rope_add, 1)
                            wait(pool, rope_add, g, 2, item % ITEMS - 1 + (2 if item >= ITEMS else 0))
                            nc.gpsimd.tensor_tensor(dst, straight[:, k, :], key_scale[:, :].broadcast_to([P, 512]), ALU.mult).then_inc(rope_sum, 1)
                        else:
                            nc.gpsimd.tensor_tensor(dst, shaped(straight[:, k, :], key), shaped(turned[:, k, :], key), ALU.add).then_inc(rope_sum, 1)

                    def normalise(g, u):
                        wait(pool, inv_done, g, UNITS, u + 1)
                        nc.gpsimd.tensor_tensor(probs[:, u % 2, :, :], probs[:, u % 2, :, :],
                                                invtotal[:, u % UNITS, :].unsqueeze(2).broadcast_to([P, GR, S]), ALU.mult).then_inc(probs_done, 1)

                    def group(g):
                        for step, u, items, _, _, _ in steps(g):
                            if step == 4 and more(g):
                                queries_weights(g + 1, 0)
                            if step == 5 and more(g):
                                queries_weights(g + 1, 1)
                            if u is not None and not items:
                                normalise(g, u)
                            for item in items:
                                item_sum(g, item)
                                if item == items[0]:
                                    normalise(g, u)
                            if step == 2 and u is not None:
                                out_weights(g)
                            if step == 3 and more(g):
                                keys_values_weights(g + 1)

                    queries_weights(0, 0)
                    queries_weights(0, 1)
                    keys_values_weights(0)
                    for item in FIRST_ITEMS:
                        item_sum(0, item)
                    group(0)
                    with pool.Fori(1, KVH - 1) as g:
                        group(g)
                    group(KVH - 1)
                    group(KVH)

                @block.scalar
                def _(act):
                    def queries_weights(g, half):
                        cols = slice(half * 2 * D, (half + 1) * 2 * D)
                        if half == 0:
                            wait(act, big_in, g, 32, 16)
                        nc.scalar.activation(wq_hi[:, :, cols], raw_big[:, :].rearrange("p (c n) -> p c n", c=KC)[:, :, cols], ACT.Copy).then_inc(wq_hi_s, 1)

                    def keys_values_weights(g):
                        wait(act, kv_in, g, 32, 32)
                        nc.scalar.activation(wk_hi[:, :, :], raw_k[:, :, :], ACT.Copy).then_inc(wkv_hi_s, 1)
                        nc.scalar.activation(wv_hi[:, :, :], raw_v[:, :, :], ACT.Copy).then_inc(wkv_hi_s, 1)

                    def out_weights(g):
                        wait(act, big_in, g, 32, 32)
                        wait(act, y_mm, g, UNITS, 0)
                        for h in range(GR):
                            nc.scalar.activation(wo_hi[:, h, :], raw_big[:, h * E:(h + 1) * E], ACT.Copy).then_inc(wo_hi_s, 1)

                    def exps(g, u):
                        wait(act, score_max, g, UNITS, u + 1)
                        wait(act, pT_mm, g, UNITS, u - 1)
                        for h in range(GR):
                            ex = nc.scalar.activation(probs[:, u % 2, h, :], filled[:, u % UNITS, h, :], ACT.Exp,
                                                      bias=negmax[:, u % UNITS, h:h + 1], accum_out=total[:, u % UNITS, h:h + 1])
                        ex.then_inc(exp_done, 1)

                    def probs_upper(g, u):
                        wait(act, pT_mm, g, UNITS, u + 1)
                        wait(act, o_mm, g, UNITS, u - 1)
                        nc.scalar.activation(pT_hi[:, u % 2, :], bank_pT[:, :], ACT.Copy).then_inc(pT_hi_s, 1)

                    def out_upper(g, u):
                        wait(act, o_mm, g, UNITS, u + 1)
                        wait(act, y_mm, g, UNITS, u - 1)
                        nc.scalar.activation(oT_hi[:, u % 2, :, :], bank_o[:, :].rearrange("p (h t) -> p h t", h=GR), ACT.Copy).then_inc(o_hi_s, 1)

                    def keep_values(g, half):
                        wait(act, v_mm, g, 2, half + 1)
                        nc.scalar.activation(vT[:, half * HALF:(half + 1) * HALF], bank_v[:, :], ACT.Copy).then_inc(v_kept, 1)

                    def values_upper(g):
                        for half in range(2):
                            wait(act, v_turned, g, 2, half + 1)
                            nc.scalar.activation(v_hi[:, 4 * half:4 * half + 4, :], bank_v[:, :].rearrange("p (b d) -> p b d", b=4),
                                                 ACT.Copy).then_inc(v_hi_s, 1)

                    def group(g):
                        for step, u, items, turn, attend, _ in steps(g):
                            if step == 4 and more(g):
                                wait(act, proj_mm, g, ITEMS, 9)
                                queries_weights(g + 1, 0)
                            if step == 5 and more(g):
                                wait(act, proj_mm, g, ITEMS, 10)
                                queries_weights(g + 1, 1)
                            if u is not None:
                                exps(g, u)
                            if step < 2 and u is not None:
                                keep_values(g, step)
                            if attend is not None:
                                out_upper(g, attend)
                            if step == 1 and u is not None:
                                values_upper(g)
                            if turn is not None:
                                probs_upper(g, turn)
                            if step == 2 and u is not None:
                                out_weights(g)
                            if step == 3 and more(g):
                                wait(act, v_mm, g, 2, 2)
                                keys_values_weights(g + 1)

                    queries_weights(0, 0)
                    queries_weights(0, 1)
                    keys_values_weights(0)
                    group(0)
                    with act.Fori(1, KVH - 1) as g:
                        group(g)
                    group(KVH - 1)
                    group(KVH)

                @block.vector
                def _(dve):
                    def item_products(g, item):
                        _, tok, key = place_of(item)
                        k = item % 2
                        wait(dve, proj_mm, g, ITEMS, item + 1)
                        wait(dve, rope_sum, g, ITEMS, item - 1)
                        bank = bank_rope[k]
                        nc.vector.tensor_tensor(shaped(straight[:, k, :], key), shaped(bank[:, :], key),
                                                spread_over(cosT[:, tok], key), ALU.mult)
                        for src, dst in ((slice(0, 64), slice(64, 128)), (slice(64, 128), slice(0, 64))):
                            last = nc.vector.tensor_tensor(shaped(turned[dst, k, :], key), shaped(bank[src, :], key),
                                                           spread_over(sinT[src, tok], key), ALU.mult)
                        last.then_inc(rope_mul, 1)

                    def keep_scores(g, u):
                        wait(dve, exp_done, g, UNITS, u - UNITS + 1)
                        wait(dve, score_mm, g, UNITS, u + 1)
                        nc.vector.memset(gatepost[:, :], 0.0)
                        for h in range(GR):
                            kept = nc.vector.copy_predicated(filled[:, u, h, :], open_key[:, u, :], bank_scores[u % 2][:, h * S:(h + 1) * S])
                        kept.then_inc(score_kept, 1)
                        wait(dve, score_kept, g, UNITS, u + 1)
                        nc.vector.tensor_reduce(negmax[:, u, :], filled[:, u, :, :], AX.X, ALU.max, negate=True).then_inc(score_max, 1)

                    def invert(g, u):
                        wait(dve, exp_done, g, UNITS, u + 1)
                        nc.vector.reciprocal(invtotal[:, u, :], total[:, u, :]).then_inc(inv_done, 1)

                    def probs_rest(g, u):
                        wait(dve, pT_hi_s, g, UNITS, u + 1)
                        nc.vector.tensor_tensor(pT_lo[:, u % 2, :], bank_pT[:, :], pT_hi[:, u % 2, :].bitcast(F32), ALU.subtract).then_inc(pT_lo_s, 1)

                    def out_rest(g, u):
                        wait(dve, o_hi_s, g, UNITS, u + 1)
                        nc.vector.tensor_tensor(oT_lo[:, u % 2, :, :], bank_o[:, :].rearrange("p (h t) -> p h t", h=GR),
                                                oT_hi[:, u % 2, :, :].bitcast(F32), ALU.subtract).then_inc(o_lo_s, 1)

                    def add_out(g, u):
                        wait(dve, y_mm, g, UNITS, u + 1)
                        nc.vector.scalar_tensor_tensor(x[:, u % UNITS, :], bank_y[:, :], gates[:, 0:1], x[:, u % UNITS, :], ALU.mult, ALU.add).then_inc(y_added, 1)

                    def values_rest(g):
                        for half in range(2):
                            wait(dve, v_hi_s, g, 2, half + 1)
                            rows = slice(4 * half, 4 * half + 4)
                            nc.vector.tensor_tensor(v_lo[:, rows, :], bank_v[:, :].rearrange("p (b d) -> p b d", b=4),
                                                    v_hi[:, rows, :].bitcast(F32), ALU.subtract).then_inc(v_lo_s, 1)

                    def group(g):
                        for step, u, items, turn, attend, out_unit in steps(g):
                            if u is not None:
                                keep_scores(g, u)
                            for item in items[:1]:
                                item_products(g, item)
                            if u is not None:
                                invert(g, u)
                            for item in items[1:]:
                                item_products(g, item)
                            if attend is not None:
                                out_rest(g, attend)
                            if step == 1 and u is not None:
                                values_rest(g)
                            if out_unit is not None:
                                add_out(g, out_unit)
                            if turn is not None:
                                probs_rest(g, turn)

                    for item in FIRST_ITEMS:
                        item_products(0, item)
                    group(0)
                    with dve.Fori(1, KVH - 1) as g:
                        group(g)
                    group(KVH - 1)
                    group(KVH)

                @block.tensor
                def _(pe):
                    def project(g, item):
                        _, tok, key = place_of(item)
                        own = item % ITEMS
                        ahead = 1 if item >= ITEMS else 0
                        j = own % 2
                        if key:
                            wait(pe, wkv_lo_s, g, 2, 2 * ahead + 2)
                        else:
                            wait(pe, wq_lo_s, g, 2, 2 * ahead + j + 1)
                        wait(pe, rope_mul, g, ITEMS, item - 1)
                        bank = bank_rope[item % 2]
                        if key:
                            for c in range(KC):
                                mm = product(bank[:, :], wk_hi[:, c, :], wk_lo[:, c, :], cT_hi[:, c, tok], cT_lo[:, c, tok], c == 0, c == KC - 1)
                        else:
                            for k in range(2):
                                h = 2 * j + k
                                cols = slice(h * D, (h + 1) * D)
                                for c in range(KC):
                                    mm = product(bank[:, k * PAIR:(k + 1) * PAIR], wq_hi[:, c, cols], wq_lo[:, c, cols],
                                                 xT_hi[:, c, tok], xT_lo[:, c, tok], c == 0, c == KC - 1)
                        mm.then_inc(proj_mm, 1)

                    def make_values(g, half):
                        wait(pe, wkv_lo_s, g, 2, 2)
                        if half == 0:
                            wait(pe, v_lo_s, g, 2, 0)
                        else:
                            wait(pe, v_kept, g, 2, 1)
                        tok = slice(half * HALF, (half + 1) * HALF)
                        for c in range(KC):
                            mm = product(bank_v[:, :], wv_hi[:, c, :], wv_lo[:, c, :], cT_hi[:, c, tok], cT_lo[:, c, tok], c == 0, c == KC - 1)
                        mm.then_inc(v_mm, 1)

                    def turn_values(g, half):
                        if half == 0:
                            wait(pe, v_kept, g, 2, 2)
                        else:
                            wait(pe, v_lo_s, g, 2, 1)
                        for b in range(4):
                            mm = nc.tensor.transpose(bank_v[:, b * D:(b + 1) * D], vT[:, (4 * half + b) * S:(4 * half + b + 1) * S], ident[:, :])
                        mm.then_inc(v_turned, 1)

                    def score(g, u):
                        if u % 2 == 0:
                            wait(pe, rope_sum, g, ITEMS, 4 + u if u else 3)
                        wait(pe, score_kept, g, UNITS, u - 1)
                        keys = slice(u * S, (u + 1) * S)
                        q = slice((u % 2) * S, (u % 2 + 1) * S)
                        for h in range(GR):
                            mm = nc.tensor.matmul(bank_scores[u % 2][:, h * S:(h + 1) * S], qT[:, (u // 2) % 2, h, q], kT[:, keys], start=True, stop=True)
                        mm.then_inc(score_mm, 1)

                    def turn_probs(g, u):
                        wait(pe, probs_done, g, UNITS, u + 1)
                        wait(pe, pT_lo_s, g, UNITS, u)
                        for h in range(GR):
                            mm = nc.tensor.transpose(bank_pT[:, h * S:(h + 1) * S], probs[:, u % 2, h, :], ident[:, :])
                        mm.then_inc(pT_mm, 1)

                    def attend(g, u):
                        if u == 0:
                            wait(pe, v_lo_s, g, 2, 2)
                        wait(pe, pT_lo_s, g, UNITS, u + 1)
                        wait(pe, o_lo_s, g, UNITS, u)
                        product(bank_o[:, :], v_hi[:, u % UNITS, :], v_lo[:, u % UNITS, :], pT_hi[:, u % 2, :], pT_lo[:, u % 2, :], True, True).then_inc(o_mm, 1)

                    def project_out(g, u):
                        wait(pe, o_lo_s, g, UNITS, u + 1)
                        wait(pe, y_added, g, UNITS, u)
                        for h in range(GR):
                            if u == 0:
                                wait(pe, wo_lo_s, g, GR, h + 1)
                            mm = product(bank_y[:, :], oT_hi[:, u % 2, h, :], oT_lo[:, u % 2, h, :], wo_hi[:, h, :], wo_lo[:, h, :], h == 0, h == GR - 1)
                        mm.then_inc(y_mm, 1)

                    def group(g):
                        for step, u, items, turn, att, out_unit in steps(g):
                            if u is not None:
                                score(g, u)
                            for item in items:
                                project(g, item)
                            if step < 2 and u is not None:
                                make_values(g, step)
                            if att is not None:
                                attend(g, att)
                            if step == 1 and u is not None:
                                turn_values(g, 0)
                            if out_unit is not None:
                                project_out(g, out_unit)
                            if step == 1 and u is not None:
                                turn_values(g, 1)
                            if turn is not None:
                                turn_probs(g, turn)

                    for item in FIRST_ITEMS:
                        project(0, item)
                    group(0)
                    with pe.Fori(1, KVH - 1) as g:
                        group(g)
                    group(KVH - 1)
                    group(KVH)

        with ExitStack() as ctx:
            xn = sb("xn1", [P, 2, E], ctx=ctx)
            wint = sb("wint", [P, KC, E], I32, ctx)
            wmask = sb("wmask", [P, KC, E], I32, ctx)
            scales = sb("scales", [P, KC, NG], ctx=ctx)
            zeros = sb("zeros", [P, KC, NG], ctx=ctx)
            scale2 = sb("scale2", [P, KC], ctx=ctx)
            weight = sb("weight", [P, KC, E], ctx=ctx)
            fmask = sb("fmask", [P, KC, E], ctx=ctx)
            f_float = sem("f_float")
            wT_hi, wT_lo = (sb(f"wT_{n}", [P, KC, E], F32R, ctx) for n in ("hi", "lo"))
            bias = sb("bias", [P, E], ctx=ctx)
            summed = sb("summed", [P, 2, E], ctx=ctx)
            f_in, f_deq, f_turned, f_hi, f_lo, f_mm, f_sum, f_added = (
                sem(f"f_{n}") for n in ("in", "deq", "turned", "hi", "lo", "mm", "sum", "added"))

            with nc.Block() as block:
                @block.sync
                def _(sp):
                    for dst, src in ((wint, "wint"), (scales, "scales"), (zeros, "zeros"), (wmask, "wmask")):
                        sp.dma_start(dst[:, :, :], a[src]).then_inc(f_in, 16)
                    sp.dma_start(scale2[:, :], a["scale2"]).then_inc(f_in, 16)
                    sp.dma_start(bias[:, :], a["fbias"].partition_broadcast(P)).then_inc(f_in, 16)

                @block.gpsimd
                def _(pool):
                    pool.wait_ge(f_in, 16 * 6)
                    pool.wait_ge(f_float, 2)
                    shape = [P, KC * NG, GROUP]
                    wide = weight[:, :, :].rearrange("p c (g n) -> p (c g) n", g=NG)
                    nc.gpsimd.tensor_tensor(wide, wide,
                                            zeros[:, :, :].rearrange("p c g -> p (c g)").unsqueeze(2).broadcast_to(shape), ALU.subtract).then_inc(f_deq, 1)
                    pool.wait_ge(f_deq, 1)
                    nc.gpsimd.tensor_tensor(wide, wide, scales[:, :, :].rearrange("p c g -> p (c g)").unsqueeze(2).broadcast_to(shape), ALU.mult).then_inc(f_deq, 1)
                    pool.wait_ge(f_deq, 2)
                    nc.gpsimd.tensor_tensor(weight[:, :, :], weight[:, :, :], scale2[:, :].unsqueeze(2).broadcast_to([P, KC, E]), ALU.mult).then_inc(f_deq, 1)
                    pool.wait_ge(f_deq, 3)
                    nc.gpsimd.tensor_tensor(weight[:, :, :], weight[:, :, :], fmask[:, :, :], ALU.mult).then_inc(f_deq, 1)

                @block.scalar
                def _(act):
                    act.wait_ge(f_in, 16 * 6)
                    nc.scalar.activation(weight[:, :, :], wint[:, :, :], ACT.Copy).then_inc(f_float, 1)
                    nc.scalar.activation(fmask[:, :, :], wmask[:, :, :], ACT.Copy).then_inc(f_float, 1)
                    norm_scalar(act, 1)
                    for c in range(KC):
                        act.wait_ge(f_turned, c + 1)
                        nc.scalar.activation(wT_hi[:, c, :], psum[2 + c % 2][:, :], ACT.Copy).then_inc(f_hi, 1)

                @block.vector
                def _(dve):
                    norm_vector(dve, 1, xn)
                    for c in range(KC):
                        dve.wait_ge(f_hi, c + 1)
                        nc.vector.tensor_tensor(wT_lo[:, c, :], psum[2 + c % 2][:, :], wT_hi[:, c, :].bitcast(F32), ALU.subtract).then_inc(f_lo, 1)
                    for t in range(NB):
                        dve.wait_ge(f_mm, t + 1)
                        nc.vector.tensor_tensor(summed[:, t % 2, :], psum[4 + t % 2][:, :], bias[:, :], ALU.add).then_inc(f_sum, 1)
                        dve.wait_ge(f_sum, t + 1)
                        nc.vector.scalar_tensor_tensor(x[:, t, :], summed[:, t % 2, :], gates[:, 2:3], x[:, t, :], ALU.mult, ALU.add).then_inc(f_added, 1)

                @block.tensor
                def _(pe):
                    norm_tensor(pe, 1, xn)
                    pe.wait_ge(f_deq, 4)
                    for c in range(KC):
                        if c >= 2:
                            pe.wait_ge(f_lo, c - 1)
                        for r in range(KC):
                            mm = nc.tensor.transpose(psum[2 + c % 2][:, r * P:(r + 1) * P], weight[:, r, c * P:(c + 1) * P], ident[:, :])
                        mm.then_inc(f_turned, 1)
                    pe.wait_ge(f_lo, KC)
                    pe.wait_ge(ln_lo, 2 * NB)
                    for t in range(NB):
                        if t >= 2:
                            pe.wait_ge(f_sum, t - 1)
                        tok = slice(t * P, (t + 1) * P)
                        for c in range(KC):
                            mm = product(psum[4 + t % 2][:, :], xT_hi[:, c, tok], xT_lo[:, c, tok], wT_hi[:, c, :], wT_lo[:, c, :], c == 0, c == KC - 1)
                        mm.then_inc(f_mm, 1)

        with ExitStack() as ctx:
            xn = sb("xn2", [P, 2, E], ctx=ctx)
            raw = sb("l1_raw", [P, 2, KC, E], ctx=ctx)
            w_hi, w_lo = (sb(f"l1_w_{n}", [P, 2, KC, E], F32R, ctx) for n in ("hi", "lo"))
            b1 = sb("l1_bias", [P, 2, KC], ctx=ctx)
            c_raw = sb("l1_ctx", [P, NB, E], ctx=ctx)
            c_hi, c_lo = (sb(f"l1_ctx_{n}", [P, NB, E], F32R, ctx) for n in ("hi", "lo"))
            k1_hi, k1_lo, q1_hi, q1_lo = (sb(f"l1_{n}", [P, KC, T // 2], F32R, ctx) for n in ("k_hi", "k_lo", "q_hi", "q_lo"))
            l1p = sb("l1_probs", [P, 4, S], ctx=ctx)
            l1pT_hi, l1pT_lo = (sb(f"l1_pT_{n}", [P, 4 * S], F32R, ctx) for n in ("hi", "lo"))
            l1max = sb("l1_max", [P, 4], ctx=ctx)
            l1nb = sb("l1_nb", [P, 4], ctx=ctx)
            l1sum = sb("l1_sum", [P, 4], ctx=ctx)
            l1inv = sb("l1_inv", [P, 4], ctx=ctx)
            SC1 = float(E) ** -0.5
            (g_in, g_whi, g_wlo, g_chi, g_clo, g_mm, g_hi, g_lo, g_smm, g_max, g_nb, g_exp, g_inv, g_norm,
             g_turned, g_phi, g_plo, g_omm, g_added) = (sem(f"g_{n}") for n in (
                 "in", "whi", "wlo", "chi", "clo", "mm", "hi", "lo", "smm", "max", "nb", "exp", "inv", "norm", "turned",
                 "phi", "plo", "omm", "added"))
            with nc.Block() as block:
                @block.sync
                def _(sp):
                    sp.dma_start(raw[:, 0, :, :], a["wk1"]).then_inc(g_in, 16)
                    sp.dma_start(raw[:, 1, :, :], a["wq1"]).then_inc(g_in, 16)
                    sp.dma_start(b1[:, :, :], a["b1"]).then_inc(g_in, 16)
                    sp.dma_start(c_raw[:, :, :], a["ctx"]).then_inc(g_in, 16)

                @block.gpsimd
                def _(pool):
                    for w in range(2):
                        pool.wait_ge(g_whi, w + 1)
                        nc.gpsimd.tensor_tensor(w_lo[:, w, :, :], raw[:, w, :, :], w_hi[:, w, :, :].bitcast(F32), ALU.subtract).then_inc(g_wlo, 1)
                    for n in range(2):
                        rows = slice(4 * n, 4 * n + 4)
                        pool.wait_ge(g_chi, n + 1)
                        nc.gpsimd.tensor_tensor(c_lo[:, rows, :], c_raw[:, rows, :], c_hi[:, rows, :].bitcast(F32), ALU.subtract).then_inc(g_clo, 1)
                    for n in range(2):
                        pool.wait_ge(g_inv, n + 1)
                        nc.gpsimd.tensor_tensor(l1p[:, :, :], l1p[:, :, :], l1inv[:, :].unsqueeze(2).broadcast_to([P, 4, S]), ALU.mult).then_inc(g_norm, 1)

                @block.scalar
                def _(act):
                    act.wait_ge(g_in, 64)
                    for w in range(2):
                        nc.scalar.activation(w_hi[:, w, :, :], raw[:, w, :, :], ACT.Copy).then_inc(g_whi, 1)
                    norm_scalar(act, 2)
                    for n in range(2):
                        rows = slice(4 * n, 4 * n + 4)
                        nc.scalar.activation(c_hi[:, rows, :], c_raw[:, rows, :], ACT.Copy).then_inc(g_chi, 1)
                    for n in range(2):
                        for i in range(2 * KC):
                            w, c = i // KC, i % KC
                            act.wait_ge(g_mm, 2 * KC * n + i + 1)
                            nc.scalar.activation((k1_hi, q1_hi)[w][:, c, :], psum[2 + i % 2][:, :], ACT.Identity, bias=b1[:, w, c:c + 1]).then_inc(g_hi, 1)
                        act.wait_ge(g_nb, n + 1)
                        for b in range(4):
                            ex = nc.scalar.activation(l1p[:, b, :], psum[4][:, b * S:(b + 1) * S], ACT.Exp, scale=SC1,
                                                      bias=l1nb[:, b:b + 1], accum_out=l1sum[:, b:b + 1])
                        ex.then_inc(g_exp, 1)
                        act.wait_ge(g_turned, n + 1)
                        nc.scalar.activation(l1pT_hi[:, :], psum[5][:, :], ACT.Copy).then_inc(g_phi, 1)

                @block.vector
                def _(dve):
                    norm_vector(dve, 2, xn)
                    for n in range(2):
                        for i in range(2 * KC):
                            w, c = i // KC, i % KC
                            dve.wait_ge(g_hi, 2 * KC * n + i + 1)
                            nc.vector.scalar_tensor_tensor((k1_lo, q1_lo)[w][:, c, :], psum[2 + i % 2][:, :], b1[:, w, c:c + 1],
                                                           (k1_hi, q1_hi)[w][:, c, :].bitcast(F32), ALU.add, ALU.subtract).then_inc(g_lo, 1)
                        dve.wait_ge(g_smm, n + 1)
                        nc.vector.tensor_reduce(l1max[:, :], psum[4][:, :].rearrange("p (b k) -> p b k", b=4), AX.X, ALU.max).then_inc(g_max, 1)
                        dve.wait_ge(g_max, n + 1)
                        nc.vector.tensor_scalar(l1nb[:, :], l1max[:, :], -SC1, None, ALU.mult).then_inc(g_nb, 1)
                        dve.wait_ge(g_exp, n + 1)
                        nc.vector.reciprocal(l1inv[:, :], l1sum[:, :]).then_inc(g_inv, 1)
                        dve.wait_ge(g_phi, n + 1)
                        nc.vector.tensor_tensor(l1pT_lo[:, :], psum[5][:, :], l1pT_hi[:, :].bitcast(F32), ALU.subtract).then_inc(g_plo, 1)
                        for b in range(4):
                            dve.wait_ge(g_omm, 4 * n + b + 1)
                            nc.vector.scalar_tensor_tensor(x[:, 4 * n + b, :], psum[6 + b % 2][:, :], gates[:, 1:2], x[:, 4 * n + b, :],
                                                           ALU.mult, ALU.add).then_inc(g_added, 1)

                @block.tensor
                def _(pe):
                    norm_tensor(pe, 2, xn)
                    pe.wait_ge(ln_lo, 3 * NB)
                    for n in range(2):
                        half = slice(n * 512, (n + 1) * 512)
                        for i in range(2 * KC):
                            w, c = i // KC, i % KC
                            pe.wait_ge(g_wlo, w + 1)
                            if 2 * KC * n + i >= 2:
                                pe.wait_ge(g_lo, 2 * KC * n + i - 1)
                            r_hi, r_lo = ((cT_hi, cT_lo), (xT_hi, xT_lo))[w]
                            for k in range(KC):
                                cols = slice(c * P, (c + 1) * P)
                                mm = product(psum[2 + i % 2][:, :], w_hi[:, w, k, cols], w_lo[:, w, k, cols], r_hi[:, k, half], r_lo[:, k, half], k == 0, k == KC - 1)
                            mm.then_inc(g_mm, 1)
                        pe.wait_ge(g_lo, 2 * KC * (n + 1))
                        if n:
                            pe.wait_ge(g_exp, n)
                        for b in range(4):
                            q = slice(b * S, (b + 1) * S)
                            for c in range(KC):
                                mm = product(psum[4][:, q], q1_hi[:, c, q], q1_lo[:, c, q], k1_hi[:, c, q], k1_lo[:, c, q], c == 0, c == KC - 1)
                        mm.then_inc(g_smm, 1)
                        pe.wait_ge(g_norm, n + 1)
                        for b in range(4):
                            mm = nc.tensor.transpose(psum[5][:, b * S:(b + 1) * S], l1p[:, b, :], ident[:, :])
                        mm.then_inc(g_turned, 1)
                        pe.wait_ge(g_plo, n + 1)
                        pe.wait_ge(g_clo, n + 1)
                        for b in range(4):
                            if 4 * n + b >= 2:
                                pe.wait_ge(g_added, 4 * n + b - 1)
                            q = slice(b * S, (b + 1) * S)
                            product(psum[6 + b % 2][:, :], l1pT_hi[:, q], l1pT_lo[:, q], c_hi[:, 4 * n + b, :], c_lo[:, 4 * n + b, :], True, True).then_inc(g_omm, 1)

        with ExitStack() as ctx:
            xn = sb("xn3", [P, 2, E], ctx=ctx)
            gw = sb("gw", [P, KC, NX], ctx=ctx)
            gw_hi, gw_lo = (sb(f"gw_{n}", [P, KC, NX], F32R, ctx) for n in ("hi", "lo"))
            logits = sb("logits", [P, NB, NX], ctx=ctx)
            best = sb("best", [P, NB, 8], ctx=ctx)
            best_at = sb("best_at", [P, NB, 8], U32, ctx)
            bestf = sb("bestf", [P, NB, 2], ctx=ctx)
            numbers = sb("numbers", [P, NX], ctx=ctx)
            diff = sb("diff", [P, NB], ctx=ctx)
            ediff = sb("ediff", [P, NB], ctx=ctx)
            edp1 = sb("edp1", [P, NB], ctx=ctx)
            wts = sb("wts", [P, 2, NB], ctx=ctx)
            onehot = sb("onehot", [P, 2, NB, NX], ctx=ctx)
            comb = sb("comb", [P, NB, NX], ctx=ctx)
            combT = sb("combT", [NX, NB, P], ctx=ctx)
            eb = sb("eb", [NX, E], ctx=ctx)
            ew = sb("ew", [P, 2, KC, E], ctx=ctx)
            ew_hi, ew_lo = (sb(f"ew_{n}", [P, 2, KC, E], F32R, ctx) for n in ("hi", "lo"))
            (m_in, m_ew, m_gh, m_gl, m_log, m_logk, m_best, m_step, m_cT, m_cTk, m_bmm, m_badd, m_ehi, m_elo, m_mm, m_add, m_out) = (
                sem(f"m_{n}") for n in ("in", "ew", "gh", "gl", "log", "logk", "best", "step", "cT", "cTk", "bmm", "badd", "ehi", "elo", "mm", "add", "out"))
            m_ew1 = sem("m_ew1")
            m_exp = sem("m_exp")
            with nc.Block() as block:
                @block.sync
                def _(sp):
                    sp.dma_start(gw[:, :, :], a["gw"]).then_inc(m_in, 16)
                    sp.dma_start(numbers[:, :], a["numbers"].partition_broadcast(P)).then_inc(m_in, 16)
                    sp.dma_start(eb[:, :], a["eb"]).then_inc(m_in, 16)

                    def experts(i):
                        for k in range(2):
                            wait(sp, m_elo, i, 2, k - 1)
                            sp.dma_start(ew[:, k, :, :], a["ew"][bass.ds(2 * i + k, 1)].rearrange("o p c n -> p (o c) n")).then_inc((m_ew, m_ew1)[k], 16)

                    experts(0)
                    with sp.Fori(1, NX // 2) as i:
                        experts(i)
                    sp.wait_ge(m_add, NX * NB)
                    sp.dma_start(out, x[:, :, :]).then_inc(m_out, 16)
                    sp.wait_ge(m_out, 16)

                @block.gpsimd
                def _(pool):
                    pool.wait_ge(m_gh, 1)
                    nc.gpsimd.tensor_tensor(gw_lo[:, :, :], gw[:, :, :], gw_hi[:, :, :].bitcast(F32), ALU.subtract).then_inc(m_gl, 1)
                    def experts(i):
                        for k in range(2):
                            wait(pool, m_ehi, i, 2, k + 1)
                            nc.gpsimd.tensor_tensor(ew_lo[:, k, :, :], ew[:, k, :, :], ew_hi[:, k, :, :].bitcast(F32), ALU.subtract).then_inc(m_elo, 1)

                    experts(0)
                    with pool.Fori(1, NX // 2) as i:
                        experts(i)

                @block.scalar
                def _(act):
                    act.wait_ge(m_in, 48)
                    nc.scalar.activation(gw_hi[:, :, :], gw[:, :, :], ACT.Copy).then_inc(m_gh, 1)
                    norm_scalar(act, 3)
                    act.wait_ge(m_log, 1)
                    nc.scalar.activation(logits[:, :, :], psum[2][:, 0:NB * NX].rearrange("p (t e) -> p t e", t=NB), ACT.Copy).then_inc(m_logk, 1)
                    act.wait_ge(m_step, 1)
                    nc.scalar.activation(ediff[:, :], diff[:, :], ACT.Exp).then_inc(m_exp, 1)
                    def experts(i):
                        for k in range(2):
                            wait(act, (m_ew, m_ew1)[k], i, 16, 16)
                            wait(act, m_mm, i, 2 * NB, (k - 1) * NB)
                            nc.scalar.activation(ew_hi[:, k, :, :], ew[:, k, :, :], ACT.Copy).then_inc(m_ehi, 1)

                    experts(0)
                    with act.Fori(1, NX // 2) as i:
                        experts(i)

                @block.vector
                def _(dve):
                    norm_vector(dve, 3, xn)
                    dve.wait_ge(m_logk, 1)
                    for t in range(NB):
                        nc.vector.max(best[:, t, :], logits[:, t, :]).then_inc(m_best, 1)
                    for t in range(NB):
                        dve.wait_ge(m_best, t + 1)
                        nc.vector.max_index(best_at[:, t, :], best[:, t, :], logits[:, t, :]).then_inc(m_best, 1)
                    steps = [0]

                    def step(op):
                        steps[0] += 1
                        op.then_inc(m_step, 1)
                        dve.wait_ge(m_step, steps[0])

                    dve.wait_ge(m_best, 2 * NB)
                    step(nc.vector.tensor_tensor(diff[:, :], best[:, :, 1], best[:, :, 0], ALU.subtract))
                    step(nc.vector.tensor_copy(bestf[:, :, :], best_at[:, :, 0:2]))
                    dve.wait_ge(m_exp, 1)
                    step(nc.vector.tensor_scalar_add(edp1[:, :], ediff[:, :], 1.0))
                    step(nc.vector.reciprocal(wts[:, 0, :], edp1[:, :]))
                    step(nc.vector.tensor_tensor(wts[:, 1, :], wts[:, 0, :], ediff[:, :], ALU.mult))
                    step(nc.vector.tensor_scalar(wts[:, :, :], wts[:, :, :], gates[:, 3:4], None, ALU.mult))
                    for k in range(2):
                        step(nc.vector.tensor_tensor(onehot[:, k, :, :], numbers[:, :].unsqueeze(1).broadcast_to([P, NB, NX]),
                                                     bestf[:, :, k].unsqueeze(2).broadcast_to([P, NB, NX]), ALU.is_equal))
                        step(nc.vector.tensor_tensor(onehot[:, k, :, :], onehot[:, k, :, :], wts[:, k, :].unsqueeze(2).broadcast_to([P, NB, NX]), ALU.mult))
                    step(nc.vector.tensor_tensor(comb[:, :, :], onehot[:, 0, :, :], onehot[:, 1, :, :], ALU.add))
                    for t in range(NB):
                        dve.wait_ge(m_cT, t + 1)
                        nc.vector.tensor_copy(combT[:, t, :], psum[3][0:NX, (t % 4) * P:(t % 4 + 1) * P]).then_inc(m_cTk, 1)
                    for t in range(NB):
                        dve.wait_ge(m_bmm, t + 1)
                        nc.vector.tensor_tensor(x[:, t, :], psum[4 + t % 2][:, :], x[:, t, :], ALU.add).then_inc(m_badd, 1)
                    def experts(e):
                        for t in range(NB):
                            wait(dve, m_mm, e, NB, t + 1)
                            nc.vector.scalar_tensor_tensor(x[:, t, :], psum[6 + t % 2][:, :], comb[:, t, bass.ds(e, 1)], x[:, t, :],
                                                           ALU.mult, ALU.add).then_inc(m_add, 1)

                    experts(0)
                    with dve.Fori(1, NX) as e:
                        experts(e)

                @block.tensor
                def _(pe):
                    norm_tensor(pe, 3, xn)
                    pe.wait_ge(ln_lo, 4 * NB)
                    pe.wait_ge(m_gl, 1)
                    for t in range(NB):
                        tok = slice(t * P, (t + 1) * P)
                        for c in range(KC):
                            mm = product(psum[2][:, t * NX:(t + 1) * NX], xT_hi[:, c, tok], xT_lo[:, c, tok], gw_hi[:, c, :], gw_lo[:, c, :], c == 0, c == KC - 1)
                    mm.then_inc(m_log, 1)
                    pe.wait_ge(m_step, 11)
                    for t in range(NB):
                        if t >= 1:
                            pe.wait_ge(m_cTk, t)
                        nc.tensor.transpose(psum[3][0:NX, (t % 4) * P:(t % 4 + 1) * P], comb[:, t, :], ident[:, :]).then_inc(m_cT, 1)
                    for t in range(NB):
                        pe.wait_ge(m_cTk, t + 1)
                        if t >= 2:
                            pe.wait_ge(m_badd, t - 1)
                        nc.tensor.matmul(psum[4 + t % 2][:, :], combT[:, t, :], eb[:, :], start=True, stop=True).then_inc(m_bmm, 1)
                    def experts(i):
                        for k in range(2):
                            wait(pe, m_elo, i, 2, k + 1)
                            for t in range(NB):
                                wait(pe, m_add, i, 2 * NB, k * NB + t - 1)
                                tok = slice(t * P, (t + 1) * P)
                                for c in range(KC):
                                    mm = product(psum[6 + t % 2][:, :], xT_hi[:, c, tok], xT_lo[:, c, tok], ew_hi[:, k, c, :], ew_lo[:, k, c, :], c == 0, c == KC - 1)
                                mm.then_inc(m_mm, 1)

                    experts(0)
                    with pe.Fori(1, NX // 2) as i:
                        experts(i)


def kernel(x, ctx_4096, pos_BxS2, mask_BxSxS2_ik0, g_xattn, g_ffn, L0_xattn_Wq, L0_xattn_Wk, L0_xattn_Wv,
           L0_xattn_Wo, L0_ffn_W_q, L0_ffn_scales, L0_ffn_zeros, L0_ffn_mask, L0_ffn_scale2, L0_ffn_bias,
           L1_xattn_Wq, L1_xattn_bq, L1_xattn_Wk, L1_xattn_bk, L1_ffn_gate_w, L1_ffn_expert_w, L1_ffn_expert_b):
    import numpy as np
    import concourse.bacc as bacc
    from concourse.bass_utils import run_bass_kernel_spmd

    def chunked(w):
        w = np.asarray(w)
        return w.reshape(-1, P, w.shape[1]).transpose(1, 0, 2)

    inv = (1.0 / np.float32(10000.0) ** (np.arange(0, D, 2, dtype=np.float32) / np.float32(D))).astype(np.float32)
    angle = np.arange(MAX_POS, dtype=np.float32)[:, None] * inv[None, :]
    cos, sin = np.cos(angle), np.sin(angle)
    wq = np.asarray(L0_xattn_Wq).reshape(KC, P, KVH, GR * D)
    wo = np.asarray(L0_xattn_Wo).reshape(KVH, GR, D, E)
    layout = {
        "x": np.asarray(x).transpose(1, 0, 2),
        "ctxT": np.asarray(ctx_4096).reshape(T, KC, P).transpose(2, 1, 0),
        "ctx": np.asarray(ctx_4096).transpose(1, 0, 2),
        "pos": np.asarray(pos_BxS2).T,
        "mask": np.asarray(mask_BxSxS2_ik0).transpose(1, 0, 2),
        "gates": np.concatenate([np.asarray(g_xattn), np.asarray(g_ffn)]),
        "wq": wq.transpose(2, 1, 0, 3).reshape(KVH, P, KC * GR * D),
        "wo": wo.transpose(0, 2, 1, 3).reshape(KVH, P, GR * E),
        "wk": np.asarray(L0_xattn_Wk).reshape(KC, P, KVH, D).transpose(2, 1, 0, 3),
        "wv": np.asarray(L0_xattn_Wv).reshape(KC, P, KVH, D).transpose(2, 1, 0, 3),
        "wint": chunked(L0_ffn_W_q),
        "wmask": chunked(L0_ffn_mask),
        "scales": chunked(L0_ffn_scales),
        "zeros": chunked(L0_ffn_zeros),
        "scale2": np.asarray(L0_ffn_scale2).reshape(KC, P).T,
        "fbias": np.asarray(L0_ffn_bias),
        "wq1": chunked(np.asarray(L1_xattn_Wq).T),
        "wk1": chunked(np.asarray(L1_xattn_Wk).T),
        "b1": np.stack([np.asarray(L1_xattn_bk).reshape(KC, P).T, np.asarray(L1_xattn_bq).reshape(KC, P).T], axis=1),
        "gw": chunked(np.asarray(L1_ffn_gate_w).T),
        "ew": np.asarray(L1_ffn_expert_w).transpose(0, 2, 1).reshape(NX, KC, P, E).transpose(0, 2, 1, 3),
        "eb": np.asarray(L1_ffn_expert_b),
        "ident": np.eye(P, dtype=np.float32),
        "numbers": np.arange(NX, dtype=np.float32),
        "rotary": np.concatenate([cos, cos, sin, -sin], axis=1).astype(np.float32),
    }
    nc = bacc.Bacc("TRN2", target_bir_lowering=False, num_devices=1, dynamic_dma_scratch_size=4096)
    arrays = {f"in_{k}": np.ascontiguousarray(v) for k, v in layout.items()}
    aps = {k: nc.dram_tensor(f"in_{k}", arrays[f"in_{k}"].shape, mybir.dt.from_np(arrays[f"in_{k}"].dtype),
                             kind="ExternalInput").ap() for k in layout}
    out = nc.dram_tensor("out", [P, NB, E], F32, kind="ExternalOutput").ap()
    program(nc, aps, out)
    r = run_bass_kernel_spmd(nc, [arrays], core_ids=[0])
    return np.asarray(r.results[0]["out"]).transpose(1, 0, 2).reshape(NB, S, E)
```

```python
import concourse.bass as bass
from concourse import mybir
from contextlib import ExitStack

F32 = mybir.dt.float32
F32R = mybir.dt.float32r
I32 = mybir.dt.int32
U32 = mybir.dt.uint32
I8 = mybir.dt.int8
ALU = mybir.AluOpType
ACT = mybir.ActivationFunctionType
AX = mybir.AxisListType

P = 128
NB = 8
S = 128
T = NB * S
E = 512
KC = E // P
H, KVH, D = 32, 8, 128
GR = H // KVH
MAX_POS = 512
NX = 32
TOP = 2
GROUP = 64
NG = E // GROUP
EPS = 1e-5
MASKED = -1e9


def wait(engine, semaphore, g, per, count):
    assert per + count > 0
    value = g * per + count
    if not (isinstance(g, int) and value <= 0):
        engine.wait_ge(semaphore, value)


def program(nc, a, out):
    root = ExitStack()
    with root:
        def sb(name, shape, dt=F32, ctx=root):
            return ctx.enter_context(nc.sbuf_tensor(name, shape, dt))

        def sem(name):
            return root.enter_context(nc.semaphore(name))

        x = sb("x", [P, NB, E])
        xT_hi = sb("xT_hi", [P, KC, T], F32R)
        xT_lo = sb("xT_lo", [P, KC, T], F32R)
        cT_hi = sb("cT_hi", [P, KC, T], F32R)
        cT_lo = sb("cT_lo", [P, KC, T], F32R)
        ident = sb("ident", [P, P])
        gates = sb("gates", [P, 4])
        stats = sb("stats", [P, NB, 6])
        meanvar = sb("meanvar", [P, NB, 2])
        spread = sb("spread", [P, NB])
        rstd = sb("rstd", [P, NB])
        psum = [root.enter_context(nc.psum_tensor(f"bank{i}", [P, 512], F32)) for i in range(8)]

        ln_stats, ln_aggr, ln_var, ln_std, ln_rstd = (sem(f"ln_{n}") for n in ("stats", "aggr", "var", "std", "rstd"))
        ln_norm, ln_turned, ln_hi, ln_lo = (sem(f"ln_{n}") for n in ("norm", "turned", "hi", "lo"))

        def norm_vector(dve, n, xn, whole=False):
            for t in range(NB):
                nc.vector.bn_stats(stats[:, t, :], x[:, t, :]).then_inc(ln_stats, 1)
            for t in range(NB):
                dve.wait_ge(ln_stats, n * NB + t + 1)
                nc.vector.bn_aggr(meanvar[:, t, :], stats[:, t, :]).then_inc(ln_aggr, 1)
            dve.wait_ge(ln_aggr, (n + 1) * NB)
            nc.vector.tensor_scalar_add(spread[:, :], meanvar[:, :, 1], EPS).then_inc(ln_var, 1)
            dve.wait_ge(ln_std, n + 1)
            nc.vector.reciprocal(rstd[:, :], spread[:, :]).then_inc(ln_rstd, 1)
            dve.wait_ge(ln_rstd, n + 1)

            def rest(t):
                dve.wait_ge(ln_hi, n * NB + t + 1)
                tok = slice(t * P, (t + 1) * P)
                nc.vector.tensor_tensor(xT_lo[:, :, tok], psum[t % 2][:, :].rearrange("p (c t) -> p c t", c=KC),
                                        xT_hi[:, :, tok].bitcast(F32), ALU.subtract).then_inc(ln_lo, 1)

            for t in range(NB):
                if t >= 2 and not whole:
                    dve.wait_ge(ln_turned, n * NB + t - 1)
                nc.vector.tensor_scalar(xn[:, t if whole else t % 2, :], x[:, t, :], meanvar[:, t, 0:1], rstd[:, t:t + 1],
                                        ALU.subtract, ALU.mult).then_inc(ln_norm, 1)
                if t >= 1:
                    rest(t - 1)
            rest(NB - 1)

        def norm_scalar(act, n):
            act.wait_ge(ln_var, n + 1)
            nc.scalar.activation(spread[:, :], spread[:, :], ACT.Sqrt).then_inc(ln_std, 1)
            for t in range(NB):
                act.wait_ge(ln_turned, n * NB + t + 1)
                nc.scalar.activation(xT_hi[:, :, t * P:(t + 1) * P],
                                     psum[t % 2][:, :].rearrange("p (c t) -> p c t", c=KC), ACT.Copy).then_inc(ln_hi, 1)

        def norm_tensor(pe, n, xn, whole=False):
            for t in range(NB):
                pe.wait_ge(ln_norm, n * NB + t + 1)
                if t >= 2:
                    pe.wait_ge(ln_lo, n * NB + t - 1)
                for c in range(KC):
                    mm = nc.tensor.transpose(psum[t % 2][:, c * P:(c + 1) * P], xn[:, t if whole else t % 2, c * P:(c + 1) * P], ident[:, :])
                mm.then_inc(ln_turned, 1)

        def product(out_, hi, lo, r_hi, r_lo, start, stop):
            nc.tensor.matmul(out_, hi, r_hi, start=start, stop=False)
            nc.tensor.matmul(out_, hi, r_lo, start=False, stop=False)
            return nc.tensor.matmul(out_, lo, r_hi, start=False, stop=stop)

        phaseA = ExitStack()
        cosT = sb("cosT", [P, T], ctx=phaseA)
        sinT = sb("sinT", [P, T], ctx=phaseA)
        open_key = sb("open_key", [P, NB, S], I8, phaseA)
        key_scale = sb("key_scale", [P, 1], ctx=phaseA)
        filled = sb("filled", [P, NB, GR, S], ctx=phaseA)

        with ExitStack() as ctx:
            xn = sb("xn0", [P, 2, E], ctx=ctx)
            ctx_raw = sb("ctx_raw", [P, KC, T], ctx=ctx)
            mask_raw = sb("mask_raw", [P, NB, S], I32, ctx)
            pos_raw = sb("pos_raw", [P, NB], I32, ctx)
            pos_neg = sb("pos_neg", [P, NB], ctx=ctx)
            pos_wrapped = sb("pos_wrapped", [P, NB], ctx=ctx)
            pos_row = sb("pos_row", [P, NB], U32, ctx)
            rotary = sb("rotary", [P, NB, 2 * D], ctx=ctx)
            gates_raw = sb("gates_raw", [P, 4], ctx=ctx)
            in_x, in_small, in_pos, in_mask, in_ctx = (sem(f"in_{n}") for n in ("x", "small", "pos", "mask", "ctx"))
            in_rot = sem("in_rot")
            pos_step, rot_turned, rot_kept, ctx_hi, mask_done, gate_done, fill_done, ctx_lo = (
                sem(n) for n in ("pos_step", "rot_turned", "rot_kept", "ctx_hi", "mask_done", "gate_done", "fill_done", "ctx_lo"))
            with nc.Block() as block:
                @block.sync
                def _(sp):
                    sp.dma_start(x[:, :, :], a["x"]).then_inc(in_x, 16)
                    sp.dma_start(ident[:, :], a["ident"]).then_inc(in_small, 16)
                    sp.dma_start(gates_raw[:, :], a["gates"].partition_broadcast(P)).then_inc(in_small, 16)
                    sp.dma_start(ctx_raw[:, :, :], a["ctxT"]).then_inc(in_ctx, 16)
                    sp.dma_start(mask_raw[:, :, :], a["mask"]).then_inc(in_mask, 16)

                @block.gpsimd
                def _(pool):
                    pool.dma_start(pos_raw[:, :], a["pos"]).then_inc(in_pos, 16)
                    nc.gpsimd.memset(filled[:, :, :, :], MASKED).then_inc(fill_done, 1)
                    nc.gpsimd.memset(key_scale[:, :], float(D) ** -0.5).then_inc(fill_done, 1)
                    pool.wait_ge(pos_step, 3)
                    for t in range(NB):
                        pool.indirect_dma_start(
                            out=rotary[:, t, :], out_offset=None, in_=a["rotary"],
                            in_offset=bass.IndirectOffsetOnAxis(ap=pos_row[:, t:t + 1], axis=0)).then_inc(in_rot, 16)
                    for c in range(KC):
                        pool.wait_ge(ctx_hi, c + 1)
                        nc.gpsimd.tensor_tensor(cT_lo[:, c, :], ctx_raw[:, c, :], cT_hi[:, c, :].bitcast(F32),
                                                ALU.subtract).then_inc(ctx_lo, 1)

                @block.scalar
                def _(act):
                    act.wait_ge(in_small, 32)
                    nc.scalar.activation(gates[:, :], gates_raw[:, :], ACT.Tanh).then_inc(gate_done, 1)
                    norm_scalar(act, 0)
                    act.wait_ge(in_ctx, 16)
                    for c in range(KC):
                        nc.scalar.activation(cT_hi[:, c, :], ctx_raw[:, c, :], ACT.Copy).then_inc(ctx_hi, 1)

                @block.vector
                def _(dve):
                    dve.wait_ge(in_pos, 16)
                    nc.vector.tensor_scalar(pos_neg[:, :], pos_raw[:, :], 0.0, float(MAX_POS), ALU.is_lt, ALU.mult).then_inc(pos_step, 1)
                    dve.wait_ge(pos_step, 1)
                    nc.vector.tensor_tensor(pos_wrapped[:, :], pos_raw[:, :], pos_neg[:, :], ALU.add).then_inc(pos_step, 1)
                    dve.wait_ge(pos_step, 2)
                    nc.vector.tensor_scalar(pos_row[:, :], pos_wrapped[:, :], 0.0, float(MAX_POS - 1), ALU.max, ALU.min).then_inc(pos_step, 1)
                    dve.wait_ge(in_x, 16)
                    norm_vector(dve, 0, xn)
                    dve.wait_ge(in_mask, 16)
                    nc.vector.tensor_scalar(open_key[:, :, :], mask_raw[:, :, :], 0.0, None, ALU.not_equal).then_inc(mask_done, 1)
                    for t in range(NB):
                        dve.wait_ge(rot_turned, t + 1)
                        tok = slice(t * P, (t + 1) * P)
                        nc.vector.tensor_copy(cosT[:, tok], psum[2 + t % 2][:, 0:P]).then_inc(rot_kept, 1)
                        nc.vector.tensor_copy(sinT[:, tok], psum[2 + t % 2][:, P:2 * P]).then_inc(rot_kept, 1)

                @block.tensor
                def _(pe):
                    pe.wait_ge(in_small, 32)
                    norm_tensor(pe, 0, xn)
                    pe.wait_ge(in_rot, 16 * NB)
                    for t in range(NB):
                        if t >= 2:
                            pe.wait_ge(rot_kept, 2 * (t - 1))
                        nc.tensor.transpose(psum[2 + t % 2][:, 0:P], rotary[:, t, 0:D], ident[:, :])
                        nc.tensor.transpose(psum[2 + t % 2][:, P:2 * P], rotary[:, t, D:2 * D], ident[:, :]).then_inc(rot_turned, 1)

        with phaseA as ctx:
            HALF = T // 2
            PAIR = 2 * S
            raw_big = sb("raw_big", [P, 4 * 512], ctx=ctx)
            raw_k = sb("raw_k", [P, KC, D], ctx=ctx)
            raw_v = sb("raw_v", [P, KC, D], ctx=ctx)
            wq_hi, wq_lo = (sb(f"wq_{n}", [P, KC, GR * D], F32R, ctx) for n in ("hi", "lo"))
            wo_hi, wo_lo = (sb(f"wo_{n}", [P, GR, E], F32R, ctx) for n in ("hi", "lo"))
            wk_hi, wk_lo = (sb(f"wk_{n}", [P, KC, D], F32R, ctx) for n in ("hi", "lo"))
            wv_hi, wv_lo = (sb(f"wv_{n}", [P, KC, D], F32R, ctx) for n in ("hi", "lo"))
            kT = sb("kT", [P, T], ctx=ctx)
            vT = sb("vT", [P, T], ctx=ctx)
            v_hi, v_lo = (sb(f"v_{n}", [P, NB, D], F32R, ctx) for n in ("hi", "lo"))
            qT = sb("qT", [P, 2, GR, PAIR], ctx=ctx)
            straight = sb("straight", [P, 2, 512], ctx=ctx)
            turned = sb("turned", [P, 2, 512], ctx=ctx)
            probs = sb("probs", [P, 2, GR, S], ctx=ctx)
            pT_hi, pT_lo = (sb(f"pT_{n}", [P, 2, GR * S], F32R, ctx) for n in ("hi", "lo"))
            oT_hi, oT_lo = (sb(f"oT_{n}", [P, 2, GR, S], F32R, ctx) for n in ("hi", "lo"))
            negmax = sb("negmax", [P, NB, GR], ctx=ctx)
            gatepost = sb("gatepost", [P, 1], ctx=ctx)
            total = sb("total", [P, NB, GR], ctx=ctx)
            invtotal = sb("invtotal", [P, NB, GR], ctx=ctx)

            bank_rope = psum[0:2]
            bank_scores = psum[2:4]
            bank_pT, bank_o, bank_y, bank_v = psum[4:8]

            big_in, kv_in = sem("big_in"), sem("kv_in")
            wq_hi_s, wq_lo_s, wo_hi_s, wo_lo_s, wkv_hi_s, wkv_lo_s = (
                sem(n) for n in ("wq_hi_done", "wq_lo_done", "wo_hi_done", "wo_lo_done", "wkv_hi_done", "wkv_lo_done"))
            proj_mm, rope_mul, rope_add, rope_sum = (sem(n) for n in ("proj_mm", "rope_mul", "rope_add", "rope_sum"))
            v_mm, v_kept, v_turned, v_hi_s, v_lo_s = (sem(n) for n in ("v_mm", "v_kept", "v_turned", "v_hi_done", "v_lo_done"))
            score_mm, score_kept, score_max, exp_done, inv_done, probs_done = (
                sem(n) for n in ("score_mm", "score_kept", "score_max", "exp_done", "inv_done", "probs_done"))
            pT_mm, pT_hi_s, pT_lo_s = sem("pT_mm"), sem("pT_hi_done"), sem("pT_lo_done")
            o_mm, o_hi_s, o_lo_s = sem("o_mm"), sem("o_hi_done"), sem("o_lo_done")
            y_mm, y_added = sem("y_mm"), sem("y_added")

            ITEMS, UNITS = 10, NB
            ITEMS_OF_STEP = [[5], [6], [7], [8], [9], [10], [11], [12, 13, 14]]
            FIRST_ITEMS = [0, 1, 2, 3, 4]

            def steps(g):
                whole = not isinstance(g, int)
                for step in range(3 if not whole and g == KVH else UNITS):
                    def unit(u):
                        if not whole and (g * UNITS + u < 0 or g * UNITS + u >= KVH * UNITS):
                            return None
                        return u
                    items = [] if not whole and g == KVH else ITEMS_OF_STEP[step]
                    if not whole and g == KVH - 1:
                        items = [i for i in items if i < ITEMS]
                    yield step, unit(step), items, unit(step - 1), unit(step - 2), unit(step - 3)

            def more(g):
                return not isinstance(g, int) or g < KVH - 1

            def place_of(item):
                i = item % ITEMS
                if i in (2, 3):
                    tok = slice((i - 2) * HALF, (i - 1) * HALF)
                    return kT[:, tok], tok, True
                pair, j = (0, i) if i < 2 else ((i - 2) // 2, i % 2)
                return qT[:, pair % 2, 2 * j:2 * j + 2, :], slice(pair * PAIR, (pair + 1) * PAIR), False

            def shaped(ap, key):
                return ap if key else ap.rearrange("p (h t) -> p h t", h=2)

            def spread_over(table, key):
                return table if key else table.unsqueeze(1).broadcast_to([table.shape[0], 2, PAIR])

            with nc.Block() as block:
                @block.sync
                def _(sp):
                    def load(g, first):
                        if not first:
                            sp.wait_ge(wkv_lo_s, 2 * g)
                        sp.dma_start(raw_k[:, :, :], a["wk"][bass.ds(g, 1)].rearrange("o p c n -> p (o c) n")).then_inc(kv_in, 16)
                        sp.dma_start(raw_v[:, :, :], a["wv"][bass.ds(g, 1)].rearrange("o p c n -> p (o c) n")).then_inc(kv_in, 16)
                        if not first:
                            sp.wait_ge(wo_lo_s, GR * g)
                        sp.dma_start(raw_big[:, :], a["wq"][bass.ds(g, 1)].rearrange("o p n -> p (o n)")).then_inc(big_in, 16)
                        sp.wait_ge(wq_lo_s, 2 * g + 2)
                        sp.dma_start(raw_big[:, :], a["wo"][bass.ds(g, 1)].rearrange("o p n -> p (o n)")).then_inc(big_in, 16)

                    load(0, True)
                    with sp.Fori(1, KVH) as g:
                        load(g, False)

                @block.gpsimd
                def _(pool):
                    def queries_weights(g, half):
                        cols = slice(half * 2 * D, (half + 1) * 2 * D)
                        wait(pool, wq_hi_s, g, 2, half + 1)
                        nc.gpsimd.tensor_tensor(wq_lo[:, :, cols], raw_big[:, :].rearrange("p (c n) -> p c n", c=KC)[:, :, cols],
                                                wq_hi[:, :, cols].bitcast(F32), ALU.subtract).then_inc(wq_lo_s, 1)

                    def keys_values_weights(g):
                        wait(pool, wkv_hi_s, g, 2, 2)
                        nc.gpsimd.tensor_tensor(wk_lo[:, :, :], raw_k[:, :, :], wk_hi[:, :, :].bitcast(F32), ALU.subtract).then_inc(wkv_lo_s, 1)
                        nc.gpsimd.tensor_tensor(wv_lo[:, :, :], raw_v[:, :, :], wv_hi[:, :, :].bitcast(F32), ALU.subtract).then_inc(wkv_lo_s, 1)

                    def out_weights(g):
                        for h in range(GR):
                            wait(pool, wo_hi_s, g, GR, h + 1)
                            nc.gpsimd.tensor_tensor(wo_lo[:, h, :], raw_big[:, h * E:(h + 1) * E],
                                                    wo_hi[:, h, :].bitcast(F32), ALU.subtract).then_inc(wo_lo_s, 1)

                    def item_sum(g, item):
                        k = item % 2
                        dst, _, key = place_of(item)
                        wait(pool, rope_mul, g, ITEMS, item + 1)
                        if key:
                            nc.gpsimd.tensor_tensor(straight[:, k, :], straight[:, k, :], turned[:, k, :], ALU.add).then_inc(rope_add, 1)
                            wait(pool, rope_add, g, 2, item % ITEMS - 1 + (2 if item >= ITEMS else 0))
                            nc.gpsimd.tensor_tensor(dst, straight[:, k, :], key_scale[:, :].broadcast_to([P, 512]), ALU.mult).then_inc(rope_sum, 1)
                        else:
                            nc.gpsimd.tensor_tensor(dst, shaped(straight[:, k, :], key), shaped(turned[:, k, :], key), ALU.add).then_inc(rope_sum, 1)

                    def normalise(g, u):
                        wait(pool, inv_done, g, UNITS, u + 1)
                        nc.gpsimd.tensor_tensor(probs[:, u % 2, :, :], probs[:, u % 2, :, :],
                                                invtotal[:, u % UNITS, :].unsqueeze(2).broadcast_to([P, GR, S]), ALU.mult).then_inc(probs_done, 1)

                    def group(g):
                        for step, u, items, _, _, _ in steps(g):
                            if step == 4 and more(g):
                                queries_weights(g + 1, 0)
                            if step == 5 and more(g):
                                queries_weights(g + 1, 1)
                            if u is not None and not items:
                                normalise(g, u)
                            for item in items:
                                item_sum(g, item)
                                if item == items[0]:
                                    normalise(g, u)
                            if step == 2 and u is not None:
                                out_weights(g)
                            if step == 3 and more(g):
                                keys_values_weights(g + 1)

                    queries_weights(0, 0)
                    queries_weights(0, 1)
                    keys_values_weights(0)
                    for item in FIRST_ITEMS:
                        item_sum(0, item)
                    group(0)
                    with pool.Fori(1, KVH - 1) as g:
                        group(g)
                    group(KVH - 1)
                    group(KVH)

                @block.scalar
                def _(act):
                    def queries_weights(g, half):
                        cols = slice(half * 2 * D, (half + 1) * 2 * D)
                        if half == 0:
                            wait(act, big_in, g, 32, 16)
                        nc.scalar.activation(wq_hi[:, :, cols], raw_big[:, :].rearrange("p (c n) -> p c n", c=KC)[:, :, cols], ACT.Copy).then_inc(wq_hi_s, 1)

                    def keys_values_weights(g):
                        wait(act, kv_in, g, 32, 32)
                        nc.scalar.activation(wk_hi[:, :, :], raw_k[:, :, :], ACT.Copy).then_inc(wkv_hi_s, 1)
                        nc.scalar.activation(wv_hi[:, :, :], raw_v[:, :, :], ACT.Copy).then_inc(wkv_hi_s, 1)

                    def out_weights(g):
                        wait(act, big_in, g, 32, 32)
                        wait(act, y_mm, g, UNITS, 0)
                        for h in range(GR):
                            nc.scalar.activation(wo_hi[:, h, :], raw_big[:, h * E:(h + 1) * E], ACT.Copy).then_inc(wo_hi_s, 1)

                    def exps(g, u):
                        wait(act, score_max, g, UNITS, u + 1)
                        wait(act, pT_mm, g, UNITS, u - 1)
                        for h in range(GR):
                            ex = nc.scalar.activation(probs[:, u % 2, h, :], filled[:, u % UNITS, h, :], ACT.Exp,
                                                      bias=negmax[:, u % UNITS, h:h + 1], accum_out=total[:, u % UNITS, h:h + 1])
                        ex.then_inc(exp_done, 1)

                    def probs_upper(g, u):
                        wait(act, pT_mm, g, UNITS, u + 1)
                        wait(act, o_mm, g, UNITS, u - 1)
                        nc.scalar.activation(pT_hi[:, u % 2, :], bank_pT[:, :], ACT.Copy).then_inc(pT_hi_s, 1)

                    def out_upper(g, u):
                        wait(act, o_mm, g, UNITS, u + 1)
                        wait(act, y_mm, g, UNITS, u - 1)
                        nc.scalar.activation(oT_hi[:, u % 2, :, :], bank_o[:, :].rearrange("p (h t) -> p h t", h=GR), ACT.Copy).then_inc(o_hi_s, 1)

                    def keep_values(g, half):
                        wait(act, v_mm, g, 2, half + 1)
                        nc.scalar.activation(vT[:, half * HALF:(half + 1) * HALF], bank_v[:, :], ACT.Copy).then_inc(v_kept, 1)

                    def values_upper(g):
                        for half in range(2):
                            wait(act, v_turned, g, 2, half + 1)
                            nc.scalar.activation(v_hi[:, 4 * half:4 * half + 4, :], bank_v[:, :].rearrange("p (b d) -> p b d", b=4),
                                                 ACT.Copy).then_inc(v_hi_s, 1)

                    def group(g):
                        for step, u, items, turn, attend, _ in steps(g):
                            if step == 4 and more(g):
                                wait(act, proj_mm, g, ITEMS, 9)
                                queries_weights(g + 1, 0)
                            if step == 5 and more(g):
                                wait(act, proj_mm, g, ITEMS, 10)
                                queries_weights(g + 1, 1)
                            if u is not None:
                                exps(g, u)
                            if step < 2 and u is not None:
                                keep_values(g, step)
                            if attend is not None:
                                out_upper(g, attend)
                            if step == 1 and u is not None:
                                values_upper(g)
                            if turn is not None:
                                probs_upper(g, turn)
                            if step == 2 and u is not None:
                                out_weights(g)
                            if step == 3 and more(g):
                                wait(act, v_mm, g, 2, 2)
                                keys_values_weights(g + 1)

                    queries_weights(0, 0)
                    queries_weights(0, 1)
                    keys_values_weights(0)
                    group(0)
                    with act.Fori(1, KVH - 1) as g:
                        group(g)
                    group(KVH - 1)
                    group(KVH)

                @block.vector
                def _(dve):
                    def item_products(g, item):
                        _, tok, key = place_of(item)
                        k = item % 2
                        wait(dve, proj_mm, g, ITEMS, item + 1)
                        wait(dve, rope_sum, g, ITEMS, item - 1)
                        bank = bank_rope[k]
                        nc.vector.tensor_tensor(shaped(straight[:, k, :], key), shaped(bank[:, :], key),
                                                spread_over(cosT[:, tok], key), ALU.mult)
                        for src, dst in ((slice(0, 64), slice(64, 128)), (slice(64, 128), slice(0, 64))):
                            last = nc.vector.tensor_tensor(shaped(turned[dst, k, :], key), shaped(bank[src, :], key),
                                                           spread_over(sinT[src, tok], key), ALU.mult)
                        last.then_inc(rope_mul, 1)

                    def keep_scores(g, u):
                        wait(dve, exp_done, g, UNITS, u - UNITS + 1)
                        wait(dve, score_mm, g, UNITS, u + 1)
                        nc.vector.memset(gatepost[:, :], 0.0)
                        for h in range(GR):
                            kept = nc.vector.copy_predicated(filled[:, u, h, :], open_key[:, u, :], bank_scores[u % 2][:, h * S:(h + 1) * S])
                        kept.then_inc(score_kept, 1)
                        wait(dve, score_kept, g, UNITS, u + 1)
                        nc.vector.tensor_reduce(negmax[:, u, :], filled[:, u, :, :], AX.X, ALU.max, negate=True).then_inc(score_max, 1)

                    def invert(g, u):
                        wait(dve, exp_done, g, UNITS, u + 1)
                        nc.vector.reciprocal(invtotal[:, u, :], total[:, u, :]).then_inc(inv_done, 1)

                    def probs_rest(g, u):
                        wait(dve, pT_hi_s, g, UNITS, u + 1)
                        nc.vector.tensor_tensor(pT_lo[:, u % 2, :], bank_pT[:, :], pT_hi[:, u % 2, :].bitcast(F32), ALU.subtract).then_inc(pT_lo_s, 1)

                    def out_rest(g, u):
                        wait(dve, o_hi_s, g, UNITS, u + 1)
                        nc.vector.tensor_tensor(oT_lo[:, u % 2, :, :], bank_o[:, :].rearrange("p (h t) -> p h t", h=GR),
                                                oT_hi[:, u % 2, :, :].bitcast(F32), ALU.subtract).then_inc(o_lo_s, 1)

                    def add_out(g, u):
                        wait(dve, y_mm, g, UNITS, u + 1)
                        nc.vector.scalar_tensor_tensor(x[:, u % UNITS, :], bank_y[:, :], gates[:, 0:1], x[:, u % UNITS, :], ALU.mult, ALU.add).then_inc(y_added, 1)

                    def values_rest(g):
                        for half in range(2):
                            wait(dve, v_hi_s, g, 2, half + 1)
                            rows = slice(4 * half, 4 * half + 4)
                            nc.vector.tensor_tensor(v_lo[:, rows, :], bank_v[:, :].rearrange("p (b d) -> p b d", b=4),
                                                    v_hi[:, rows, :].bitcast(F32), ALU.subtract).then_inc(v_lo_s, 1)

                    def group(g):
                        for step, u, items, turn, attend, out_unit in steps(g):
                            if u is not None:
                                keep_scores(g, u)
                            for item in items[:1]:
                                item_products(g, item)
                            if u is not None:
                                invert(g, u)
                            for item in items[1:]:
                                item_products(g, item)
                            if attend is not None:
                                out_rest(g, attend)
                            if step == 1 and u is not None:
                                values_rest(g)
                            if out_unit is not None:
                                add_out(g, out_unit)
                            if turn is not None:
                                probs_rest(g, turn)

                    for item in FIRST_ITEMS:
                        item_products(0, item)
                    group(0)
                    with dve.Fori(1, KVH - 1) as g:
                        group(g)
                    group(KVH - 1)
                    group(KVH)

                @block.tensor
                def _(pe):
                    def project(g, item):
                        _, tok, key = place_of(item)
                        own = item % ITEMS
                        ahead = 1 if item >= ITEMS else 0
                        j = own % 2
                        if key:
                            wait(pe, wkv_lo_s, g, 2, 2 * ahead + 2)
                        else:
                            wait(pe, wq_lo_s, g, 2, 2 * ahead + j + 1)
                        wait(pe, rope_mul, g, ITEMS, item - 1)
                        bank = bank_rope[item % 2]
                        if key:
                            for c in range(KC):
                                mm = product(bank[:, :], wk_hi[:, c, :], wk_lo[:, c, :], cT_hi[:, c, tok], cT_lo[:, c, tok], c == 0, c == KC - 1)
                        else:
                            for k in range(2):
                                h = 2 * j + k
                                cols = slice(h * D, (h + 1) * D)
                                for c in range(KC):
                                    mm = product(bank[:, k * PAIR:(k + 1) * PAIR], wq_hi[:, c, cols], wq_lo[:, c, cols],
                                                 xT_hi[:, c, tok], xT_lo[:, c, tok], c == 0, c == KC - 1)
                        mm.then_inc(proj_mm, 1)

                    def make_values(g, half):
                        wait(pe, wkv_lo_s, g, 2, 2)
                        if half == 0:
                            wait(pe, v_lo_s, g, 2, 0)
                        else:
                            wait(pe, v_kept, g, 2, 1)
                        tok = slice(half * HALF, (half + 1) * HALF)
                        for c in range(KC):
                            mm = product(bank_v[:, :], wv_hi[:, c, :], wv_lo[:, c, :], cT_hi[:, c, tok], cT_lo[:, c, tok], c == 0, c == KC - 1)
                        mm.then_inc(v_mm, 1)

                    def turn_values(g, half):
                        if half == 0:
                            wait(pe, v_kept, g, 2, 2)
                        else:
                            wait(pe, v_lo_s, g, 2, 1)
                        for b in range(4):
                            mm = nc.tensor.transpose(bank_v[:, b * D:(b + 1) * D], vT[:, (4 * half + b) * S:(4 * half + b + 1) * S], ident[:, :])
                        mm.then_inc(v_turned, 1)

                    def score(g, u):
                        if u % 2 == 0:
                            wait(pe, rope_sum, g, ITEMS, 4 + u if u else 3)
                        wait(pe, score_kept, g, UNITS, u - 1)
                        keys = slice(u * S, (u + 1) * S)
                        q = slice((u % 2) * S, (u % 2 + 1) * S)
                        for h in range(GR):
                            mm = nc.tensor.matmul(bank_scores[u % 2][:, h * S:(h + 1) * S], qT[:, (u // 2) % 2, h, q], kT[:, keys], start=True, stop=True)
                        mm.then_inc(score_mm, 1)

                    def turn_probs(g, u):
                        wait(pe, probs_done, g, UNITS, u + 1)
                        wait(pe, pT_lo_s, g, UNITS, u)
                        for h in range(GR):
                            mm = nc.tensor.transpose(bank_pT[:, h * S:(h + 1) * S], probs[:, u % 2, h, :], ident[:, :])
                        mm.then_inc(pT_mm, 1)

                    def attend(g, u):
                        if u == 0:
                            wait(pe, v_lo_s, g, 2, 2)
                        wait(pe, pT_lo_s, g, UNITS, u + 1)
                        wait(pe, o_lo_s, g, UNITS, u)
                        product(bank_o[:, :], v_hi[:, u % UNITS, :], v_lo[:, u % UNITS, :], pT_hi[:, u % 2, :], pT_lo[:, u % 2, :], True, True).then_inc(o_mm, 1)

                    def project_out(g, u):
                        wait(pe, o_lo_s, g, UNITS, u + 1)
                        wait(pe, y_added, g, UNITS, u)
                        for h in range(GR):
                            if u == 0:
                                wait(pe, wo_lo_s, g, GR, h + 1)
                            mm = product(bank_y[:, :], oT_hi[:, u % 2, h, :], oT_lo[:, u % 2, h, :], wo_hi[:, h, :], wo_lo[:, h, :], h == 0, h == GR - 1)
                        mm.then_inc(y_mm, 1)

                    def group(g):
                        for step, u, items, turn, att, out_unit in steps(g):
                            if u is not None:
                                score(g, u)
                            for item in items:
                                project(g, item)
                            if step < 2 and u is not None:
                                make_values(g, step)
                            if att is not None:
                                attend(g, att)
                            if step == 1 and u is not None:
                                turn_values(g, 0)
                            if out_unit is not None:
                                project_out(g, out_unit)
                            if step == 1 and u is not None:
                                turn_values(g, 1)
                            if turn is not None:
                                turn_probs(g, turn)

                    for item in FIRST_ITEMS:
                        project(0, item)
                    group(0)
                    with pe.Fori(1, KVH - 1) as g:
                        group(g)
                    group(KVH - 1)
                    group(KVH)

        with ExitStack() as ctx:
            xn = sb("xn1", [P, 2, E], ctx=ctx)
            wint = sb("wint", [P, KC, E], I32, ctx)
            wmask = sb("wmask", [P, KC, E], I32, ctx)
            scales = sb("scales", [P, KC, NG], ctx=ctx)
            zeros = sb("zeros", [P, KC, NG], ctx=ctx)
            scale2 = sb("scale2", [P, KC], ctx=ctx)
            weight = sb("weight", [P, KC, E], ctx=ctx)
            fmask = sb("fmask", [P, KC, E], ctx=ctx)
            f_float = sem("f_float")
            wT_hi, wT_lo = (sb(f"wT_{n}", [P, KC, E], F32R, ctx) for n in ("hi", "lo"))
            bias = sb("bias", [P, E], ctx=ctx)
            summed = sb("summed", [P, 2, E], ctx=ctx)
            f_in, f_deq, f_turned, f_hi, f_lo, f_mm, f_sum, f_added = (
                sem(f"f_{n}") for n in ("in", "deq", "turned", "hi", "lo", "mm", "sum", "added"))

            with nc.Block() as block:
                @block.sync
                def _(sp):
                    for dst, src in ((wint, "wint"), (scales, "scales"), (zeros, "zeros"), (wmask, "wmask")):
                        sp.dma_start(dst[:, :, :], a[src]).then_inc(f_in, 16)
                    sp.dma_start(scale2[:, :], a["scale2"]).then_inc(f_in, 16)
                    sp.dma_start(bias[:, :], a["fbias"].partition_broadcast(P)).then_inc(f_in, 16)

                @block.gpsimd
                def _(pool):
                    pool.wait_ge(f_in, 16 * 6)
                    pool.wait_ge(f_float, 2)
                    shape = [P, KC * NG, GROUP]
                    wide = weight[:, :, :].rearrange("p c (g n) -> p (c g) n", g=NG)
                    nc.gpsimd.tensor_tensor(wide, wide,
                                            zeros[:, :, :].rearrange("p c g -> p (c g)").unsqueeze(2).broadcast_to(shape), ALU.subtract).then_inc(f_deq, 1)
                    pool.wait_ge(f_deq, 1)
                    nc.gpsimd.tensor_tensor(wide, wide, scales[:, :, :].rearrange("p c g -> p (c g)").unsqueeze(2).broadcast_to(shape), ALU.mult).then_inc(f_deq, 1)
                    pool.wait_ge(f_deq, 2)
                    nc.gpsimd.tensor_tensor(weight[:, :, :], weight[:, :, :], scale2[:, :].unsqueeze(2).broadcast_to([P, KC, E]), ALU.mult).then_inc(f_deq, 1)
                    pool.wait_ge(f_deq, 3)
                    nc.gpsimd.tensor_tensor(weight[:, :, :], weight[:, :, :], fmask[:, :, :], ALU.mult).then_inc(f_deq, 1)

                @block.scalar
                def _(act):
                    act.wait_ge(f_in, 16 * 6)
                    nc.scalar.activation(weight[:, :, :], wint[:, :, :], ACT.Copy).then_inc(f_float, 1)
                    nc.scalar.activation(fmask[:, :, :], wmask[:, :, :], ACT.Copy).then_inc(f_float, 1)
                    norm_scalar(act, 1)
                    for c in range(KC):
                        act.wait_ge(f_turned, c + 1)
                        nc.scalar.activation(wT_hi[:, c, :], psum[2 + c % 2][:, :], ACT.Copy).then_inc(f_hi, 1)

                @block.vector
                def _(dve):
                    norm_vector(dve, 1, xn)
                    for c in range(KC):
                        dve.wait_ge(f_hi, c + 1)
                        nc.vector.tensor_tensor(wT_lo[:, c, :], psum[2 + c % 2][:, :], wT_hi[:, c, :].bitcast(F32), ALU.subtract).then_inc(f_lo, 1)
                    for t in range(NB):
                        dve.wait_ge(f_mm, t + 1)
                        nc.vector.tensor_tensor(summed[:, t % 2, :], psum[4 + t % 2][:, :], bias[:, :], ALU.add).then_inc(f_sum, 1)
                        dve.wait_ge(f_sum, t + 1)
                        nc.vector.scalar_tensor_tensor(x[:, t, :], summed[:, t % 2, :], gates[:, 2:3], x[:, t, :], ALU.mult, ALU.add).then_inc(f_added, 1)

                @block.tensor
                def _(pe):
                    norm_tensor(pe, 1, xn)
                    pe.wait_ge(f_deq, 4)
                    for c in range(KC):
                        if c >= 2:
                            pe.wait_ge(f_lo, c - 1)
                        for r in range(KC):
                            mm = nc.tensor.transpose(psum[2 + c % 2][:, r * P:(r + 1) * P], weight[:, r, c * P:(c + 1) * P], ident[:, :])
                        mm.then_inc(f_turned, 1)
                    pe.wait_ge(f_lo, KC)
                    pe.wait_ge(ln_lo, 2 * NB)
                    for t in range(NB):
                        if t >= 2:
                            pe.wait_ge(f_sum, t - 1)
                        tok = slice(t * P, (t + 1) * P)
                        for c in range(KC):
                            mm = product(psum[4 + t % 2][:, :], xT_hi[:, c, tok], xT_lo[:, c, tok], wT_hi[:, c, :], wT_lo[:, c, :], c == 0, c == KC - 1)
                        mm.then_inc(f_mm, 1)

        RING = 4
        ew = sb("ew", [P, RING, KC, E])
        w_in = [sem(f"w_in{k}") for k in range(RING)]
        with ExitStack() as ctx:
            xn = sb("xn2", [P, 2, E], ctx=ctx)
            raw = sb("l1_raw", [P, 2, KC, E], ctx=ctx)
            w_hi, w_lo = (sb(f"l1_w_{n}", [P, 2, KC, E], F32R, ctx) for n in ("hi", "lo"))
            b1 = sb("l1_bias", [P, 2, KC], ctx=ctx)
            c_raw = sb("l1_ctx", [P, NB, E], ctx=ctx)
            k1, q1 = (sb(f"l1_{n}", [P, KC, T // 2], ctx=ctx) for n in ("k", "q"))
            l1p = sb("l1_probs", [P, 4, S], ctx=ctx)
            l1pT = sb("l1_pT", [P, 4 * S], ctx=ctx)
            l1max = sb("l1_max", [P, 4], ctx=ctx)
            l1nb = sb("l1_nb", [P, 4], ctx=ctx)
            l1sum = sb("l1_sum", [P, 4], ctx=ctx)
            l1inv = sb("l1_inv", [P, 4], ctx=ctx)
            SC1 = float(E) ** -0.5
            (g_in, g_whi, g_wlo, g_mm, g_kept, g_smm, g_max, g_nb, g_exp, g_inv, g_norm, g_turned, g_pkept, g_omm, g_added) = (
                sem(f"g_{n}") for n in ("in", "whi", "wlo", "mm", "kept", "smm", "max", "nb", "exp", "inv", "norm", "turned",
                                        "pkept", "omm", "added"))
            with nc.Block() as block:
                @block.sync
                def _(sp):
                    sp.dma_start(raw[:, 0, :, :], a["wk1"]).then_inc(g_in, 16)
                    sp.dma_start(raw[:, 1, :, :], a["wq1"]).then_inc(g_in, 16)
                    sp.dma_start(b1[:, :, :], a["b1"]).then_inc(g_in, 16)
                    sp.dma_start(c_raw[:, :, :], a["ctx"]).then_inc(g_in, 16)
                    for k in range(RING):
                        sp.dma_start(ew[:, k, :, :], a["ew"][k]).then_inc(w_in[k], 16)

                @block.gpsimd
                def _(pool):
                    for w in range(2):
                        pool.wait_ge(g_whi, w + 1)
                        nc.gpsimd.tensor_tensor(w_lo[:, w, :, :], raw[:, w, :, :], w_hi[:, w, :, :].bitcast(F32), ALU.subtract).then_inc(g_wlo, 1)
                    for n in range(2):
                        pool.wait_ge(g_inv, n + 1)
                        nc.gpsimd.tensor_tensor(l1p[:, :, :], l1p[:, :, :], l1inv[:, :].unsqueeze(2).broadcast_to([P, 4, S]), ALU.mult).then_inc(g_norm, 1)

                @block.scalar
                def _(act):
                    act.wait_ge(g_in, 64)
                    for w in range(2):
                        nc.scalar.activation(w_hi[:, w, :, :], raw[:, w, :, :], ACT.Copy).then_inc(g_whi, 1)
                    norm_scalar(act, 2)
                    for n in range(2):
                        for i in range(2 * KC):
                            w, c = i // KC, i % KC
                            act.wait_ge(g_mm, 2 * KC * n + i + 1)
                            nc.scalar.activation((k1, q1)[w][:, c, :], psum[2 + i % 2][:, :], ACT.Identity, bias=b1[:, w, c:c + 1]).then_inc(g_kept, 1)
                        act.wait_ge(g_nb, n + 1)
                        for b in range(4):
                            ex = nc.scalar.activation(l1p[:, b, :], psum[4][:, b * S:(b + 1) * S], ACT.Exp, scale=SC1,
                                                      bias=l1nb[:, b:b + 1], accum_out=l1sum[:, b:b + 1])
                        ex.then_inc(g_exp, 1)
                        act.wait_ge(g_turned, n + 1)
                        nc.scalar.activation(l1pT[:, :], psum[5][:, :], ACT.Copy).then_inc(g_pkept, 1)

                @block.vector
                def _(dve):
                    norm_vector(dve, 2, xn)
                    for n in range(2):
                        dve.wait_ge(g_smm, n + 1)
                        nc.vector.tensor_reduce(l1max[:, :], psum[4][:, :].rearrange("p (b k) -> p b k", b=4), AX.X, ALU.max).then_inc(g_max, 1)
                        dve.wait_ge(g_max, n + 1)
                        nc.vector.tensor_scalar(l1nb[:, :], l1max[:, :], -SC1, None, ALU.mult).then_inc(g_nb, 1)
                        dve.wait_ge(g_exp, n + 1)
                        nc.vector.reciprocal(l1inv[:, :], l1sum[:, :]).then_inc(g_inv, 1)
                        for b in range(4):
                            dve.wait_ge(g_omm, 4 * n + b + 1)
                            nc.vector.scalar_tensor_tensor(x[:, 4 * n + b, :], psum[6 + b % 2][:, :], gates[:, 1:2], x[:, 4 * n + b, :],
                                                           ALU.mult, ALU.add).then_inc(g_added, 1)

                @block.tensor
                def _(pe):
                    norm_tensor(pe, 2, xn)
                    pe.wait_ge(ln_lo, 3 * NB)
                    for n in range(2):
                        half = slice(n * 512, (n + 1) * 512)
                        for i in range(2 * KC):
                            w, c = i // KC, i % KC
                            pe.wait_ge(g_wlo, w + 1)
                            if 2 * KC * n + i >= 2:
                                pe.wait_ge(g_kept, 2 * KC * n + i - 1)
                            r_hi, r_lo = ((cT_hi, cT_lo), (xT_hi, xT_lo))[w]
                            for k in range(KC):
                                cols = slice(c * P, (c + 1) * P)
                                mm = product(psum[2 + i % 2][:, :], w_hi[:, w, k, cols], w_lo[:, w, k, cols], r_hi[:, k, half], r_lo[:, k, half], k == 0, k == KC - 1)
                            mm.then_inc(g_mm, 1)
                        pe.wait_ge(g_kept, 2 * KC * (n + 1))
                        if n:
                            pe.wait_ge(g_exp, n)
                        for b in range(4):
                            q = slice(b * S, (b + 1) * S)
                            for c in range(KC):
                                mm = nc.tensor.matmul(psum[4][:, q], q1[:, c, q], k1[:, c, q], start=c == 0, stop=c == KC - 1)
                        mm.then_inc(g_smm, 1)
                        pe.wait_ge(g_norm, n + 1)
                        for b in range(4):
                            mm = nc.tensor.transpose(psum[5][:, b * S:(b + 1) * S], l1p[:, b, :], ident[:, :])
                        mm.then_inc(g_turned, 1)
                        pe.wait_ge(g_pkept, n + 1)
                        for b in range(4):
                            if 4 * n + b >= 2:
                                pe.wait_ge(g_added, 4 * n + b - 1)
                            q = slice(b * S, (b + 1) * S)
                            nc.tensor.matmul(psum[6 + b % 2][:, :], l1pT[:, q], c_raw[:, 4 * n + b, :], start=True, stop=True).then_inc(g_omm, 1)

        EXTRA = (TOP * T - 1) // P
        SLOTS = NX + EXTRA
        ROUNDS = -(-SLOTS // RING)
        NOWHERE = 4 * T
        xn_rows = nc.dram_tensor("xn_rows", [T, E], F32, kind="Internal").ap()
        places = nc.dram_tensor("places", [P * SLOTS, 1], I32, kind="Internal").ap()
        picked = nc.dram_tensor("picked", [TOP * T, E], F32, kind="Internal").ap()
        with ExitStack() as ctx:
            xn = sb("xn3", [P, NB, E], ctx=ctx)
            gw = sb("gw", [P, KC, NX], ctx=ctx)
            gw_hi, gw_lo = (sb(f"gw_{n}", [P, KC, NX], F32R, ctx) for n in ("hi", "lo"))
            logits = sb("logits", [P, NB, NX], ctx=ctx)
            best = sb("best", [P, NB, 8], ctx=ctx)
            best_at = sb("best_at", [P, NB, 8], U32, ctx)
            bestf = sb("bestf", [P, NB, TOP], ctx=ctx)
            numbers = sb("numbers", [P, NX], ctx=ctx)
            before = sb("before", [P, P], ctx=ctx)
            ones = sb("ones", [P, P], ctx=ctx)
            pair_rows = sb("pair_rows", [P, TOP, NB], I32, ctx)
            diff, ediff, edp1 = (sb(n, [P, NB], ctx=ctx) for n in ("diff", "ediff", "edp1"))
            wts = sb("wts", [P, TOP, NB], ctx=ctx)
            onehot = sb("onehot", [P, TOP, NB, NX], ctx=ctx)
            chosen = sb("chosen", [P, NB, NX], ctx=ctx)
            weighted = sb("weighted", [P, TOP, NB, NX], ctx=ctx)
            comb = sb("comb", [P, NB, NX], ctx=ctx)
            combT = sb("combT", [NX, NB, P], ctx=ctx)
            rank = sb("rank", [P, NB, NX], ctx=ctx)
            count = sb("count", [P, NX], ctx=ctx)
            extra = sb("extra", [P, NX], ctx=ctx)
            upto = sb("upto", [P, 2, 16 + NX], ctx=ctx)
            ahead = sb("ahead", [P, NX], ctx=ctx)
            full = sb("full", [P, NB, NX], ctx=ctx)
            over = sb("over", [P, NB, NX], ctx=ctx)
            spot = sb("spot", [P, NB, NX], ctx=ctx)
            spot_of = sb("spot_of", [P, TOP, NB], ctx=ctx)
            spot_at = sb("spot_at", [P, TOP, NB], U32, ctx)
            passed = sb("passed", [P, 16, NX], ctx=ctx)
            owner = sb("owner", [P, 16], ctx=ctx)
            owner_at = sb("owner_at", [P, 16], I32, ctx)
            nowhere = sb("nowhere", [P, SLOTS], I32, ctx)
            place_row = sb("place_row", [P, SLOTS], I32, ctx)
            place_token = sb("place_token", [P, SLOTS], I32, ctx)
            eb = sb("eb", [NX, E], ctx=ctx)
            taken = sb("taken", [P, RING, E], ctx=ctx)
            takenT = sb("takenT", [P, RING, KC, P], ctx=ctx)
            result = sb("result", [P, RING, E], ctx=ctx)
            chosen_y = sb("chosen_y", [P, TOP, NB, E], ctx=ctx)
            (m_in, m_gh, m_gl, m_log, m_logk, m_best, m_step, m_exp, m_rank, m_cT, m_cTk, m_bmm, m_badd, m_out) = (
                sem(f"m_{n}") for n in ("in", "gh", "gl", "log", "logk", "best", "step", "exp", "rank", "cT", "cTk", "bmm", "badd", "out"))
            rows_out, prefilled, scattered, places_in, tokens_ready, nowhere_set = (
                sem(n) for n in ("rows_out", "prefilled", "scattered", "places_in", "tokens_ready", "nowhere_set"))
            spots_ready, comb_ready = sem("spots_ready"), sem("comb_ready")
            t_in = [sem(f"t_in{k}") for k in range(RING)]
            y_out = [sem(f"y_out{k}") for k in range(RING)]
            t_turned, t_kept, e_mm, e_kept = (sem(n) for n in ("t_turned", "t_kept", "e_mm", "e_kept"))
            y_in = [sem(f"y_in{k}") for k in range(2)]
            y_added2 = sem("y_added2")
            gatepost3 = sb("gatepost3", [P, 1], ctx=ctx)
            gatepost4 = sb("gatepost4", [P, 2], ctx=ctx)
            zero = sb("zero", [P, 1], ctx=ctx)
            take_at, give_at = (sb(n, [P, RING], I32, ctx) for n in ("take_at", "give_at"))
            take_set, give_set = sem("take_set"), sem("give_set")

            def slots(r):
                return range(SLOTS - RING * (ROUNDS - 1) if isinstance(r, int) and r == ROUNDS - 1 else RING)

            def rounds(engine, one):
                one(0)
                with engine.Fori(1, ROUNDS - 1) as r:
                    one(r)
                one(ROUNDS - 1)

            with nc.Block() as block:
                @block.sync
                def _(sp):
                    sp.dma_start(gw[:, :, :], a["gw"]).then_inc(m_in, 16)
                    sp.dma_start(numbers[:, :], a["numbers"].partition_broadcast(P)).then_inc(m_in, 16)
                    sp.dma_start(before[:, :], a["before"]).then_inc(m_in, 16)
                    sp.dma_start(pair_rows[:, :, :], a["pair_rows"]).then_inc(m_in, 16)
                    sp.dma_start(eb[:, :], a["eb"]).then_inc(m_in, 16)
                    sp.wait_ge(nowhere_set, 1)
                    sp.dma_start(places.rearrange("(p s) o -> p (s o)", s=SLOTS), nowhere[:, :]).then_inc(prefilled, 16)
                    sp.wait_ge(ln_norm, 4 * NB)
                    sp.dma_start(xn_rows.rearrange("(t p) e -> p t e", p=P), xn[:, :, :]).then_inc(rows_out, 16)

                    def weights(r, expert):
                        for k in slots(r):
                            wait(sp, e_mm, r, RING, k - RING + 1)
                            sp.dma_start(ew[:, k, :, :], a["ew"][bass.ds(expert(k), 1)].rearrange("o p c n -> p (o c) n")).then_inc(w_in[k], 16)

                    STATIC = NX // RING
                    with sp.Fori(1, STATIC) as r:
                        weights(r, lambda k: r * RING + k)
                    sp.wait_ge(spots_ready, 1)
                    with sp.Fori(STATIC, ROUNDS - 1) as r:
                        weights(r, lambda k: sp.value_load(owner_at[0:1, bass.ds((r - STATIC) * RING + k, 1)], min_val=0, max_val=NX - 1))
                    weights(ROUNDS - 1, lambda k: sp.value_load(owner_at[0:1, (ROUNDS - 1 - STATIC) * RING + k:(ROUNDS - 1 - STATIC) * RING + k + 1],
                                                                min_val=0, max_val=NX - 1))
                    for k in range(RING):
                        sp.wait_ge(y_out[k], 16 * len([s for s in range(SLOTS) if s % RING == k]))
                    for k in range(2):
                        for c in range(TOP):
                            sp.dma_start(chosen_y[:, c, 4 * k:4 * k + 4, :],
                                         picked.rearrange("(c t p) e -> p c t e", c=TOP, p=P)[:, c, 4 * k:4 * k + 4, :]).then_inc(y_in[k], 16)
                    for k in range(2):
                        sp.wait_ge(y_added2, NB * (k + 1))
                        sp.dma_start(out[:, 4 * k:4 * k + 4, :], x[:, 4 * k:4 * k + 4, :]).then_inc(m_out, 16)
                    sp.wait_ge(m_out, 32)

                @block.gpsimd
                def _(pool):
                    nc.gpsimd.memset(nowhere[:, :], NOWHERE).then_inc(nowhere_set, 1)
                    nc.gpsimd.memset(ones[:, :], 1.0).then_inc(nowhere_set, 1)
                    nc.gpsimd.memset(zero[:, :], 0.0).then_inc(nowhere_set, 1)
                    pool.wait_ge(m_gh, 1)
                    nc.gpsimd.tensor_tensor(gw_lo[:, :, :], gw[:, :, :], gw_hi[:, :, :].bitcast(F32), ALU.subtract).then_inc(m_gl, 1)
                    pool.wait_ge(prefilled, 16)
                    pool.wait_ge(spots_ready, 1)
                    for k in range(TOP):
                        for t in range(NB):
                            pool.indirect_dma_start(out=places, out_offset=bass.IndirectOffsetOnAxis(ap=spot_at[:, k, t:t + 1], axis=0),
                                                    in_=pair_rows[:, k, t:t + 1], in_offset=None).then_inc(scattered, 16)
                    pool.wait_ge(scattered, 16 * TOP * NB)
                    pool.dma_start(place_row[:, :], places.rearrange("(p s) o -> p (s o)", s=SLOTS)).then_inc(places_in, 16)
                    pool.wait_ge(nowhere_set, 3)
                    pool.wait_ge(tokens_ready, 1)
                    pool.wait_ge(rows_out, 16)

                    def carry(n):
                        nc.gpsimd.tensor_tensor(gatepost4[:, n:n + 1], zero[:, :], zero[:, :], ALU.add)

                    def take(r, k):
                        wait(pool, t_turned, r, RING, k - RING + 1)
                        carry(0)
                        nc.gpsimd.tensor_copy(take_at[:, k:k + 1], place_token[:, bass.ds(r * RING + k, 1)]).then_inc(take_set, 1)
                        wait(pool, take_set, r, RING, k + 1)
                        carry(1)
                        pool.indirect_dma_start(out=taken[:, k, :], out_offset=None, in_=xn_rows,
                                                in_offset=bass.IndirectOffsetOnAxis(ap=take_at[:, k:k + 1].bitcast(U32), axis=0)).then_inc(t_in[k], 16)

                    def give(r, k):
                        wait(pool, e_kept, r, RING, k + 1)
                        carry(0)
                        nc.gpsimd.tensor_copy(give_at[:, k:k + 1], place_row[:, bass.ds(r * RING + k, 1)]).then_inc(give_set, 1)
                        wait(pool, give_set, r, RING, k + 1)
                        carry(1)
                        pool.indirect_dma_start(out=picked, out_offset=bass.IndirectOffsetOnAxis(ap=give_at[:, k:k + 1].bitcast(U32), axis=0),
                                                in_=result[:, k, :], in_offset=None, bounds_check=TOP * T - 1, oob_is_err=False).then_inc(y_out[k], 16)

                    for k in range(RING):
                        take(0, k)

                    def one(r):
                        for k in slots(r):
                            give(r, k)
                            if not (isinstance(r, int) and (r == ROUNDS - 1 or (r == ROUNDS - 2 and k not in slots(ROUNDS - 1)))):
                                take(r + 1, k)
                    one(0)
                    with pool.Fori(1, ROUNDS - 2) as r:
                        one(r)
                    one(ROUNDS - 2)
                    one(ROUNDS - 1)

                @block.scalar
                def _(act):
                    act.wait_ge(m_in, 80)
                    nc.scalar.activation(gw_hi[:, :, :], gw[:, :, :], ACT.Copy).then_inc(m_gh, 1)
                    norm_scalar(act, 3)
                    act.wait_ge(m_log, 1)
                    nc.scalar.activation(logits[:, :, :], psum[2][:, 0:NB * NX].rearrange("p (t e) -> p t e", t=NB), ACT.Copy).then_inc(m_logk, 1)
                    act.wait_ge(m_step, 1)
                    nc.scalar.activation(ediff[:, :], diff[:, :], ACT.Exp).then_inc(m_exp, 1)

                    def one(r):
                        for k in slots(r):
                            wait(act, t_turned, r, RING, k + 1)
                            wait(act, e_mm, r, RING, k - RING + 1)
                            nc.scalar.activation(takenT[:, k, :, :], psum[k % 2][:, :].rearrange("p (c t) -> p c t", c=KC), ACT.Copy).then_inc(t_kept, 1)
                    rounds(act, one)

                @block.vector
                def _(dve):
                    norm_vector(dve, 3, xn, whole=True)
                    dve.wait_ge(m_logk, 1)
                    for t in range(NB):
                        nc.vector.max(best[:, t, :], logits[:, t, :]).then_inc(m_best, 1)
                    for t in range(NB):
                        dve.wait_ge(m_best, t + 1)
                        nc.vector.max_index(best_at[:, t, :], best[:, t, :], logits[:, t, :]).then_inc(m_best, 1)
                    done = [0]

                    def step(op):
                        done[0] += 1
                        op.then_inc(m_step, 1)
                        dve.wait_ge(m_step, done[0])

                    def over_experts(ap):
                        return ap.unsqueeze(1).broadcast_to([P, NB, NX])

                    def over_tokens(ap):
                        return ap.unsqueeze(2).broadcast_to([P, NB, NX])

                    dve.wait_ge(m_best, 2 * NB)
                    step(nc.vector.tensor_tensor(diff[:, :], best[:, :, 1], best[:, :, 0], ALU.subtract))
                    step(nc.vector.tensor_copy(bestf[:, :, :], best_at[:, :, 0:TOP]))
                    for k in range(TOP):
                        step(nc.vector.tensor_tensor(onehot[:, k, :, :], over_experts(numbers[:, :]), over_tokens(bestf[:, :, k]), ALU.is_equal))
                    step(nc.vector.tensor_tensor(chosen[:, :, :], onehot[:, 0, :, :], onehot[:, 1, :, :], ALU.add))
                    step(nc.vector.memset(extra[:, :], 0.0))
                    step(nc.vector.memset(full[:, :, :], 0.0))
                    step(nc.vector.memset(upto[:, :, :], 0.0))
                    dve.wait_ge(m_rank, 1)
                    step(nc.vector.tensor_copy(rank[:, :, :], psum[3][:, 0:NB * NX].rearrange("p (t e) -> p t e", t=NB)))
                    step(nc.vector.tensor_copy(count[:, :], psum[3][:, NB * NX:(NB + 1) * NX]))
                    for m in range(1, NB):
                        step(nc.vector.scalar_tensor_tensor(extra[:, :], count[:, :], float(m * P), extra[:, :], ALU.is_gt, ALU.add))
                        step(nc.vector.scalar_tensor_tensor(full[:, :, :], rank[:, :, :], float(m * P), full[:, :, :], ALU.is_ge, ALU.add))
                    step(nc.vector.tensor_copy(upto[:, 0, 16:], extra[:, :]))
                    for n in range(5):
                        src, dst, by = n % 2, (n + 1) % 2, 1 << n
                        step(nc.vector.tensor_tensor(upto[:, dst, 16:], upto[:, src, 16:], upto[:, src, 16 - by:16 + NX - by], ALU.add))
                    summed_to = upto[:, 1, 16:]
                    step(nc.vector.tensor_tensor(ahead[:, :], summed_to, extra[:, :], ALU.subtract))
                    for j in range(16):
                        last = nc.vector.tensor_scalar(passed[:, j, :], summed_to, float(j), None, ALU.is_le)
                    step(last)
                    step(nc.vector.tensor_reduce(owner[:, :], passed[:, :, :], AX.X, ALU.add))
                    step(nc.vector.tensor_scalar(owner_at[:, :], owner[:, :], float(NX - 1), None, ALU.min))
                    step(nc.vector.scalar_tensor_tensor(spot[:, :, :], full[:, :, :], -float(P), rank[:, :, :], ALU.mult, ALU.add))
                    step(nc.vector.scalar_tensor_tensor(spot[:, :, :], spot[:, :, :], float(SLOTS), over_experts(numbers[:, :]), ALU.mult, ALU.add))
                    step(nc.vector.tensor_tensor(over[:, :, :], full[:, :, :], over_experts(ahead[:, :]), ALU.add))
                    step(nc.vector.scalar_tensor_tensor(over[:, :, :], over[:, :, :], float(NX - 1), over_experts(numbers[:, :]), ALU.add, ALU.subtract))
                    step(nc.vector.scalar_tensor_tensor(over[:, :, :], full[:, :, :], 0.0, over[:, :, :], ALU.is_gt, ALU.mult))
                    step(nc.vector.tensor_tensor(spot[:, :, :], spot[:, :, :], over[:, :, :], ALU.add))
                    for k in range(TOP):
                        step(nc.vector.tensor_tensor(weighted[:, k, :, :], onehot[:, k, :, :], spot[:, :, :], ALU.mult))
                        step(nc.vector.tensor_reduce(spot_of[:, k, :], weighted[:, k, :, :], AX.X, ALU.add))
                    step(nc.vector.tensor_copy(spot_at[:, :, :], spot_of[:, :, :]))
                    nc.vector.memset(gatepost3[:, :], 0.0).then_inc(spots_ready, 1)
                    dve.wait_ge(m_exp, 1)
                    step(nc.vector.tensor_scalar_add(edp1[:, :], ediff[:, :], 1.0))
                    step(nc.vector.reciprocal(wts[:, 0, :], edp1[:, :]))
                    step(nc.vector.tensor_tensor(wts[:, 1, :], wts[:, 0, :], ediff[:, :], ALU.mult))
                    step(nc.vector.tensor_scalar(wts[:, :, :], wts[:, :, :], gates[:, 3:4], None, ALU.mult))
                    for k in range(TOP):
                        step(nc.vector.tensor_tensor(weighted[:, k, :, :], onehot[:, k, :, :], over_tokens(wts[:, k, :]), ALU.mult))
                    nc.vector.tensor_tensor(comb[:, :, :], weighted[:, 0, :, :], weighted[:, 1, :, :], ALU.add).then_inc(comb_ready, 1)
                    for t in range(NB):
                        dve.wait_ge(m_cT, t + 1)
                        nc.vector.tensor_copy(combT[:, t, :], psum[2][0:NX, (t % 4) * P:(t % 4 + 1) * P]).then_inc(m_cTk, 1)
                    for t in range(NB):
                        dve.wait_ge(m_bmm, t + 1)
                        nc.vector.tensor_tensor(x[:, t, :], psum[4 + t % 2][:, :], x[:, t, :], ALU.add).then_inc(m_badd, 1)
                    dve.wait_ge(places_in, 16)
                    nc.vector.tensor_scalar(place_token[:, :], place_row[:, :], T - 1, None, ALU.bitwise_and).then_inc(tokens_ready, 1)

                    def one(r):
                        for k in slots(r):
                            wait(dve, e_mm, r, RING, k + 1)
                            wait(dve, y_out[k], r, 16, 0)
                            nc.vector.tensor_copy(result[:, k, :], psum[4 + k][:, :]).then_inc(e_kept, 1)
                    rounds(dve, one)
                    for n in range(2):
                        dve.wait_ge(y_in[n], 16 * TOP)
                        for c in range(TOP):
                            for t in range(4 * n, 4 * n + 4):
                                if c:
                                    dve.wait_ge(y_added2, NB * n + t % 4 + 1)
                                nc.vector.scalar_tensor_tensor(x[:, t, :], chosen_y[:, c, t, :], wts[:, c, t:t + 1], x[:, t, :],
                                                               ALU.mult, ALU.add).then_inc(y_added2, 1)

                @block.tensor
                def _(pe):
                    norm_tensor(pe, 3, xn, whole=True)
                    pe.wait_ge(ln_lo, 4 * NB)
                    pe.wait_ge(m_gl, 1)
                    for t in range(NB):
                        tok = slice(t * P, (t + 1) * P)
                        for c in range(KC):
                            mm = product(psum[2][:, t * NX:(t + 1) * NX], xT_hi[:, c, tok], xT_lo[:, c, tok], gw_hi[:, c, :], gw_lo[:, c, :], c == 0, c == KC - 1)
                    mm.then_inc(m_log, 1)
                    pe.wait_ge(m_step, 5)
                    pe.wait_ge(nowhere_set, 2)
                    nc.tensor.matmul(psum[3][:, 0:NB * NX], before[:, :], chosen[:, :, :].rearrange("p t e -> p (t e)"),
                                     start=True, stop=False, skip_group_check=True)
                    for t in range(NB):
                        rest = NB - t
                        mm = nc.tensor.matmul(psum[3][:, (t + 1) * NX:(NB + 1) * NX].rearrange("p (t e) -> p t e", e=NX), ones[:, :],
                                              chosen[:, t, :].unsqueeze(1).broadcast_to([P, rest, NX]), start=False, stop=t == NB - 1,
                                              skip_group_check=True)
                    mm.then_inc(m_rank, 1)
                    pe.wait_ge(comb_ready, 1)
                    pe.wait_ge(m_logk, 1)
                    for t in range(NB):
                        if t >= 1:
                            pe.wait_ge(m_cTk, t)
                        nc.tensor.transpose(psum[2][0:NX, (t % 4) * P:(t % 4 + 1) * P], comb[:, t, :], ident[:, :]).then_inc(m_cT, 1)
                    for t in range(NB):
                        pe.wait_ge(m_cTk, t + 1)
                        if t >= 2:
                            pe.wait_ge(m_badd, t - 1)
                        nc.tensor.matmul(psum[4 + t % 2][:, :], combT[:, t, :], eb[:, :], start=True, stop=True).then_inc(m_bmm, 1)
                    pe.wait_ge(m_badd, NB)

                    def turn(r, k):
                        wait(pe, t_in[k], r, 16, 16)
                        wait(pe, t_kept, r, RING, k - 1)
                        for c in range(KC):
                            mm = nc.tensor.transpose(psum[k % 2][:, c * P:(c + 1) * P], taken[:, k, c * P:(c + 1) * P], ident[:, :])
                        mm.then_inc(t_turned, 1)

                    def one(r):
                        last = isinstance(r, int) and r == ROUNDS - 1
                        for k in slots(r):
                            if k + 1 < len(slots(r)):
                                turn(r, k + 1)
                            elif not last:
                                turn(r + 1, 0)
                            wait(pe, t_kept, r, RING, k + 1)
                            wait(pe, w_in[k], r, 16, 16)
                            wait(pe, e_kept, r, RING, k - RING + 1)
                            for c in range(KC):
                                mm = nc.tensor.matmul(psum[4 + k][:, :], takenT[:, k, c, :], ew[:, k, c, :], start=c == 0, stop=c == KC - 1)
                            mm.then_inc(e_mm, 1)
                    turn(0, 0)
                    rounds(pe, one)


def kernel(x, ctx_4096, pos_BxS2, mask_BxSxS2_ik0, g_xattn, g_ffn, L0_xattn_Wq, L0_xattn_Wk, L0_xattn_Wv,
           L0_xattn_Wo, L0_ffn_W_q, L0_ffn_scales, L0_ffn_zeros, L0_ffn_mask, L0_ffn_scale2, L0_ffn_bias,
           L1_xattn_Wq, L1_xattn_bq, L1_xattn_Wk, L1_xattn_bk, L1_ffn_gate_w, L1_ffn_expert_w, L1_ffn_expert_b):
    import numpy as np
    import concourse.bacc as bacc
    from concourse.bass_utils import run_bass_kernel_spmd

    def chunked(w):
        w = np.asarray(w)
        return w.reshape(-1, P, w.shape[1]).transpose(1, 0, 2)

    inv = (1.0 / np.float32(10000.0) ** (np.arange(0, D, 2, dtype=np.float32) / np.float32(D))).astype(np.float32)
    angle = np.arange(MAX_POS, dtype=np.float32)[:, None] * inv[None, :]
    cos, sin = np.cos(angle), np.sin(angle)
    wq = np.asarray(L0_xattn_Wq).reshape(KC, P, KVH, GR * D)
    wo = np.asarray(L0_xattn_Wo).reshape(KVH, GR, D, E)
    layout = {
        "x": np.asarray(x).transpose(1, 0, 2),
        "ctxT": np.asarray(ctx_4096).reshape(T, KC, P).transpose(2, 1, 0),
        "ctx": np.asarray(ctx_4096).transpose(1, 0, 2),
        "pos": np.asarray(pos_BxS2).T,
        "mask": np.asarray(mask_BxSxS2_ik0).transpose(1, 0, 2),
        "gates": np.concatenate([np.asarray(g_xattn), np.asarray(g_ffn)]),
        "wq": wq.transpose(2, 1, 0, 3).reshape(KVH, P, KC * GR * D),
        "wo": wo.transpose(0, 2, 1, 3).reshape(KVH, P, GR * E),
        "wk": np.asarray(L0_xattn_Wk).reshape(KC, P, KVH, D).transpose(2, 1, 0, 3),
        "wv": np.asarray(L0_xattn_Wv).reshape(KC, P, KVH, D).transpose(2, 1, 0, 3),
        "wint": chunked(L0_ffn_W_q),
        "wmask": chunked(L0_ffn_mask),
        "scales": chunked(L0_ffn_scales),
        "zeros": chunked(L0_ffn_zeros),
        "scale2": np.asarray(L0_ffn_scale2).reshape(KC, P).T,
        "fbias": np.asarray(L0_ffn_bias),
        "wq1": chunked(np.asarray(L1_xattn_Wq).T),
        "wk1": chunked(np.asarray(L1_xattn_Wk).T),
        "b1": np.stack([np.asarray(L1_xattn_bk).reshape(KC, P).T, np.asarray(L1_xattn_bq).reshape(KC, P).T], axis=1),
        "gw": chunked(np.asarray(L1_ffn_gate_w).T),
        "ew": np.asarray(L1_ffn_expert_w).transpose(0, 2, 1).reshape(NX, KC, P, E).transpose(0, 2, 1, 3),
        "eb": np.asarray(L1_ffn_expert_b),
        "ident": np.eye(P, dtype=np.float32),
        "numbers": np.arange(NX, dtype=np.float32),
        "before": np.triu(np.ones((P, P), dtype=np.float32), 1),
        "pair_rows": np.arange(TOP * T, dtype=np.int32).reshape(TOP, NB, P).transpose(2, 0, 1),
        "rotary": np.concatenate([cos, cos, sin, -sin], axis=1).astype(np.float32),
    }
    nc = bacc.Bacc("TRN2", target_bir_lowering=False, num_devices=1, dynamic_dma_scratch_size=4096)
    arrays = {f"in_{k}": np.ascontiguousarray(v) for k, v in layout.items()}
    aps = {k: nc.dram_tensor(f"in_{k}", arrays[f"in_{k}"].shape, mybir.dt.from_np(arrays[f"in_{k}"].dtype),
                             kind="ExternalInput").ap() for k in layout}
    out = nc.dram_tensor("out", [P, NB, E], F32, kind="ExternalOutput").ap()
    program(nc, aps, out)
    r = run_bass_kernel_spmd(nc, [arrays], core_ids=[0])
    return np.asarray(r.results[0]["out"]).transpose(1, 0, 2).reshape(NB, S, E)
```

```python
import concourse.bass as bass
from concourse import mybir
from contextlib import ExitStack

F32 = mybir.dt.float32
F32R = mybir.dt.float32r
I32 = mybir.dt.int32
U32 = mybir.dt.uint32
I8 = mybir.dt.int8
ALU = mybir.AluOpType
ACT = mybir.ActivationFunctionType
AX = mybir.AxisListType

P = 128
NB = 8
S = 128
T = NB * S
E = 512
KC = E // P
H, KVH, D = 32, 8, 128
GR = H // KVH
MAX_POS = 512
NX = 32
TOP = 2
GROUP = 64
NG = E // GROUP
EPS = 1e-5
MASKED = -1e9


def wait(engine, semaphore, g, per, count):
    assert per + count > 0
    value = g * per + count
    if not (isinstance(g, int) and value <= 0):
        engine.wait_ge(semaphore, value)


def program(nc, a, out):
    root = ExitStack()
    with root:
        def sb(name, shape, dt=F32, ctx=root):
            return ctx.enter_context(nc.sbuf_tensor(name, shape, dt))

        def sem(name):
            return root.enter_context(nc.semaphore(name))

        x = sb("x", [P, NB, E])
        xT_hi = sb("xT_hi", [P, KC, T], F32R)
        xT_lo = sb("xT_lo", [P, KC, T], F32R)
        cT_hi = sb("cT_hi", [P, KC, T], F32R)
        cT_lo = sb("cT_lo", [P, KC, T], F32R)
        ident = sb("ident", [P, P])
        gates = sb("gates", [P, 4])
        stats = sb("stats", [P, NB, 6])
        meanvar = sb("meanvar", [P, NB, 2])
        spread = sb("spread", [P, NB])
        rstd = sb("rstd", [P, NB])
        psum = [root.enter_context(nc.psum_tensor(f"bank{i}", [P, 512], F32)) for i in range(8)]

        TILES = range(NB)
        HALVES = (range(0, NB // 2), range(NB // 2, NB))
        ln_stats, ln_aggr, ln_var, ln_std, ln_rstd = (sem(f"ln_{n}") for n in ("stats", "aggr", "var", "std", "rstd"))
        ln_norm, ln_turned, ln_hi, ln_lo = (sem(f"ln_{n}") for n in ("norm", "turned", "hi", "lo"))

        def tile_stats(t):
            nc.vector.bn_stats(stats[:, t, :], x[:, t, :]).then_inc(ln_stats, 1)

        def norm_stats(dve, n, group, tiles):
            for t in tiles:
                dve.wait_ge(ln_stats, n * NB + t + 1)
                nc.vector.bn_aggr(meanvar[:, t, :], stats[:, t, :]).then_inc(ln_aggr, 1)
            cols = slice(tiles[0], tiles[-1] + 1)
            dve.wait_ge(ln_aggr, n * NB + tiles[-1] + 1)
            nc.vector.tensor_scalar_add(spread[:, cols], meanvar[:, cols, 1], EPS).then_inc(ln_var, 1)
            dve.wait_ge(ln_std, group + 1)
            nc.vector.reciprocal(rstd[:, cols], spread[:, cols]).then_inc(ln_rstd, 1)
            dve.wait_ge(ln_rstd, group + 1)

        def norm_apply(dve, n, t, xn):
            if t >= xn.shape[1]:
                dve.wait_ge(ln_turned, n * NB + t - 1)
            nc.vector.tensor_scalar(xn[:, t % xn.shape[1], :], x[:, t, :], meanvar[:, t, 0:1], rstd[:, t:t + 1],
                                    ALU.subtract, ALU.mult).then_inc(ln_norm, 1)

        def norm_rest(dve, n, t):
            dve.wait_ge(ln_hi, n * NB + t + 1)
            tok = slice(t * P, (t + 1) * P)
            nc.vector.tensor_tensor(xT_lo[:, :, tok], psum[t % 2][:, :].rearrange("p (c t) -> p c t", c=KC),
                                    xT_hi[:, :, tok].bitcast(F32), ALU.subtract).then_inc(ln_lo, 1)

        def norm_sqrt(act, group, tiles):
            cols = slice(tiles[0], tiles[-1] + 1)
            act.wait_ge(ln_var, group + 1)
            nc.scalar.activation(spread[:, cols], spread[:, cols], ACT.Sqrt).then_inc(ln_std, 1)

        def norm_upper(act, n, t):
            act.wait_ge(ln_turned, n * NB + t + 1)
            nc.scalar.activation(xT_hi[:, :, t * P:(t + 1) * P],
                                 psum[t % 2][:, :].rearrange("p (c t) -> p c t", c=KC), ACT.Copy).then_inc(ln_hi, 1)

        def norm_turn(pe, n, t, xn):
            pe.wait_ge(ln_norm, n * NB + t + 1)
            if n * NB + t >= 2:
                pe.wait_ge(ln_lo, n * NB + t - 1)
            for c in range(KC):
                mm = nc.tensor.transpose(psum[t % 2][:, c * P:(c + 1) * P], xn[:, t % xn.shape[1], c * P:(c + 1) * P], ident[:, :])
            mm.then_inc(ln_turned, 1)

        def product(out_, hi, lo, r_hi, r_lo, start, stop):
            nc.tensor.matmul(out_, hi, r_hi, start=start, stop=False)
            nc.tensor.matmul(out_, hi, r_lo, start=False, stop=False)
            return nc.tensor.matmul(out_, lo, r_hi, start=False, stop=stop)

        loaded = sb("loaded", [P, KC, E])
        g_in = [sem(f"g_in_{n}") for n in ("wk", "wq")]
        phaseA = ExitStack()
        cosT = sb("cosT", [P, T], ctx=phaseA)
        sinT = sb("sinT", [P, T], ctx=phaseA)
        open_key = sb("open_key", [P, NB, S], I8, phaseA)
        key_scale = sb("key_scale", [P, 1], ctx=phaseA)
        filled = sb("filled", [P, NB, GR, S], ctx=phaseA)
        raw_big = sb("raw_big", [P, 4 * 512], ctx=phaseA)
        raw_k = sb("raw_k", [P, KC, D], ctx=phaseA)
        raw_v = sb("raw_v", [P, KC, D], ctx=phaseA)
        wq_hi, wq_lo = (sb(f"wq_{n}", [P, KC, GR * D], F32R, phaseA) for n in ("hi", "lo"))
        wk_hi, wk_lo = (sb(f"wk_{n}", [P, KC, D], F32R, phaseA) for n in ("hi", "lo"))
        wv_hi, wv_lo = (sb(f"wv_{n}", [P, KC, D], F32R, phaseA) for n in ("hi", "lo"))
        big_in, kv_in = sem("big_in"), sem("kv_in")
        wq_hi_s, wq_lo_s, wkv_hi_s, wkv_lo_s = (sem(n) for n in ("wq_hi_done", "wq_lo_done", "wkv_hi_done", "wkv_lo_done"))

        def queries_rest(pool, g, half):
            cols = slice(half * 2 * D, (half + 1) * 2 * D)
            wait(pool, wq_hi_s, g, 2, half + 1)
            nc.gpsimd.tensor_tensor(wq_lo[:, :, cols], raw_big[:, :].rearrange("p (c n) -> p c n", c=KC)[:, :, cols],
                                    wq_hi[:, :, cols].bitcast(F32), ALU.subtract).then_inc(wq_lo_s, 1)

        def keys_values_rest(pool, g):
            wait(pool, wkv_hi_s, g, 2, 2)
            nc.gpsimd.tensor_tensor(wk_lo[:, :, :], raw_k[:, :, :], wk_hi[:, :, :].bitcast(F32), ALU.subtract).then_inc(wkv_lo_s, 1)
            nc.gpsimd.tensor_tensor(wv_lo[:, :, :], raw_v[:, :, :], wv_hi[:, :, :].bitcast(F32), ALU.subtract).then_inc(wkv_lo_s, 1)

        def queries_upper(act, g, half):
            cols = slice(half * 2 * D, (half + 1) * 2 * D)
            if half == 0:
                wait(act, big_in, g, 32, 16)
            nc.scalar.activation(wq_hi[:, :, cols], raw_big[:, :].rearrange("p (c n) -> p c n", c=KC)[:, :, cols], ACT.Copy).then_inc(wq_hi_s, 1)

        def keys_values_upper(act, g):
            wait(act, kv_in, g, 32, 32)
            nc.scalar.activation(wk_hi[:, :, :], raw_k[:, :, :], ACT.Copy).then_inc(wkv_hi_s, 1)
            nc.scalar.activation(wv_hi[:, :, :], raw_v[:, :, :], ACT.Copy).then_inc(wkv_hi_s, 1)

        PAIR = 2 * S
        FIRST_ON_PE = (0, 1)
        proj_mm = sem("proj_mm")

        def project_queries(j, bank, tok):
            for k in range(2):
                cols = slice((2 * j + k) * D, (2 * j + k + 1) * D)
                for c in range(KC):
                    mm = product(bank[:, k * PAIR:(k + 1) * PAIR], wq_hi[:, c, cols], wq_lo[:, c, cols],
                                 xT_hi[:, c, tok], xT_lo[:, c, tok], c == 0, c == KC - 1)
            return mm

        with ExitStack() as ctx:
            xn = sb("xn0", [P, 2, E], ctx=ctx)
            ctx_raw = sb("ctx_raw", [P, KC, T], ctx=ctx)
            mask_raw = sb("mask_raw", [P, NB, S], I32, ctx)
            pos_raw = sb("pos_raw", [P, NB], I32, ctx)
            pos_neg = sb("pos_neg", [P, NB], ctx=ctx)
            pos_wrapped = sb("pos_wrapped", [P, NB], ctx=ctx)
            pos_row = sb("pos_row", [P, NB], U32, ctx)
            rotary = sb("rotary", [P, NB, 2 * D], ctx=ctx)
            gates_raw = sb("gates_raw", [P, 4], ctx=ctx)
            in_small, in_pos, in_mask = (sem(f"in_{n}") for n in ("small", "pos", "mask"))
            in_x, in_ctx = ([sem(f"in_{n}{half}") for half in range(2)] for n in ("x", "ctx"))
            in_rot = sem("in_rot")
            pos_step, rot_turned, ctx_hi = (sem(n) for n in ("pos_step", "rot_turned", "ctx_hi"))
            with nc.Block() as block:
                @block.sync
                def _(sp):
                    sp.dma_start(pos_raw[:, :], a["pos"]).then_inc(in_pos, 16)
                    sp.dma_start(gates_raw[:, :], a["gates"].partition_broadcast(P)).then_inc(in_small, 16)
                    for n, tiles in enumerate(HALVES):
                        sp.dma_start(x[:, tiles[0]:tiles[-1] + 1, :], a["x"][:, tiles[0]:tiles[-1] + 1, :]).then_inc(in_x[n], 16)
                        if n == 0:
                            sp.dma_start(ident[:, :], a["ident"]).then_inc(in_small, 16)
                    sp.dma_start(raw_k[:, :, :], a["wk"][0]).then_inc(kv_in, 16)
                    sp.dma_start(raw_v[:, :, :], a["wv"][0]).then_inc(kv_in, 16)
                    sp.dma_start(raw_big[:, :], a["wq"][0]).then_inc(big_in, 16)
                    for n in range(2):
                        sp.dma_start(ctx_raw[:, 2 * n:2 * n + 2, :], a["ctxT"][:, 2 * n:2 * n + 2, :]).then_inc(in_ctx[n], 16)
                    sp.dma_start(mask_raw[:, :, :], a["mask"]).then_inc(in_mask, 16)
                    sp.dma_start(loaded[:, :, :], a["wk1"]).then_inc(g_in[0], 16)
                    sp.wait_ge(wq_lo_s, 2)
                    sp.dma_start(raw_big[:, :], a["wo"][0]).then_inc(big_in, 16)

                @block.gpsimd
                def _(pool):
                    nc.gpsimd.memset(filled[:, :, :, :], MASKED)
                    nc.gpsimd.memset(key_scale[:, :], float(D) ** -0.5)
                    pool.wait_ge(pos_step, 3)
                    for t in TILES:
                        pool.indirect_dma_start(
                            out=rotary[:, t, :], out_offset=None, in_=a["rotary"],
                            in_offset=bass.IndirectOffsetOnAxis(ap=pos_row[:, t:t + 1], axis=0)).then_inc(in_rot, 16)
                    keys_values_rest(pool, 0)
                    queries_rest(pool, 0, 0)
                    queries_rest(pool, 0, 1)
                    for c in (1, 3):
                        pool.wait_ge(ctx_hi, c + 1)
                        nc.gpsimd.tensor_tensor(cT_lo[:, c, :], ctx_raw[:, c, :], cT_hi[:, c, :].bitcast(F32),
                                                ALU.subtract)

                @block.scalar
                def _(act):
                    def keep_cos(n):
                        act.wait_ge(rot_turned, n + 1)
                        nc.scalar.activation(cosT[:, 4 * n * P:4 * (n + 1) * P], psum[2 + n][:, :], ACT.Copy)

                    act.wait_ge(in_small, 32)
                    nc.scalar.activation(gates[:, :], gates_raw[:, :], ACT.Tanh)
                    norm_sqrt(act, 0, HALVES[0])
                    norm_upper(act, 0, 0)
                    norm_upper(act, 0, 1)
                    keys_values_upper(act, 0)
                    norm_upper(act, 0, 2)
                    norm_upper(act, 0, 3)
                    norm_sqrt(act, 1, HALVES[1])
                    queries_upper(act, 0, 0)
                    queries_upper(act, 0, 1)
                    for t in HALVES[1]:
                        norm_upper(act, 0, t)
                    for c in range(KC):
                        act.wait_ge(in_ctx[c // 2], 16)
                        nc.scalar.activation(cT_hi[:, c, :], ctx_raw[:, c, :], ACT.Copy).then_inc(ctx_hi, 1)
                    keep_cos(0)
                    keep_cos(1)

                @block.vector
                def _(dve):
                    dve.wait_ge(in_pos, 16)
                    nc.vector.tensor_scalar(pos_neg[:, :], pos_raw[:, :], 0.0, float(MAX_POS), ALU.is_lt, ALU.mult).then_inc(pos_step, 1)
                    dve.wait_ge(pos_step, 1)
                    nc.vector.tensor_tensor(pos_wrapped[:, :], pos_raw[:, :], pos_neg[:, :], ALU.add).then_inc(pos_step, 1)
                    dve.wait_ge(pos_step, 2)
                    nc.vector.tensor_scalar(pos_row[:, :], pos_wrapped[:, :], 0.0, float(MAX_POS - 1), ALU.max, ALU.min).then_inc(pos_step, 1)
                    for n, tiles in enumerate(HALVES):
                        dve.wait_ge(in_x[n], 16)
                        for t in tiles:
                            tile_stats(t)
                        norm_stats(dve, 0, n, tiles)
                        for t in tiles:
                            norm_apply(dve, 0, t, xn)
                            if t > tiles[0]:
                                norm_rest(dve, 0, t - 1)
                        norm_rest(dve, 0, tiles[-1])
                    for c in (0, 2):
                        dve.wait_ge(ctx_hi, c + 1)
                        nc.vector.tensor_tensor(cT_lo[:, c, :], ctx_raw[:, c, :], cT_hi[:, c, :].bitcast(F32),
                                                ALU.subtract)
                    for n in range(2):
                        dve.wait_ge(rot_turned, n + 1)
                        nc.vector.tensor_copy(sinT[:, 4 * n * P:4 * (n + 1) * P], psum[4 + n][:, :])
                    dve.wait_ge(in_mask, 16)
                    nc.vector.tensor_scalar(open_key[:, :, :], mask_raw[:, :, :], 0.0, None, ALU.not_equal)

                @block.tensor
                def _(pe):
                    pe.wait_ge(in_small, 32)
                    for t in TILES:
                        norm_turn(pe, 0, t, xn)
                    pe.wait_ge(in_rot, 16 * NB)
                    for n, tiles in enumerate(HALVES):
                        for t in tiles:
                            for k in range(2):
                                mm = nc.tensor.transpose(psum[2 + 2 * k + n][:, (t - 4 * n) * P:(t - 4 * n + 1) * P],
                                                         rotary[:, t, k * D:(k + 1) * D], ident[:, :])
                        mm.then_inc(rot_turned, 1)
                    pe.wait_ge(ln_lo, NB)
                    for item in FIRST_ON_PE:
                        pe.wait_ge(wq_lo_s, item + 1)
                        project_queries(item % 2, psum[item], slice(0, PAIR)).then_inc(proj_mm, 1)

        with phaseA as ctx:
            HALF = T // 2
            wo_hi, wo_lo = (sb(f"wo_{n}", [P, GR, E], F32R, ctx) for n in ("hi", "lo"))
            kT = sb("kT", [P, T], ctx=ctx)
            vT = sb("vT", [P, T], ctx=ctx)
            v_hi, v_lo = (sb(f"v_{n}", [P, NB, D], F32R, ctx) for n in ("hi", "lo"))
            qT = sb("qT", [P, 2, GR, PAIR], ctx=ctx)
            straight = sb("straight", [P, 2, 512], ctx=ctx)
            turned = sb("turned", [P, 2, 512], ctx=ctx)
            probs = sb("probs", [P, 2, GR, S], ctx=ctx)
            pT_hi, pT_lo = (sb(f"pT_{n}", [P, 2, GR * S], F32R, ctx) for n in ("hi", "lo"))
            oT_hi, oT_lo = (sb(f"oT_{n}", [P, 2, GR, S], F32R, ctx) for n in ("hi", "lo"))
            negmax = sb("negmax", [P, NB, GR], ctx=ctx)
            gatepost = sb("gatepost", [P, 1], ctx=ctx)
            total = sb("total", [P, NB, GR], ctx=ctx)
            invtotal = sb("invtotal", [P, NB, GR], ctx=ctx)

            bank_rope = psum[0:2]
            bank_scores = psum[2:4]
            bank_pT, bank_o, bank_y, bank_v = psum[4:8]

            wo_hi_s, wo_lo_s = sem("wo_hi_done"), sem("wo_lo_done")
            rope_mul, rope_add, rope_sum = (sem(n) for n in ("rope_mul", "rope_add", "rope_sum"))
            v_mm, v_kept, v_turned, v_hi_s, v_lo_s = (sem(n) for n in ("v_mm", "v_kept", "v_turned", "v_hi_done", "v_lo_done"))
            score_mm, score_kept, score_max, exp_done, inv_done, probs_done = (
                sem(n) for n in ("score_mm", "score_kept", "score_max", "exp_done", "inv_done", "probs_done"))
            pT_mm, pT_hi_s, pT_lo_s = sem("pT_mm"), sem("pT_hi_done"), sem("pT_lo_done")
            o_mm, o_hi_s, o_lo_s = sem("o_mm"), sem("o_hi_done"), sem("o_lo_done")
            y_mm, y_added = sem("y_mm"), sem("y_added")

            ITEMS, UNITS = 10, NB
            ITEMS_OF_STEP = [[5], [6], [7], [8], [9], [10], [11], [12, 13, 14]]
            FIRST_ITEMS = [0, 1, 2, 3, 4]

            def steps(g):
                whole = not isinstance(g, int)
                for step in range(3 if not whole and g == KVH else UNITS):
                    def unit(u):
                        if not whole and (g * UNITS + u < 0 or g * UNITS + u >= KVH * UNITS):
                            return None
                        return u
                    items = [] if not whole and g == KVH else ITEMS_OF_STEP[step]
                    if not whole and g == KVH - 1:
                        items = [i for i in items if i < ITEMS]
                    yield step, unit(step), items, unit(step - 1), unit(step - 2), unit(step - 3)

            def more(g):
                return not isinstance(g, int) or g < KVH - 1

            def place_of(item):
                i = item % ITEMS
                if i in (2, 3):
                    tok = slice((i - 2) * HALF, (i - 1) * HALF)
                    return kT[:, tok], tok, True
                pair, j = (0, i) if i < 2 else ((i - 2) // 2, i % 2)
                return qT[:, pair % 2, 2 * j:2 * j + 2, :], slice(pair * PAIR, (pair + 1) * PAIR), False

            def shaped(ap, key):
                return ap if key else ap.rearrange("p (h t) -> p h t", h=2)

            def spread_over(table, key):
                return table if key else table.unsqueeze(1).broadcast_to([table.shape[0], 2, PAIR])

            with nc.Block() as block:
                @block.sync
                def _(sp):
                    def load_out(g):
                        sp.wait_ge(wq_lo_s, 2 * g + 2)
                        sp.dma_start(raw_big[:, :], a["wo"][bass.ds(g, 1)].rearrange("o p n -> p (o n)")).then_inc(big_in, 16)

                    with sp.Fori(1, KVH) as g:
                        sp.wait_ge(wkv_lo_s, 2 * g)
                        sp.dma_start(raw_k[:, :, :], a["wk"][bass.ds(g, 1)].rearrange("o p c n -> p (o c) n")).then_inc(kv_in, 16)
                        sp.dma_start(raw_v[:, :, :], a["wv"][bass.ds(g, 1)].rearrange("o p c n -> p (o c) n")).then_inc(kv_in, 16)
                        sp.wait_ge(wo_lo_s, GR * g)
                        sp.dma_start(raw_big[:, :], a["wq"][bass.ds(g, 1)].rearrange("o p n -> p (o n)")).then_inc(big_in, 16)
                        load_out(g)

                @block.gpsimd
                def _(pool):
                    def out_weights(g):
                        for h in range(GR):
                            wait(pool, wo_hi_s, g, GR, h + 1)
                            nc.gpsimd.tensor_tensor(wo_lo[:, h, :], raw_big[:, h * E:(h + 1) * E],
                                                    wo_hi[:, h, :].bitcast(F32), ALU.subtract).then_inc(wo_lo_s, 1)

                    def item_sum(g, item):
                        k = item % 2
                        dst, _, key = place_of(item)
                        wait(pool, rope_mul, g, ITEMS, item + 1)
                        if key:
                            nc.gpsimd.tensor_tensor(straight[:, k, :], straight[:, k, :], turned[:, k, :], ALU.add).then_inc(rope_add, 1)
                            wait(pool, rope_add, g, 2, item % ITEMS - 1 + (2 if item >= ITEMS else 0))
                            nc.gpsimd.tensor_tensor(dst, straight[:, k, :], key_scale[:, :].broadcast_to([P, 512]), ALU.mult).then_inc(rope_sum, 1)
                        else:
                            nc.gpsimd.tensor_tensor(dst, shaped(straight[:, k, :], key), shaped(turned[:, k, :], key), ALU.add).then_inc(rope_sum, 1)

                    def normalise(g, u):
                        wait(pool, inv_done, g, UNITS, u + 1)
                        nc.gpsimd.tensor_tensor(probs[:, u % 2, :, :], probs[:, u % 2, :, :],
                                                invtotal[:, u % UNITS, :].unsqueeze(2).broadcast_to([P, GR, S]), ALU.mult).then_inc(probs_done, 1)

                    def group(g):
                        for step, u, items, _, _, _ in steps(g):
                            if step == 4 and more(g):
                                queries_rest(pool, g + 1, 0)
                            if step == 5 and more(g):
                                queries_rest(pool, g + 1, 1)
                            if u is not None and not items:
                                normalise(g, u)
                            for item in items:
                                item_sum(g, item)
                                if item == items[0]:
                                    normalise(g, u)
                            if step == 2 and u is not None:
                                out_weights(g)
                            if step == 3 and more(g):
                                keys_values_rest(pool, g + 1)

                    for item in FIRST_ITEMS:
                        item_sum(0, item)
                    group(0)
                    with pool.Fori(1, KVH - 1) as g:
                        group(g)
                    group(KVH - 1)
                    group(KVH)

                @block.scalar
                def _(act):
                    def out_weights(g):
                        wait(act, big_in, g, 32, 32)
                        wait(act, y_mm, g, UNITS, 0)
                        for h in range(GR):
                            nc.scalar.activation(wo_hi[:, h, :], raw_big[:, h * E:(h + 1) * E], ACT.Copy).then_inc(wo_hi_s, 1)

                    def exps(g, u):
                        wait(act, score_max, g, UNITS, u + 1)
                        wait(act, pT_mm, g, UNITS, u - 1)
                        for h in range(GR):
                            ex = nc.scalar.activation(probs[:, u % 2, h, :], filled[:, u % UNITS, h, :], ACT.Exp,
                                                      bias=negmax[:, u % UNITS, h:h + 1], accum_out=total[:, u % UNITS, h:h + 1])
                        ex.then_inc(exp_done, 1)

                    def probs_upper(g, u):
                        wait(act, pT_mm, g, UNITS, u + 1)
                        wait(act, o_mm, g, UNITS, u - 1)
                        nc.scalar.activation(pT_hi[:, u % 2, :], bank_pT[:, :], ACT.Copy).then_inc(pT_hi_s, 1)

                    def out_upper(g, u):
                        wait(act, o_mm, g, UNITS, u + 1)
                        wait(act, y_mm, g, UNITS, u - 1)
                        nc.scalar.activation(oT_hi[:, u % 2, :, :], bank_o[:, :].rearrange("p (h t) -> p h t", h=GR), ACT.Copy).then_inc(o_hi_s, 1)

                    def keep_values(g, half):
                        wait(act, v_mm, g, 2, half + 1)
                        nc.scalar.activation(vT[:, half * HALF:(half + 1) * HALF], bank_v[:, :], ACT.Copy).then_inc(v_kept, 1)

                    def values_upper(g):
                        for half in range(2):
                            wait(act, v_turned, g, 2, half + 1)
                            nc.scalar.activation(v_hi[:, 4 * half:4 * half + 4, :], bank_v[:, :].rearrange("p (b d) -> p b d", b=4),
                                                 ACT.Copy).then_inc(v_hi_s, 1)

                    def group(g):
                        for step, u, items, turn, attend, _ in steps(g):
                            if step == 4 and more(g):
                                wait(act, proj_mm, g, ITEMS, 9)
                                queries_upper(act, g + 1, 0)
                            if step == 5 and more(g):
                                wait(act, proj_mm, g, ITEMS, 10)
                                queries_upper(act, g + 1, 1)
                            if u is not None:
                                exps(g, u)
                            if step < 2 and u is not None:
                                keep_values(g, step)
                            if attend is not None:
                                out_upper(g, attend)
                            if step == 1 and u is not None:
                                values_upper(g)
                            if turn is not None:
                                probs_upper(g, turn)
                            if step == 2 and u is not None:
                                out_weights(g)
                            if step == 3 and more(g):
                                wait(act, v_mm, g, 2, 2)
                                keys_values_upper(act, g + 1)

                    group(0)
                    with act.Fori(1, KVH - 1) as g:
                        group(g)
                    group(KVH - 1)
                    group(KVH)

                @block.vector
                def _(dve):
                    def item_products(g, item):
                        _, tok, key = place_of(item)
                        k = item % 2
                        wait(dve, proj_mm, g, ITEMS, item + 1)
                        wait(dve, rope_sum, g, ITEMS, item - 1)
                        bank = bank_rope[k]
                        nc.vector.tensor_tensor(shaped(straight[:, k, :], key), shaped(bank[:, :], key),
                                                spread_over(cosT[:, tok], key), ALU.mult)
                        for src, dst in ((slice(0, 64), slice(64, 128)), (slice(64, 128), slice(0, 64))):
                            last = nc.vector.tensor_tensor(shaped(turned[dst, k, :], key), shaped(bank[src, :], key),
                                                           spread_over(sinT[src, tok], key), ALU.mult)
                        last.then_inc(rope_mul, 1)

                    def keep_scores(g, u):
                        wait(dve, exp_done, g, UNITS, u - UNITS + 1)
                        wait(dve, score_mm, g, UNITS, u + 1)
                        nc.vector.memset(gatepost[:, :], 0.0)
                        for h in range(GR):
                            kept = nc.vector.copy_predicated(filled[:, u, h, :], open_key[:, u, :], bank_scores[u % 2][:, h * S:(h + 1) * S])
                        kept.then_inc(score_kept, 1)
                        wait(dve, score_kept, g, UNITS, u + 1)
                        nc.vector.tensor_reduce(negmax[:, u, :], filled[:, u, :, :], AX.X, ALU.max, negate=True).then_inc(score_max, 1)

                    def invert(g, u):
                        wait(dve, exp_done, g, UNITS, u + 1)
                        nc.vector.reciprocal(invtotal[:, u, :], total[:, u, :]).then_inc(inv_done, 1)

                    def probs_rest(g, u):
                        wait(dve, pT_hi_s, g, UNITS, u + 1)
                        nc.vector.tensor_tensor(pT_lo[:, u % 2, :], bank_pT[:, :], pT_hi[:, u % 2, :].bitcast(F32), ALU.subtract).then_inc(pT_lo_s, 1)

                    def out_rest(g, u):
                        wait(dve, o_hi_s, g, UNITS, u + 1)
                        nc.vector.tensor_tensor(oT_lo[:, u % 2, :, :], bank_o[:, :].rearrange("p (h t) -> p h t", h=GR),
                                                oT_hi[:, u % 2, :, :].bitcast(F32), ALU.subtract).then_inc(o_lo_s, 1)

                    def add_out(g, u):
                        wait(dve, y_mm, g, UNITS, u + 1)
                        nc.vector.scalar_tensor_tensor(x[:, u % UNITS, :], bank_y[:, :], gates[:, 0:1], x[:, u % UNITS, :], ALU.mult, ALU.add).then_inc(y_added, 1)

                    def values_rest(g):
                        for half in range(2):
                            wait(dve, v_hi_s, g, 2, half + 1)
                            rows = slice(4 * half, 4 * half + 4)
                            nc.vector.tensor_tensor(v_lo[:, rows, :], bank_v[:, :].rearrange("p (b d) -> p b d", b=4),
                                                    v_hi[:, rows, :].bitcast(F32), ALU.subtract).then_inc(v_lo_s, 1)

                    def group(g):
                        for step, u, items, turn, attend, out_unit in steps(g):
                            if u is not None:
                                keep_scores(g, u)
                            for item in items[:1]:
                                item_products(g, item)
                            if u is not None:
                                invert(g, u)
                            for item in items[1:]:
                                item_products(g, item)
                            if attend is not None and items:
                                out_rest(g, attend)
                            if step == 1 and u is not None:
                                values_rest(g)
                            if out_unit is not None:
                                add_out(g, out_unit)
                            if attend is not None and not items:
                                out_rest(g, attend)
                            if turn is not None:
                                probs_rest(g, turn)

                    for item in FIRST_ITEMS:
                        item_products(0, item)
                    group(0)
                    with dve.Fori(1, KVH - 1) as g:
                        group(g)
                    group(KVH - 1)
                    group(KVH)

                @block.tensor
                def _(pe):
                    def project(g, item):
                        _, tok, key = place_of(item)
                        own = item % ITEMS
                        ahead = 1 if item >= ITEMS else 0
                        j = own % 2
                        if key:
                            wait(pe, wkv_lo_s, g, 2, 2 * ahead + 2)
                        else:
                            wait(pe, wq_lo_s, g, 2, 2 * ahead + j + 1)
                        wait(pe, rope_mul, g, ITEMS, item - 1)
                        bank = bank_rope[item % 2]
                        if key:
                            for c in range(KC):
                                mm = product(bank[:, :], wk_hi[:, c, :], wk_lo[:, c, :], cT_hi[:, c, tok], cT_lo[:, c, tok], c == 0, c == KC - 1)
                        else:
                            mm = project_queries(j, bank, tok)
                        mm.then_inc(proj_mm, 1)

                    def make_values(g, half):
                        wait(pe, wkv_lo_s, g, 2, 2)
                        if half == 0:
                            wait(pe, v_lo_s, g, 2, 0)
                        else:
                            wait(pe, v_kept, g, 2, 1)
                        tok = slice(half * HALF, (half + 1) * HALF)
                        for c in range(KC):
                            mm = product(bank_v[:, :], wv_hi[:, c, :], wv_lo[:, c, :], cT_hi[:, c, tok], cT_lo[:, c, tok], c == 0, c == KC - 1)
                        mm.then_inc(v_mm, 1)

                    def turn_values(g, half):
                        if half == 0:
                            wait(pe, v_kept, g, 2, 2)
                        else:
                            wait(pe, v_lo_s, g, 2, 1)
                        for b in range(4):
                            mm = nc.tensor.transpose(bank_v[:, b * D:(b + 1) * D], vT[:, (4 * half + b) * S:(4 * half + b + 1) * S], ident[:, :])
                        mm.then_inc(v_turned, 1)

                    def score(g, u):
                        if u % 2 == 0:
                            wait(pe, rope_sum, g, ITEMS, 4 + u if u else 3)
                        wait(pe, score_kept, g, UNITS, u - 1)
                        keys = slice(u * S, (u + 1) * S)
                        q = slice((u % 2) * S, (u % 2 + 1) * S)
                        for h in range(GR):
                            mm = nc.tensor.matmul(bank_scores[u % 2][:, h * S:(h + 1) * S], qT[:, (u // 2) % 2, h, q], kT[:, keys], start=True, stop=True)
                        mm.then_inc(score_mm, 1)

                    def turn_probs(g, u):
                        wait(pe, probs_done, g, UNITS, u + 1)
                        wait(pe, pT_lo_s, g, UNITS, u)
                        for h in range(GR):
                            mm = nc.tensor.transpose(bank_pT[:, h * S:(h + 1) * S], probs[:, u % 2, h, :], ident[:, :])
                        mm.then_inc(pT_mm, 1)

                    def attend(g, u):
                        if u == 0:
                            wait(pe, v_lo_s, g, 2, 2)
                        wait(pe, pT_lo_s, g, UNITS, u + 1)
                        wait(pe, o_lo_s, g, UNITS, u)
                        product(bank_o[:, :], v_hi[:, u % UNITS, :], v_lo[:, u % UNITS, :], pT_hi[:, u % 2, :], pT_lo[:, u % 2, :], True, True).then_inc(o_mm, 1)

                    def project_out(g, u):
                        wait(pe, o_lo_s, g, UNITS, u + 1)
                        wait(pe, y_added, g, UNITS, u)
                        for h in range(GR):
                            if u == 0:
                                wait(pe, wo_lo_s, g, GR, h + 1)
                            mm = product(bank_y[:, :], oT_hi[:, u % 2, h, :], oT_lo[:, u % 2, h, :], wo_hi[:, h, :], wo_lo[:, h, :], h == 0, h == GR - 1)
                        mm.then_inc(y_mm, 1)

                    def group(g):
                        for step, u, items, turn, att, out_unit in steps(g):
                            if u is not None:
                                score(g, u)
                            for item in items:
                                project(g, item)
                            if step < 2 and u is not None:
                                make_values(g, step)
                            if att is not None and items:
                                attend(g, att)
                            if step == 1 and u is not None:
                                turn_values(g, 0)
                            if out_unit is not None:
                                project_out(g, out_unit)
                            if att is not None and not items:
                                attend(g, att)
                            if step == 1 and u is not None:
                                turn_values(g, 1)
                            if turn is not None:
                                turn_probs(g, turn)

                    for item in FIRST_ITEMS:
                        if item not in FIRST_ON_PE:
                            project(0, item)
                    group(0)
                    with pe.Fori(1, KVH - 1) as g:
                        group(g)
                    group(KVH - 1)
                    group(KVH)

        words = sb("words", [P, 2, KC, E], I32)
        last_xn = words[:, :, :, :].bitcast(F32).rearrange("p a c n -> p (a c) n")
        logitsT = sb("logitsT", [NX, T])
        logits = sb("logits", [P, NB, NX])
        best = sb("best", [P, NB, 8])
        best_at = sb("best_at", [P, NB, 8], U32)
        m_best = sem("m_best")
        EARLY = 2
        RING = 8
        early_w = sb("early_w", [P, EARLY, KC, E])
        w_in = [sem(f"w_in{k}") for k in range(RING)]
        numbers = sb("numbers", [P, P])
        pair_codes = sb("pair_codes", [P, TOP, NB])
        m_in = sem("m_in")
        xn_rows = nc.dram_tensor("xn_rows", [T, E], F32, kind="Internal").ap()
        rows_out = sem("rows_out")
        with ExitStack() as ctx:
            xn = sb("xn1", [P, 2, E], ctx=ctx)
            wint, wmask = words[:, 0, :, :], words[:, 1, :, :]
            scales = sb("scales", [P, KC, NG], ctx=ctx)
            zeros = sb("zeros", [P, KC, NG], ctx=ctx)
            scale2 = sb("scale2", [P, KC], ctx=ctx)
            weight = sb("weight", [P, KC, E], ctx=ctx)
            wT_hi, wT_lo = (sb(f"wT_{n}", [P, KC, E], F32R, ctx) for n in ("hi", "lo"))
            bias = sb("bias", [P, E], ctx=ctx)
            summed = sb("summed", [P, 2, E], ctx=ctx)
            w_hi, w_lo = (sb(f"l1_w_{n}", [P, KC, E], F32R, ctx) for n in ("hi", "lo"))
            b1 = sb("l1_bias", [P, 2, KC], ctx=ctx)
            c_raw = sb("l1_ctx", [P, NB, E], ctx=ctx)
            k1 = sb("l1_k", [P, KC, T], ctx=ctx)
            q1 = weight
            l1p = sb("l1_probs", [P, 4, S], ctx=ctx)
            l1pT = sb("l1_pT", [P, 4 * S], ctx=ctx)
            l1max, l1nb, l1sum, l1inv = (sb(f"l1_{n}", [P, 4], ctx=ctx) for n in ("max", "nb", "sum", "inv"))
            l1scale = sb("l1_scale", [P, 4], ctx=ctx)
            gw = sb("gw", [P, KC, NX], ctx=ctx)
            gw_hi, gw_lo = (sb(f"gw_{n}", [P, KC, NX], F32R, ctx) for n in ("hi", "lo"))
            SC1 = float(E) ** -0.5
            f_words, f_small, f_float, f_deq, f_turned, f_hi, f_lo, f_mm, f_sum, f_added = (
                sem(f"f_{n}") for n in ("words", "small", "float", "deq", "turned", "hi", "lo", "mm", "sum", "added"))
            g_bias, g_ctx, g_gate = (sem(f"g_in_{n}") for n in ("bias", "ctx", "gate"))
            (g_whi, g_wlo, g_mm, g_kept, g_smm, g_max, g_nb, g_exp, g_inv, g_turned, g_pkept, g_omm, g_added) = (
                sem(f"g_{n}") for n in ("whi", "wlo", "mm", "kept", "smm", "max", "nb", "exp", "inv", "turned",
                                        "pkept", "omm", "added"))
            m_ghi, m_glo, m_log, m_logk, m_lturn, m_lkept = (sem(f"m_{n}") for n in ("ghi", "glo", "log", "logk", "lturn", "lkept"))

            def item(i):
                return (0, i // 2, i % 2) if i < 2 * KC else (1, i % KC, i // KC - 2)

            def columns(c):
                return slice(c * P, (c + 1) * P)

            def half_of(n):
                return slice(n * (T // 2), (n + 1) * (T // 2))

            with nc.Block() as block:
                @block.sync
                def _(sp):
                    sp.dma_start(words[:, 0, :, :], a["wint"]).then_inc(f_words, 16)
                    for dst, src in ((scales, "scales"), (zeros, "zeros"), (scale2, "scale2")):
                        sp.dma_start(dst[:], a[src]).then_inc(f_small, 16)
                    sp.dma_start(b1[:, :, :], a["b1"]).then_inc(g_bias, 16)
                    sp.wait_ge(f_words, 16)
                    sp.dma_start(words[:, 1, :, :], a["wmask"]).then_inc(f_words, 16)
                    sp.dma_start(bias[:, :], a["fbias"].partition_broadcast(P)).then_inc(f_small, 16)
                    sp.dma_start(gw[:, :, :], a["gw"]).then_inc(g_gate, 16)
                    sp.dma_start(c_raw[:, :, :], a["ctx"]).then_inc(g_ctx, 16)
                    sp.dma_start(numbers[:, :], a["numbers"].partition_broadcast(P)).then_inc(m_in, 16)
                    sp.dma_start(pair_codes[:, :, :], a["pair_codes"]).then_inc(m_in, 16)
                    for k in range(EARLY):
                        sp.dma_start(early_w[:, k, :, :], a["ew"][k]).then_inc(w_in[k], 16)
                    sp.wait_ge(f_deq, 4)
                    sp.dma_start(loaded[:, :, :], a["wq1"]).then_inc(g_in[1], 16)
                    for n in range(2):
                        sp.wait_ge(ln_norm, 3 * NB + 4 * (n + 1))
                        sp.dma_start(xn_rows.rearrange("(t p) e -> p t e", p=P)[:, 4 * n:4 * n + 4, :],
                                     last_xn[:, 4 * n:4 * n + 4, :]).then_inc(rows_out, 16)

                @block.gpsimd
                def _(pool):
                    def weights_rest(w):
                        for c in range(KC):
                            pool.wait_ge(g_whi, KC * w + c + 1)
                            nc.gpsimd.tensor_tensor(w_lo[:, :, columns(c)], loaded[:, :, columns(c)],
                                                    w_hi[:, :, columns(c)].bitcast(F32), ALU.subtract).then_inc(g_wlo, 1)

                    weights_rest(0)
                    pool.wait_ge(f_small, 16 * 4)
                    pool.wait_ge(f_float, 1)
                    shape = [P, KC * NG, GROUP]
                    wide = weight[:, :, :].rearrange("p c (g n) -> p (c g) n", g=NG)
                    nc.gpsimd.tensor_tensor(wide, wide,
                                            zeros[:, :, :].rearrange("p c g -> p (c g)").unsqueeze(2).broadcast_to(shape), ALU.subtract).then_inc(f_deq, 1)
                    pool.wait_ge(f_deq, 1)
                    nc.gpsimd.tensor_tensor(wide, wide, scales[:, :, :].rearrange("p c g -> p (c g)").unsqueeze(2).broadcast_to(shape), ALU.mult).then_inc(f_deq, 1)
                    pool.wait_ge(f_deq, 2)
                    nc.gpsimd.tensor_tensor(weight[:, :, :], weight[:, :, :], scale2[:, :].unsqueeze(2).broadcast_to([P, KC, E]), ALU.mult).then_inc(f_deq, 1)
                    pool.wait_ge(f_deq, 3)
                    pool.wait_ge(f_float, 2)
                    nc.gpsimd.tensor_tensor(weight[:, :, :], weight[:, :, :], loaded[:, :, :], ALU.mult).then_inc(f_deq, 1)
                    weights_rest(1)
                    pool.wait_ge(m_ghi, 1)
                    nc.gpsimd.tensor_tensor(gw_lo[:, :, :], gw[:, :, :], gw_hi[:, :, :].bitcast(F32), ALU.subtract).then_inc(m_glo, 1)

                @block.scalar
                def _(act):
                    def weights_upper(w):
                        act.wait_ge(g_in[w], 16)
                        if w:
                            act.wait_ge(g_mm, 2 * KC)
                        for c in range(KC):
                            nc.scalar.activation(w_hi[:, :, columns(c)], loaded[:, :, columns(c)], ACT.Copy).then_inc(g_whi, 1)

                    def keep(i):
                        w, c, half = item(i)
                        act.wait_ge(g_mm, i + 1)
                        if i == 3 * KC:
                            act.wait_ge(g_smm, 1)
                        dst = q1[:, c, :] if w else k1[:, c, half_of(half)]
                        nc.scalar.activation(dst, psum[2 + i % 2][:, :], ACT.Identity, bias=b1[:, w, c:c + 1]).then_inc(g_kept, 1)

                    def exps(n):
                        act.wait_ge(g_nb, n + 1)
                        for b in range(4):
                            ex = nc.scalar.activation(l1p[:, b, :], psum[4][:, b * S:(b + 1) * S], ACT.Exp, scale=SC1,
                                                      bias=l1nb[:, b:b + 1], accum_out=l1sum[:, b:b + 1])
                        ex.then_inc(g_exp, 1)

                    def probs_kept(n):
                        act.wait_ge(g_turned, n + 1)
                        nc.scalar.activation(l1pT[:, :], psum[5][:, :], ACT.Copy).then_inc(g_pkept, 1)

                    def logits_kept(n):
                        act.wait_ge(m_log, n + 1)
                        nc.scalar.activation(logitsT[:, half_of(n)], psum[5][0:NX, :], ACT.Copy).then_inc(m_logk, 1)
                        act.wait_ge(m_lturn, n + 1)
                        nc.scalar.activation(logits[:, 4 * n:4 * n + 4, :], psum[2 + n][:, 0:4 * NX].rearrange("p (t e) -> p t e", t=4),
                                             ACT.Copy).then_inc(m_lkept, 1)

                    weights_upper(0)
                    act.wait_ge(g_bias, 16)
                    keep(0)
                    act.wait_ge(f_words, 16)
                    nc.scalar.activation(weight[:, :, :], wint, ACT.Copy).then_inc(f_float, 1)
                    norm_sqrt(act, 2, TILES)
                    keep(1)
                    act.wait_ge(f_words, 32)
                    act.wait_ge(g_wlo, KC)
                    nc.scalar.activation(loaded[:, :, :], wmask, ACT.Copy).then_inc(f_float, 1)
                    keep(2)
                    for t in TILES:
                        norm_upper(act, 1, t)
                        if t % 2:
                            keep(3 + t // 2)
                    keep(7)
                    for c in range(KC):
                        act.wait_ge(f_turned, c + 1)
                        nc.scalar.activation(wT_hi[:, c, :], psum[4 + c][:, :], ACT.Copy).then_inc(f_hi, 1)
                    weights_upper(1)
                    act.wait_ge(g_gate, 16)
                    nc.scalar.activation(gw_hi[:, :, :], gw[:, :, :], ACT.Copy).then_inc(m_ghi, 1)
                    norm_sqrt(act, 3, HALVES[0])
                    for t in HALVES[0]:
                        norm_upper(act, 2, t)
                    keep(8)
                    norm_sqrt(act, 4, HALVES[1])
                    keep(9)
                    norm_upper(act, 2, 4)
                    norm_upper(act, 2, 5)
                    keep(10)
                    norm_upper(act, 2, 6)
                    norm_upper(act, 2, 7)
                    keep(11)
                    exps(0)
                    keep(12)
                    keep(13)
                    probs_kept(0)
                    keep(14)
                    keep(15)
                    norm_sqrt(act, 5, HALVES[0])
                    exps(1)
                    for t in HALVES[0]:
                        norm_upper(act, 3, t)
                    probs_kept(1)
                    norm_sqrt(act, 6, HALVES[1])
                    logits_kept(0)
                    for t in HALVES[1]:
                        norm_upper(act, 3, t)
                    logits_kept(1)

                @block.vector
                def _(dve):
                    for t in TILES:
                        tile_stats(t)
                    norm_stats(dve, 1, 2, TILES)
                    for t in TILES:
                        norm_apply(dve, 1, t, xn)
                        if t:
                            norm_rest(dve, 1, t - 1)
                    norm_rest(dve, 1, NB - 1)
                    for c in range(KC):
                        dve.wait_ge(f_hi, c + 1)
                        nc.vector.tensor_tensor(wT_lo[:, c, :], psum[4 + c][:, :], wT_hi[:, c, :].bitcast(F32), ALU.subtract).then_inc(f_lo, 1)

                    def add_forward(t):
                        dve.wait_ge(f_mm, t + 1)
                        nc.vector.tensor_tensor(summed[:, t % 2, :], psum[4 + t % 2][:, :], bias[:, :], ALU.add).then_inc(f_sum, 1)
                        dve.wait_ge(f_sum, t + 1)
                        nc.vector.scalar_tensor_tensor(x[:, t, :], summed[:, t % 2, :], gates[:, 2:3], x[:, t, :], ALU.mult, ALU.add).then_inc(f_added, 1)
                        dve.wait_ge(f_added, t + 1)
                        tile_stats(t)

                    for t in range(4):
                        add_forward(t)
                    norm_stats(dve, 2, 3, HALVES[0])
                    norm_apply(dve, 2, 0, last_xn)
                    norm_apply(dve, 2, 1, last_xn)
                    add_forward(4)
                    norm_apply(dve, 2, 2, last_xn)
                    norm_apply(dve, 2, 3, last_xn)
                    norm_rest(dve, 2, 0)
                    add_forward(5)
                    norm_rest(dve, 2, 1)
                    norm_rest(dve, 2, 2)
                    add_forward(6)
                    norm_rest(dve, 2, 3)
                    add_forward(7)
                    norm_stats(dve, 2, 4, HALVES[1])
                    for t in HALVES[1]:
                        norm_apply(dve, 2, t, last_xn)
                    for t in HALVES[1]:
                        norm_rest(dve, 2, t)

                    def softmax_parts(n):
                        dve.wait_ge(g_smm, n + 1)
                        nc.vector.tensor_reduce(l1max[:, :], psum[4][:, :].rearrange("p (b k) -> p b k", b=4), AX.X, ALU.max).then_inc(g_max, 1)
                        dve.wait_ge(g_max, n + 1)
                        nc.vector.tensor_scalar(l1nb[:, :], l1max[:, :], -SC1, None, ALU.mult).then_inc(g_nb, 1)
                        dve.wait_ge(g_exp, n + 1)
                        nc.vector.reciprocal(l1inv[:, :], l1sum[:, :]).then_inc(g_inv, 1)
                        dve.wait_ge(g_inv, 2 * n + 1)
                        nc.vector.tensor_scalar(l1scale[:, :], l1inv[:, :], gates[:, 1:2], None, ALU.mult).then_inc(g_inv, 1)
                        dve.wait_ge(g_inv, 2 * n + 2)

                    def add_attended(n):
                        for b in range(4):
                            dve.wait_ge(g_omm, 4 * n + b + 1)
                            nc.vector.scalar_tensor_tensor(x[:, 4 * n + b, :], psum[6 + b % 2][:, :], l1scale[:, b:b + 1], x[:, 4 * n + b, :],
                                                           ALU.mult, ALU.add).then_inc(g_added, 1)
                            dve.wait_ge(g_added, 4 * n + b + 1)
                            tile_stats(4 * n + b)

                    softmax_parts(0)
                    add_attended(0)
                    norm_stats(dve, 3, 5, HALVES[0])
                    for t in HALVES[0]:
                        norm_apply(dve, 3, t, last_xn)
                    softmax_parts(1)
                    for t in HALVES[0]:
                        norm_rest(dve, 3, t)
                    add_attended(1)
                    norm_stats(dve, 3, 6, HALVES[1])

                    def choose(n):
                        dve.wait_ge(m_lkept, n + 1)
                        for t in HALVES[n]:
                            nc.vector.max(best[:, t, :], logits[:, t, :]).then_inc(m_best, 1)
                        for t in HALVES[n]:
                            dve.wait_ge(m_best, 4 * n + t + 1)
                            nc.vector.max_index(best_at[:, t, :], best[:, t, :], logits[:, t, :]).then_inc(m_best, 1)

                    for t in HALVES[1]:
                        norm_apply(dve, 3, t, last_xn)
                        if t > 4:
                            norm_rest(dve, 3, t - 1)
                    norm_rest(dve, 3, 7)
                    choose(0)
                    choose(1)

                @block.tensor
                def _(pe):
                    def project(i):
                        w, c, half = item(i)
                        pe.wait_ge(g_wlo, KC * w + c + 1)
                        if i >= 2:
                            pe.wait_ge(g_kept, i - 1)
                        if w and c == 0:
                            pe.wait_ge(ln_lo, 2 * NB + 4 * (half + 1))
                        r_hi, r_lo = ((cT_hi, cT_lo), (xT_hi, xT_lo))[w]
                        for k in range(KC):
                            mm = product(psum[2 + i % 2][:, :], w_hi[:, k, columns(c)], w_lo[:, k, columns(c)],
                                         r_hi[:, k, half_of(half)], r_lo[:, k, half_of(half)], k == 0, k == KC - 1)
                        mm.then_inc(g_mm, 1)

                    def forward(t):
                        if t >= 2:
                            pe.wait_ge(f_sum, t - 1)
                        tok = slice(t * P, (t + 1) * P)
                        for c in range(KC):
                            if t == 0:
                                pe.wait_ge(f_lo, c + 1)
                            mm = product(psum[4 + t % 2][:, :], xT_hi[:, c, tok], xT_lo[:, c, tok], wT_hi[:, c, :], wT_lo[:, c, :], c == 0, c == KC - 1)
                        mm.then_inc(f_mm, 1)

                    def score(n):
                        pe.wait_ge(g_kept, 2 * KC + KC * (n + 1))
                        if n:
                            pe.wait_ge(g_exp, n)
                        else:
                            pe.wait_ge(f_sum, NB)
                        for b in range(4):
                            q = slice(b * S, (b + 1) * S)
                            keys = slice((4 * n + b) * S, (4 * n + b + 1) * S)
                            for c in range(KC):
                                mm = nc.tensor.matmul(psum[4][:, q], q1[:, c, q], k1[:, c, keys], start=c == 0, stop=c == KC - 1)
                        mm.then_inc(g_smm, 1)

                    def turn_probs(n):
                        pe.wait_ge(g_exp, n + 1)
                        if n:
                            pe.wait_ge(g_pkept, n)
                        for b in range(4):
                            mm = nc.tensor.transpose(psum[5][:, b * S:(b + 1) * S], l1p[:, b, :], ident[:, :])
                        mm.then_inc(g_turned, 1)

                    def attend(n):
                        pe.wait_ge(g_pkept, n + 1)
                        pe.wait_ge(g_ctx, 16)
                        for b in range(4):
                            if 4 * n + b >= 2:
                                pe.wait_ge(g_added, 4 * n + b - 1)
                            q = slice(b * S, (b + 1) * S)
                            nc.tensor.matmul(psum[6 + b % 2][:, :], l1pT[:, q], c_raw[:, 4 * n + b, :], start=True, stop=True).then_inc(g_omm, 1)

                    def route(n):
                        pe.wait_ge(m_glo, 1)
                        pe.wait_ge(ln_lo, 3 * NB + 4 * (n + 1))
                        pe.wait_ge(g_pkept, 2)
                        if n:
                            pe.wait_ge(m_logk, 1)
                        for c in range(KC):
                            mm = product(psum[5][0:NX, :], gw_hi[:, c, :], gw_lo[:, c, :], xT_hi[:, c, half_of(n)], xT_lo[:, c, half_of(n)], c == 0, c == KC - 1)
                        mm.then_inc(m_log, 1)

                    for i in range(3):
                        project(i)
                    for t in TILES:
                        norm_turn(pe, 1, t, xn)
                        if t % 2:
                            project(3 + t // 2)
                    project(7)
                    pe.wait_ge(f_deq, 4)
                    for c in range(KC):
                        for r in range(KC):
                            mm = nc.tensor.transpose(psum[4 + c][:, r * P:(r + 1) * P], weight[:, r, c * P:(c + 1) * P], ident[:, :])
                        mm.then_inc(f_turned, 1)
                    pe.wait_ge(ln_lo, 2 * NB)
                    for t in range(6):
                        forward(t)
                    norm_turn(pe, 2, 0, last_xn)
                    norm_turn(pe, 2, 1, last_xn)
                    forward(6)
                    norm_turn(pe, 2, 2, last_xn)
                    norm_turn(pe, 2, 3, last_xn)
                    forward(7)
                    project(8)
                    project(9)
                    norm_turn(pe, 2, 4, last_xn)
                    norm_turn(pe, 2, 5, last_xn)
                    project(10)
                    norm_turn(pe, 2, 6, last_xn)
                    norm_turn(pe, 2, 7, last_xn)
                    project(11)
                    score(0)
                    project(12)
                    project(13)
                    turn_probs(0)
                    project(14)
                    attend(0)
                    project(15)
                    score(1)
                    for t in HALVES[0]:
                        norm_turn(pe, 3, t, last_xn)
                    turn_probs(1)
                    attend(1)
                    def turn_logits(n):
                        pe.wait_ge(m_logk, n + 1)
                        for t in HALVES[n]:
                            mm = nc.tensor.transpose(psum[2 + n][:, (t - 4 * n) * NX:(t - 4 * n + 1) * NX], logitsT[:, t * P:(t + 1) * P], ident[0:NX, 0:NX])
                        mm.then_inc(m_lturn, 1)

                    route(0)
                    turn_logits(0)
                    for t in HALVES[1]:
                        norm_turn(pe, 3, t, last_xn)
                    route(1)
                    turn_logits(1)

        EXTRA = (TOP * T - 1) // P
        SLOTS = NX + EXTRA
        COLUMNS = SLOTS + SLOTS % 2
        LANES = 4
        ALWAYS = NX + LANES
        ROUNDS = -(-ALWAYS // RING)
        NOWHERE = 4 * T
        picked = nc.dram_tensor("picked", [TOP * T, E], F32, kind="Internal").ap()
        with ExitStack() as ctx:
            late_w = sb("late_w", [P, RING - EARLY, KC, E], ctx=ctx)

            def expert_weights(k):
                return early_w[:, k, :, :] if k < EARLY else late_w[:, k - EARLY, :, :]

            bestf = sb("bestf", [P, NB, TOP], ctx=ctx)
            diff, ediff, edp1 = (sb(n, [P, NB], ctx=ctx) for n in ("diff", "ediff", "edp1"))
            wts = sb("wts", [P, TOP, NB], ctx=ctx)
            onehot = sb("onehot", [P, TOP, NB, NX], ctx=ctx)
            at_place = xT_hi[:, 0:2, :].rearrange("p c (j n) -> p (c j) n", n=P)
            in_slot = xT_lo[:, 0:2, :].rearrange("p c (j n) -> p (c j) n", n=P)[:, :, 0:COLUMNS]
            chosen = xT_hi[:, 2, 0:NB * NX].rearrange("p (t e) -> p t e", e=NX)
            chosen_upto = xT_hi[:, 3, 0:NB * NX].rearrange("p (t e) -> p t e", e=NX)
            before = xT_lo[:, 2, 0:P]
            ones = xT_lo[:, 3, 0:P]
            weighted = sb("weighted", [P, TOP, NB, NX], ctx=ctx)
            combT = logitsT[:, :].rearrange("e (t p) -> e t p", p=P)
            rank = sb("rank", [P, NB + 1, NX], I32, ctx)
            rank_full, rank_rest = (sb(n, [P, NB + 1, NX], I32, ctx) for n in ("rank_full", "rank_rest"))
            full, place = (sb(n, [P, NB + 1, NX], ctx=ctx) for n in ("full", "place"))
            upto = sb("upto", [P, 2, 16 + NX], ctx=ctx)
            ahead = sb("ahead", [P, NX], ctx=ctx)
            over = sb("over", [P, NB, NX], ctx=ctx)
            slot = sb("slot", [P, NB, NX], ctx=ctx)
            comb = over
            place_of_pair, slot_of_pair = (sb(n, [P, TOP, NB], ctx=ctx) for n in ("place_of_pair", "slot_of_pair"))
            passed = sb("passed", [P, 16, NX], ctx=ctx)
            owner = sb("owner", [P, 16], ctx=ctx)
            owner_at = sb("owner_at", [P, 17], I32, ctx)
            place_row = sb("place_row", [P, SLOTS], I32, ctx)
            place_token = sb("place_token", [P, SLOTS], I32, ctx)
            nobody = sb("nobody", [P, SLOTS], ctx=ctx)
            eb = sb("eb", [NX, E], ctx=ctx)
            taken = sb("taken", [P, RING, E], ctx=ctx)
            takenT = sb("takenT", [P, LANES, KC, P], ctx=ctx)
            before_raw, ones_raw = taken[:, 4, 0:P], taken[:, 5, 0:P]
            tile_sums = taken[:, 6:8, 0:(4 + NB) * NX].rearrange("p k (t e) -> p k t e", e=NX)
            result = loaded
            chosen_y = late_w[:, 0:4, :, :].rearrange("p k c n -> p (k c) n").rearrange("p (k t) n -> p k t n", k=TOP)
            take_at = sb("take_at", [P, RING], I32, ctx)
            give_at = sb("give_at", [P, LANES], I32, ctx)
            gatepost = sb("gatepost3", [P, 2], ctx=ctx)
            zero = sb("zero", [P, 1], ctx=ctx)
            m_const, m_step, m_exp, m_rank, m_built, m_laid, m_cT, m_cTk, m_bmm, m_badd, m_out = (
                sem(f"m_{n}") for n in ("const", "step", "exp", "rank", "built", "laid", "cT", "cTk", "bmm", "badd", "out"))
            rows_ready, tokens_ready, owners_ready, constants, chosen_ready, diff_ready, comb_ready = (
                sem(n) for n in ("rows_ready", "tokens_ready", "owners_ready", "constants", "chosen_ready", "diff_ready", "comb_ready"))
            t_in = [sem(f"t_in{k}") for k in range(RING)]
            y_out = [sem(f"y_out{k}") for k in range(LANES)]
            take_set, give_set, t_turned, t_kept, e_mm, e_kept = (
                sem(n) for n in ("take_set", "give_set", "t_turned", "t_kept", "e_mm", "e_kept"))
            y_in = [sem(f"y_in{t}") for t in TILES]
            y_added2 = sem("y_added2")
            exact = sem("exact")

            def slots(r):
                return range(ALWAYS - RING * (ROUNDS - 1) if isinstance(r, int) and r == ROUNDS - 1 else RING)

            REST = [divmod(s, RING) for s in range(ALWAYS, SLOTS)]

            def if_needed(engine):
                extra_slots = engine.value_load(owner_at[0:1, 16:17], min_val=0, max_val=EXTRA)
                return engine.If(extra_slots > ALWAYS - NX)

            def lane_turn(k):
                return k // LANES

            def rounds(engine, one):
                one(0)
                with engine.Fori(1, ROUNDS - 1) as r:
                    one(r)
                one(ROUNDS - 1)

            LANE_ROUND = 16 * RING // LANES

            with nc.Block() as block:
                @block.sync
                def _(sp):
                    sp.dma_start(before_raw, a["before"]).then_inc(m_const, 16)
                    sp.dma_start(eb[:, :], a["eb"]).then_inc(m_const, 16)
                    for k in range(EARLY, RING):
                        sp.dma_start(expert_weights(k), a["ew"][k]).then_inc(w_in[k], 16)

                    def weights(r, k, expert):
                        wait(sp, e_mm, r, RING, k - RING + 1)
                        sp.dma_start(expert_weights(k), a["ew"][bass.ds(expert, 1)].rearrange("o p c n -> p (o c) n")).then_inc(w_in[k], 16)

                    def extra_weights(r, k):
                        n = r * RING + k - NX
                        weights(r, k, sp.value_load(owner_at[0:1, n:n + 1], min_val=0, max_val=NX - 1))

                    def given(slots):
                        for lane in range(LANES):
                            sp.wait_ge(y_out[lane], 16 * len(range(lane, slots, LANES)))

                    STATIC = NX // RING
                    with sp.Fori(1, STATIC) as r:
                        for k in range(RING):
                            weights(r, k, r * RING + k)
                    sp.wait_ge(owners_ready, 1)
                    for k in slots(ROUNDS - 1):
                        extra_weights(ROUNDS - 1, k)
                    given(ALWAYS)
                    with if_needed(sp):
                        for r, k in REST:
                            extra_weights(r, k)
                        given(SLOTS)
                    for t in TILES:
                        sp.dma_start(chosen_y[:, :, t, :],
                                     picked.rearrange("(c t p) e -> p c t e", c=TOP, p=P)[:, :, t, :]).then_inc(y_in[t], 16)
                    for first, last in ((0, 3), (3, 6), (6, 8)):
                        sp.wait_ge(y_added2, TOP * last)
                        sp.dma_start(out[:, first:last, :], x[:, first:last, :]).then_inc(m_out, 16)
                    sp.wait_ge(m_out, 16 * 3)

                @block.gpsimd
                def _(pool):
                    nc.gpsimd.memset(ones_raw, 1.0).then_inc(constants, 1)
                    nc.gpsimd.memset(zero[:, :], 0.0).then_inc(constants, 1)
                    pool.wait_ge(constants, 2)
                    pool.wait_ge(rows_out, 32)
                    pool.wait_ge(tokens_ready, 1)

                    def carry(n):
                        nc.gpsimd.tensor_tensor(gatepost[:, n:n + 1], zero[:, :], zero[:, :], ALU.add)

                    def take(r, k):
                        lane = k % RING
                        wait(pool, t_turned, r, RING, k - RING + 1)
                        carry(0)
                        nc.gpsimd.tensor_copy(take_at[:, lane:lane + 1], place_token[:, bass.ds(r * RING + k, 1)]).then_inc(take_set, 1)
                        wait(pool, take_set, r, RING, k + 1)
                        carry(1)
                        pool.indirect_dma_start(out=taken[:, lane, :], out_offset=None, in_=xn_rows,
                                                in_offset=bass.IndirectOffsetOnAxis(ap=take_at[:, lane:lane + 1].bitcast(U32), axis=0)).then_inc(t_in[lane], 16)

                    def give(r, k):
                        lane = k % LANES
                        wait(pool, e_kept, r, RING, k + 1)
                        carry(0)
                        nc.gpsimd.tensor_copy(give_at[:, lane:lane + 1], place_row[:, bass.ds(r * RING + k, 1)]).then_inc(give_set, 1)
                        wait(pool, give_set, r, RING, k + 1)
                        carry(1)
                        pool.indirect_dma_start(out=picked, out_offset=bass.IndirectOffsetOnAxis(ap=give_at[:, lane:lane + 1].bitcast(U32), axis=0),
                                                in_=result[:, lane, :], in_offset=None, bounds_check=TOP * T - 1, oob_is_err=False).then_inc(y_out[lane], 16)

                    for k in range(RING):
                        take(0, k)

                    def one(r):
                        for k in slots(r):
                            if not (isinstance(r, int) and RING * (r + 1) + k >= ALWAYS):
                                take(r, k + RING)
                            give(r, k)
                    one(0)
                    with pool.Fori(1, ROUNDS - 2) as r:
                        one(r)
                    one(ROUNDS - 2)
                    one(ROUNDS - 1)
                    pool.wait_ge(owners_ready, 1)
                    with if_needed(pool):
                        for r, k in REST[:RING]:
                            take(r, k)
                        for r, k in REST:
                            if RING * (r + 1) + k < SLOTS:
                                take(r, k + RING)
                            give(r, k)

                @block.scalar
                def _(act):
                    act.wait_ge(m_const, 32)
                    nc.scalar.activation(before, before_raw, ACT.Copy).then_inc(exact, 1)
                    act.wait_ge(constants, 2)
                    nc.scalar.activation(ones, ones_raw, ACT.Copy).then_inc(exact, 1)
                    act.wait_ge(diff_ready, 1)
                    nc.scalar.activation(ediff[:, :], diff[:, :], ACT.Exp).then_inc(m_exp, 1)

                    def keep_turned(r, k):
                        wait(act, t_turned, r, RING, k + 1)
                        wait(act, e_mm, r, RING, k - LANES + 1)
                        nc.scalar.activation(takenT[:, k % LANES, :, :], psum[k % 2][:, :].rearrange("p (c t) -> p c t", c=KC), ACT.Copy).then_inc(t_kept, 1)

                    def one(r):
                        for k in slots(r):
                            keep_turned(r, k)
                    rounds(act, one)
                    act.wait_ge(owners_ready, 1)
                    with if_needed(act):
                        for r, k in REST:
                            keep_turned(r, k)

                @block.vector
                def _(dve):
                    dve.wait_ge(m_best, 2 * NB)
                    nc.vector.tensor_tensor(diff[:, :], best[:, :, 1], best[:, :, 0], ALU.subtract).then_inc(diff_ready, 1)
                    done = [0]

                    def step(op):
                        done[0] += 1
                        op.then_inc(m_step, 1)

                    def ready():
                        dve.wait_ge(m_step, done[0])

                    def over_experts(ap):
                        return ap.unsqueeze(1).broadcast_to([P, NB, NX])

                    def over_tokens(ap):
                        return ap.unsqueeze(2).broadcast_to([P, NB, NX])

                    def by_pair(ap, n):
                        return ap.rearrange("p k t -> p (k t)").unsqueeze(2).broadcast_to([P, TOP * NB, n])

                    def number(n):
                        return numbers[:, 0:n].unsqueeze(1).broadcast_to([P, TOP * NB, n])

                    experts = numbers[:, 0:NX]
                    step(nc.vector.tensor_copy(bestf[:, :, :], best_at[:, :, 0:TOP]))
                    step(nc.vector.memset(upto[:, :, 0:16], 0.0))
                    step(nc.vector.memset(tile_sums[:, :, 0:4, :], 0.0))
                    ready()
                    dve.wait_ge(m_in, 32)
                    for k in range(TOP):
                        step(nc.vector.tensor_tensor(onehot[:, k, :, :], over_experts(experts), over_tokens(bestf[:, :, k]), ALU.is_equal))
                    ready()
                    nc.vector.tensor_tensor(chosen, onehot[:, 0, :, :], onehot[:, 1, :, :], ALU.add).then_inc(chosen_ready, 1)
                    step(nc.vector.tensor_tensor(tile_sums[:, 0, 4:, :], onehot[:, 0, :, :], onehot[:, 1, :, :], ALU.add))
                    ready()
                    for n in range(3):
                        src, dst, by = n % 2, (n + 1) % 2, 1 << n
                        total = chosen_upto if n == 2 else tile_sums[:, dst, 4:, :]
                        step(nc.vector.tensor_tensor(total, tile_sums[:, src, 4:, :], tile_sums[:, src, 4 - by:4 + NB - by, :], ALU.add))
                        ready()
                    nc.vector.memset(gatepost[:, 0:1], 0.0).then_inc(chosen_ready, 1)
                    dve.wait_ge(m_rank, 1)
                    step(nc.vector.tensor_copy(rank[:, 0:NB, :], psum[3][:, 0:NB * NX].rearrange("p (t e) -> p t e", t=NB)))
                    step(nc.vector.tensor_scalar(rank[:, NB, :], psum[3][:, NB * NX:(NB + 1) * NX], -1.0, 0.0, ALU.add, ALU.max))
                    ready()
                    step(nc.vector.tensor_scalar(rank_full[:, :, :], rank[:, :, :], P.bit_length() - 1, None, ALU.arith_shift_right))
                    step(nc.vector.tensor_scalar(rank_rest[:, :, :], rank[:, :, :], P - 1, None, ALU.bitwise_and))
                    ready()
                    step(nc.vector.tensor_copy(upto[:, 0, 16:], rank_full[:, NB, :]))
                    step(nc.vector.tensor_copy(full[:, :, :], rank_full[:, :, :]))
                    ready()
                    for n in range(5):
                        src, dst, by = n % 2, (n + 1) % 2, 1 << n
                        step(nc.vector.tensor_tensor(upto[:, dst, 16:], upto[:, src, 16:], upto[:, src, 16 - by:16 + NX - by], ALU.add))
                        if n == 0:
                            step(nc.vector.tensor_copy(place[:, :, :], rank_rest[:, :, :]))
                        ready()
                    summed_to = upto[:, 1, 16:]
                    step(nc.vector.scalar_tensor_tensor(ahead[:, :], summed_to, float(NX - 1), full[:, NB, :], ALU.add, ALU.subtract))
                    for k in range(TOP):
                        step(nc.vector.tensor_tensor(weighted[:, k, :, :], onehot[:, k, :, :], place[:, 0:NB, :], ALU.mult))
                    ready()
                    step(nc.vector.tensor_tensor(over[:, :, :], full[:, 0:NB, :], over_experts(ahead[:, :]), ALU.add))
                    step(nc.vector.tensor_reduce(place_of_pair[:, :, :], weighted[:, :, :, :], AX.X, ALU.add))
                    ready()
                    nc.vector.tensor_tensor(at_place, number(P), by_pair(place_of_pair[:, :, :], P), ALU.is_equal).then_inc(m_built, 1)
                    step(nc.vector.tensor_tensor(over[:, :, :], over[:, :, :], over_experts(experts), ALU.subtract))
                    ready()
                    step(nc.vector.scalar_tensor_tensor(over[:, :, :], full[:, 0:NB, :], 0.0, over[:, :, :], ALU.is_gt, ALU.mult))
                    ready()
                    step(nc.vector.tensor_tensor(slot[:, :, :], over[:, :, :], over_experts(experts), ALU.add))
                    ready()
                    for k in range(TOP):
                        step(nc.vector.tensor_tensor(weighted[:, k, :, :], onehot[:, k, :, :], slot[:, :, :], ALU.mult))
                    ready()
                    step(nc.vector.tensor_reduce(slot_of_pair[:, :, :], weighted[:, :, :, :], AX.X, ALU.add))
                    ready()
                    step(nc.vector.tensor_tensor(in_slot, number(COLUMNS), by_pair(slot_of_pair[:, :, :], COLUMNS), ALU.is_equal))
                    ready()
                    nc.vector.tensor_tensor(in_slot, in_slot.bitcast(F32), by_pair(pair_codes[:, :, :], COLUMNS), ALU.mult).then_inc(m_built, 1)
                    dve.wait_ge(m_exp, 1)
                    step(nc.vector.tensor_scalar_add(edp1[:, :], ediff[:, :], 1.0))
                    ready()
                    step(nc.vector.reciprocal(wts[:, 0, :], edp1[:, :]))
                    ready()
                    step(nc.vector.tensor_tensor(wts[:, 1, :], wts[:, 0, :], ediff[:, :], ALU.mult))
                    ready()
                    step(nc.vector.tensor_scalar(wts[:, :, :], wts[:, :, :], gates[:, 3:4], None, ALU.mult))
                    ready()
                    for k in range(TOP):
                        step(nc.vector.tensor_tensor(weighted[:, k, :, :], onehot[:, k, :, :], over_tokens(wts[:, k, :]), ALU.mult))
                    ready()
                    nc.vector.tensor_tensor(comb[:, :, :], weighted[:, 0, :, :], weighted[:, 1, :, :], ALU.add).then_inc(comb_ready, 1)
                    dve.wait_ge(m_laid, 1)
                    step(nc.vector.tensor_scalar(nobody[:, :], psum[2][:, 0:SLOTS], 0.0, float(NOWHERE + 1), ALU.is_equal, ALU.mult))
                    ready()
                    nc.vector.scalar_tensor_tensor(place_row[:, :], psum[2][:, 0:SLOTS], -1.0, nobody[:, :], ALU.add, ALU.add).then_inc(rows_ready, 1)
                    dve.wait_ge(rows_ready, 1)
                    nc.vector.tensor_scalar(place_token[:, :], place_row[:, :], T - 1, None, ALU.bitwise_and).then_inc(tokens_ready, 1)
                    for n in range(2):
                        dve.wait_ge(m_cT, n + 1)
                        nc.vector.tensor_copy(combT[:, 4 * n:4 * n + 4, :], psum[3 + n][0:NX, :].rearrange("p (t q) -> p t q", t=4)).then_inc(m_cTk, 1)
                    for j in range(16):
                        last = nc.vector.tensor_scalar(passed[:, j, :], summed_to, float(j), None, ALU.is_le)
                    step(last)
                    ready()
                    step(nc.vector.tensor_reduce(owner[:, :], passed[:, :, :], AX.X, ALU.add))
                    ready()
                    nc.vector.tensor_copy(owner_at[:, 16:17], summed_to[:, NX - 1:NX])
                    nc.vector.tensor_scalar(owner_at[:, 0:16], owner[:, :], float(NX - 1), None, ALU.min).then_inc(owners_ready, 1)

                    def keep_result(r, k):
                        lane = k % LANES
                        wait(dve, e_mm, r, RING, k + 1)
                        wait(dve, y_out[lane], r, LANE_ROUND, 16 * lane_turn(k))
                        nc.vector.tensor_copy(result[:, lane, :], psum[4 + lane][:, :]).then_inc(e_kept, 1)

                    def one(r):
                        for k in slots(r):
                            keep_result(r, k)
                    rounds(dve, one)
                    for t in TILES:
                        dve.wait_ge(m_bmm, t + 1)
                        nc.vector.tensor_tensor(x[:, t, :], psum[2 + t % 2][:, :], x[:, t, :], ALU.add).then_inc(m_badd, 1)
                    dve.wait_ge(owners_ready, 1)
                    with if_needed(dve):
                        for r, k in REST:
                            keep_result(r, k)
                    dve.wait_ge(m_badd, NB)
                    for t in TILES:
                        dve.wait_ge(y_in[t], 16)
                        for c in range(TOP):
                            if c:
                                dve.wait_ge(y_added2, 2 * t + 1)
                            nc.vector.scalar_tensor_tensor(x[:, t, :], chosen_y[:, c, t, :], wts[:, c, t:t + 1], x[:, t, :],
                                                           ALU.mult, ALU.add).then_inc(y_added2, 1)

                @block.tensor
                def _(pe):
                    pe.wait_ge(exact, 2)
                    pe.wait_ge(chosen_ready, 1)
                    nc.tensor.matmul(psum[3][:, 0:NB * NX], before, chosen.rearrange("p t e -> p (t e)"),
                                     start=True, stop=False, skip_group_check=True)
                    pe.wait_ge(chosen_ready, 2)
                    nc.tensor.matmul(psum[3][:, NX:(NB + 1) * NX], ones, chosen_upto.rearrange("p t e -> p (t e)"),
                                     start=False, stop=True, skip_group_check=True).then_inc(m_rank, 1)
                    pe.wait_ge(m_built, 2)
                    for j in range(TOP * NB):
                        mm = nc.tensor.matmul(psum[2][:, 0:COLUMNS], at_place[:, j, :], in_slot[:, j, :], start=j == 0, stop=j == TOP * NB - 1)
                    mm.then_inc(m_laid, 1)

                    def turn(r, k):
                        lane = k % RING
                        wait(pe, t_in[lane], r, 16, 16 + 16 * (k // RING))
                        wait(pe, t_kept, r, RING, k - 1)
                        for c in range(KC):
                            mm = nc.tensor.transpose(psum[k % 2][:, c * P:(c + 1) * P], taken[:, lane, c * P:(c + 1) * P], ident[:, :])
                        mm.then_inc(t_turned, 1)

                    def multiply(r, k):
                        lane = k % LANES
                        wait(pe, t_kept, r, RING, k + 1)
                        wait(pe, w_in[k], r, 16, 16)
                        wait(pe, e_kept, r, RING, k - LANES + 1)
                        for c in range(KC):
                            mm = nc.tensor.matmul(psum[4 + lane][:, :], takenT[:, lane, c, :], expert_weights(k)[:, c, :], start=c == 0, stop=c == KC - 1)
                        mm.then_inc(e_mm, 1)

                    def one(r):
                        for k in slots(r):
                            if not (isinstance(r, int) and RING * r + k + 1 == ALWAYS):
                                turn(r, k + 1)
                            multiply(r, k)
                    pe.wait_ge(comb_ready, 1)
                    for t in TILES:
                        mm = nc.tensor.transpose(psum[3 + t // 4][0:NX, (t % 4) * P:(t % 4 + 1) * P], comb[:, t, :], ident[:, :])
                        if t % 4 == 3:
                            mm.then_inc(m_cT, 1)
                    turn(0, 0)
                    pe.wait_ge(m_cTk, 2)
                    rounds(pe, one)
                    pe.wait_ge(rows_ready, 1)
                    for t in TILES:
                        if t >= 2:
                            pe.wait_ge(m_badd, t - 1)
                        nc.tensor.matmul(psum[2 + t % 2][:, :], combT[:, t, :], eb[:, :], start=True, stop=True).then_inc(m_bmm, 1)
                    pe.wait_ge(owners_ready, 1)
                    with if_needed(pe):
                        turn(*REST[0])
                        for r, k in REST:
                            if (r, k) != REST[-1]:
                                turn(r, k + 1)
                            multiply(r, k)


def kernel(x, ctx_4096, pos_BxS2, mask_BxSxS2_ik0, g_xattn, g_ffn, L0_xattn_Wq, L0_xattn_Wk, L0_xattn_Wv,
           L0_xattn_Wo, L0_ffn_W_q, L0_ffn_scales, L0_ffn_zeros, L0_ffn_mask, L0_ffn_scale2, L0_ffn_bias,
           L1_xattn_Wq, L1_xattn_bq, L1_xattn_Wk, L1_xattn_bk, L1_ffn_gate_w, L1_ffn_expert_w, L1_ffn_expert_b):
    import numpy as np
    import concourse.bacc as bacc
    from concourse.bass_utils import run_bass_kernel_spmd

    def chunked(w):
        w = np.asarray(w)
        return w.reshape(-1, P, w.shape[1]).transpose(1, 0, 2)

    inv = (1.0 / np.float32(10000.0) ** (np.arange(0, D, 2, dtype=np.float32) / np.float32(D))).astype(np.float32)
    angle = np.arange(MAX_POS, dtype=np.float32)[:, None] * inv[None, :]
    cos, sin = np.cos(angle), np.sin(angle)
    wq = np.asarray(L0_xattn_Wq).reshape(KC, P, KVH, GR * D)
    wo = np.asarray(L0_xattn_Wo).reshape(KVH, GR, D, E)
    layout = {
        "x": np.asarray(x).transpose(1, 0, 2),
        "ctxT": np.asarray(ctx_4096).reshape(T, KC, P).transpose(2, 1, 0),
        "ctx": np.asarray(ctx_4096).transpose(1, 0, 2),
        "pos": np.asarray(pos_BxS2).T,
        "mask": np.asarray(mask_BxSxS2_ik0).transpose(1, 0, 2),
        "gates": np.concatenate([np.asarray(g_xattn), np.asarray(g_ffn)]),
        "wq": wq.transpose(2, 1, 0, 3).reshape(KVH, P, KC * GR * D),
        "wo": wo.transpose(0, 2, 1, 3).reshape(KVH, P, GR * E),
        "wk": np.asarray(L0_xattn_Wk).reshape(KC, P, KVH, D).transpose(2, 1, 0, 3),
        "wv": np.asarray(L0_xattn_Wv).reshape(KC, P, KVH, D).transpose(2, 1, 0, 3),
        "wint": chunked(L0_ffn_W_q),
        "wmask": chunked(L0_ffn_mask),
        "scales": chunked(L0_ffn_scales),
        "zeros": chunked(L0_ffn_zeros),
        "scale2": np.asarray(L0_ffn_scale2).reshape(KC, P).T,
        "fbias": np.asarray(L0_ffn_bias),
        "wq1": chunked(np.asarray(L1_xattn_Wq).T),
        "wk1": chunked(np.asarray(L1_xattn_Wk).T),
        "b1": np.stack([np.asarray(L1_xattn_bk).reshape(KC, P).T, np.asarray(L1_xattn_bq).reshape(KC, P).T], axis=1),
        "gw": chunked(np.asarray(L1_ffn_gate_w).T),
        "ew": np.asarray(L1_ffn_expert_w).transpose(0, 2, 1).reshape(NX, KC, P, E).transpose(0, 2, 1, 3),
        "eb": np.asarray(L1_ffn_expert_b),
        "ident": np.eye(P, dtype=np.float32),
        "numbers": np.arange(P, dtype=np.float32),
        "before": np.triu(np.ones((P, P), dtype=np.float32), 1),
        "pair_codes": (np.arange(TOP * T) + 1).astype(np.float32).reshape(TOP, NB, P).transpose(2, 0, 1),
        "rotary": np.concatenate([cos, cos, sin, -sin], axis=1).astype(np.float32),
    }
    nc = bacc.Bacc("TRN2", target_bir_lowering=False, num_devices=1, dynamic_dma_scratch_size=4096)
    arrays = {f"in_{k}": np.ascontiguousarray(v) for k, v in layout.items()}
    aps = {k: nc.dram_tensor(f"in_{k}", arrays[f"in_{k}"].shape, mybir.dt.from_np(arrays[f"in_{k}"].dtype),
                             kind="ExternalInput").ap() for k in layout}
    out = nc.dram_tensor("out", [P, NB, E], F32, kind="ExternalOutput").ap()
    program(nc, aps, out)
    r = run_bass_kernel_spmd(nc, [arrays], core_ids=[0])
    return np.asarray(r.results[0]["out"]).transpose(1, 0, 2).reshape(NB, S, E)
```
